# Optimizing a Trainium2 kernel written in Bass

```python
import numpy as np
import jax
import jax.numpy as jnp

def _softmax(x, axis=-1):
    return jax.nn.softmax(x, axis=axis)

def _gelu(x):
    return jax.nn.gelu(x, approximate=True)

def _silu(x):
    return jax.nn.silu(x)

def _sigmoid(x):
    return jax.nn.sigmoid(x)

def _layernorm(x, axis=-1, eps=1e-05):
    m = jnp.mean(x, axis=axis, keepdims=True)
    v = jnp.var(x, axis=axis, keepdims=True)
    return (x - m) / jnp.sqrt(v + eps)

def _scatter_add(tgt, idx, src, axis=0):
    return tgt.at[idx].add(src)

def _segment_sum(src, seg, n):
    return jax.ops.segment_sum(src, seg, n)
kernel_name = 'mk_adaln_d1_jaxref_r8_84b564'

def setup_inputs(seed: int=0):
    np.random.seed(seed)
    _w = jnp.asarray

    def _L0_attn_setup():
        import jax, jax.numpy as jnp
        import numpy as np
        import math
        B, L, HID = (2, 512, 128)
        NH, DK, DV = (12, 64, 128)
        KD, VD, CS = (NH * DK, NH * DV, 4)
        SCALE = DK ** (-0.5)

        def _causal_depthwise_conv(x, w):
            c, k = w.shape
            xt = jnp.transpose(x, (0, 2, 1))
            out = jax.lax.conv_general_dilated(xt, w[:, None, :], window_strides=(1,), padding=[(k - 1, 0)], feature_group_count=c, dimension_numbers=('NCH', 'OIH', 'NCH'))
            return jnp.transpose(out, (0, 2, 1))

        def _l2norm(x, eps=1e-06):
            return x * jax.lax.rsqrt(jnp.sum(x * x, axis=-1, keepdims=True) + eps)

        def _gated_delta_net(hidden_states, Wq, Wk, Wv, Wg, Wo, conv_q, conv_k, conv_v, Wgk, Wb, b_b, A_log, dt_bias, g_norm_weight):
            b, l, _ = hidden_states.shape
            q = jax.nn.silu(_causal_depthwise_conv(hidden_states @ Wq, conv_q))
            k = jax.nn.silu(_causal_depthwise_conv(hidden_states @ Wk, conv_k))
            v = jax.nn.silu(_causal_depthwise_conv(hidden_states @ Wv, conv_v))
            gk = -jnp.exp(A_log) * jax.nn.softplus(hidden_states @ Wgk + dt_bias)
            beta = jax.nn.sigmoid(hidden_states @ Wb + b_b)
            q = jnp.transpose(q.reshape(b, l, NH, DK), (0, 2, 1, 3))
            k = jnp.transpose(k.reshape(b, l, NH, DK), (0, 2, 1, 3))
            v = jnp.transpose(v.reshape(b, l, NH, DV), (0, 2, 1, 3))
            q = _l2norm(q) * SCALE
            k = _l2norm(k)
            qs = jnp.moveaxis(q, 2, 0)
            ks_ = jnp.moveaxis(k, 2, 0)
            vs = jnp.moveaxis(v, 2, 0)
            bs = jnp.moveaxis(beta, 1, 0)
            gs = jnp.moveaxis(gk, 1, 0)

            def step(S, inp):
                qt, kt, vt, bt, gt = inp
                S = S * jnp.exp(gt)[..., None, None]
                kv = jnp.einsum('bhk,bhkv->bhv', kt, S)
                delta = (vt - kv) * bt[..., None]
                S = S + jnp.einsum('bhk,bhv->bhkv', kt, delta)
                ot = jnp.einsum('bhk,bhkv->bhv', qt, S)
                return (S, ot)
            S0 = jnp.zeros((b, NH, DK, DV), hidden_states.dtype)
            _, os_ = jax.lax.scan(step, S0, (qs, ks_, vs, bs, gs))
            o = jnp.moveaxis(os_, 0, 1)
            g = (hidden_states @ Wg).reshape(b, l, NH, DV)
            var = jnp.mean(o * o, axis=-1, keepdims=True)
            o = o * jax.lax.rsqrt(var + 1e-05) * g_norm_weight
            o = o * g * jax.nn.sigmoid(g)
            return o.reshape(b, l, VD) @ Wo
        key = jax.random.key(seed)
        ks = jax.random.split(key, 16)
        rn = lambda i, shape, s: jax.random.normal(ks[i], shape, jnp.float32) * s
        hidden_states = rn(0, (B, L, HID), 1.0)
        Wq = rn(1, (HID, KD), HID ** (-0.5))
        Wk = rn(2, (HID, KD), HID ** (-0.5))
        Wv = rn(3, (HID, VD), HID ** (-0.5))
        Wg = rn(4, (HID, VD), HID ** (-0.5))
        Wo = rn(5, (VD, HID), VD ** (-0.5))
        conv_q = rn(6, (KD, CS), 0.5)
        conv_k = rn(7, (KD, CS), 0.5)
        conv_v = rn(8, (VD, CS), 0.5)
        Wgk = rn(9, (HID, NH), HID ** (-0.5))
        Wb = rn(10, (HID, NH), HID ** (-0.5))
        b_b = rn(11, (NH,), 0.1)
        A = jax.random.uniform(ks[12], (NH,), jnp.float32, 0.5, 16.0)
        A_log = jnp.log(A)
        dt = jnp.exp(jax.random.uniform(ks[13], (NH,), jnp.float32) * (math.log(0.1) - math.log(0.001)) + math.log(0.001))
        dt = jnp.clip(dt, 0.0001, None)
        dt_bias = dt + jnp.log(-jnp.expm1(-dt))
        g_norm_weight = jnp.ones((DV,), jnp.float32)
        return dict(hidden_states=hidden_states, Wq=Wq, Wk=Wk, Wv=Wv, Wg=Wg, Wo=Wo, conv_q=conv_q, conv_k=conv_k, conv_v=conv_v, Wgk=Wgk, Wb=Wb, b_b=b_b, A_log=A_log, dt_bias=dt_bias, g_norm_weight=g_norm_weight)
    _L0_attn_in = _L0_attn_setup()

    def _L0_ffn_setup():
        import jax, jax.numpy as jnp
        import numpy as np
        D_MODEL = 128
        N_HEADS = 16
        D_HEAD = D_MODEL // N_HEADS
        N_EXPERTS = 8
        TOP_K = 2
        D_FF = 256
        EPS = 1e-06

        def rmsnorm(x, w):
            return x * jax.lax.rsqrt(jnp.mean(x * x, axis=-1, keepdims=True) + EPS) * w

        def swiglu(x, w_gate, w_up, w_down):
            return jax.nn.silu(x @ w_gate) * (x @ w_up) @ w_down
        key = jax.random.key(seed)
        ks = jax.random.split(key, 16)
        s = 0.02
        B, S = (2, 256)
        return {'X': jax.random.normal(ks[0], (B, S, D_MODEL), dtype=jnp.float32), 'norm1_w': jnp.ones((D_MODEL,), jnp.float32), 'norm2_w': jnp.ones((D_MODEL,), jnp.float32), 'wq': jax.random.normal(ks[1], (D_MODEL, D_MODEL), jnp.float32) * s, 'wk': jax.random.normal(ks[2], (D_MODEL, D_MODEL), jnp.float32) * s, 'wv': jax.random.normal(ks[3], (D_MODEL, D_MODEL), jnp.float32) * s, 'wo': jax.random.normal(ks[4], (D_MODEL, D_MODEL), jnp.float32) * s, 'router_w': jax.random.normal(ks[5], (D_MODEL, N_EXPERTS), jnp.float32) * s, 'sh_gate': jax.random.normal(ks[6], (D_MODEL, D_FF), jnp.float32) * s, 'sh_up': jax.random.normal(ks[7], (D_MODEL, D_FF), jnp.float32) * s, 'sh_down': jax.random.normal(ks[8], (D_FF, D_MODEL), jnp.float32) * s, 'e_gate': jax.random.normal(ks[9], (N_EXPERTS, D_MODEL, D_FF), jnp.float32) * s, 'e_up': jax.random.normal(ks[10], (N_EXPERTS, D_MODEL, D_FF), jnp.float32) * s, 'e_down': jax.random.normal(ks[11], (N_EXPERTS, D_FF, D_MODEL), jnp.float32) * s}
    _L0_ffn_in = _L0_ffn_setup()
    _L0_c = _w((lambda *s: np.random.randn(*s).astype(np.float32) * 0.05)(8, 128))
    _L0_wmod = _w((lambda *s: np.random.randn(*s).astype(np.float32) * 0.05)(128, 6 * 128) * 128 ** (-0.5))
    _d = {'L0_attn_hidden_states': _L0_attn_in['hidden_states'], 'L0_attn_Wq': _L0_attn_in['Wq'], 'L0_attn_Wk': _L0_attn_in['Wk'], 'L0_attn_Wv': _L0_attn_in['Wv'], 'L0_attn_Wg': _L0_attn_in['Wg'], 'L0_attn_Wo': _L0_attn_in['Wo'], 'L0_attn_conv_q': _L0_attn_in['conv_q'], 'L0_attn_conv_k': _L0_attn_in['conv_k'], 'L0_attn_conv_v': _L0_attn_in['conv_v'], 'L0_attn_Wgk': _L0_attn_in['Wgk'], 'L0_attn_Wb': _L0_attn_in['Wb'], 'L0_attn_b_b': _L0_attn_in['b_b'], 'L0_attn_A_log': _L0_attn_in['A_log'], 'L0_attn_dt_bias': _L0_attn_in['dt_bias'], 'L0_attn_g_norm_weight': _L0_attn_in['g_norm_weight'], 'L0_ffn_norm1_w': _L0_ffn_in['norm1_w'], 'L0_ffn_norm2_w': _L0_ffn_in['norm2_w'], 'L0_ffn_wq': _L0_ffn_in['wq'], 'L0_ffn_wk': _L0_ffn_in['wk'], 'L0_ffn_wv': _L0_ffn_in['wv'], 'L0_ffn_wo': _L0_ffn_in['wo'], 'L0_ffn_router_w': _L0_ffn_in['router_w'], 'L0_ffn_sh_gate': _L0_ffn_in['sh_gate'], 'L0_ffn_sh_up': _L0_ffn_in['sh_up'], 'L0_ffn_sh_down': _L0_ffn_in['sh_down'], 'L0_ffn_e_gate': _L0_ffn_in['e_gate'], 'L0_ffn_e_up': _L0_ffn_in['e_up'], 'L0_ffn_e_down': _L0_ffn_in['e_down'], 'L0_c': _L0_c, 'L0_wmod': _L0_wmod}
    _x0 = _d['L0_attn_hidden_states']
    _d['L0_attn_hidden_states'] = jax.random.normal(jax.random.fold_in(jax.random.key(seed), 1), (8, 512, 128), dtype=_x0.dtype)
    del _x0
    return _d

def reference(L0_attn_hidden_states, L0_attn_Wq, L0_attn_Wk, L0_attn_Wv, L0_attn_Wg, L0_attn_Wo, L0_attn_conv_q, L0_attn_conv_k, L0_attn_conv_v, L0_attn_Wgk, L0_attn_Wb, L0_attn_b_b, L0_attn_A_log, L0_attn_dt_bias, L0_attn_g_norm_weight, L0_ffn_norm1_w, L0_ffn_norm2_w, L0_ffn_wq, L0_ffn_wk, L0_ffn_wv, L0_ffn_wo, L0_ffn_router_w, L0_ffn_sh_gate, L0_ffn_sh_up, L0_ffn_sh_down, L0_ffn_e_gate, L0_ffn_e_up, L0_ffn_e_down, L0_c, L0_wmod):

    def _L0_attn_ref(hidden_states, Wq, Wk, Wv, Wg, Wo, conv_q, conv_k, conv_v, Wgk, Wb, b_b, A_log, dt_bias, g_norm_weight):
        import jax, jax.numpy as jnp
        import numpy as np
        import math
        B, L, HID = (2, 512, 128)
        NH, DK, DV = (12, 64, 128)
        KD, VD, CS = (NH * DK, NH * DV, 4)
        SCALE = DK ** (-0.5)

        def _causal_depthwise_conv(x, w):
            c, k = w.shape
            xt = jnp.transpose(x, (0, 2, 1))
            out = jax.lax.conv_general_dilated(xt, w[:, None, :], window_strides=(1,), padding=[(k - 1, 0)], feature_group_count=c, dimension_numbers=('NCH', 'OIH', 'NCH'))
            return jnp.transpose(out, (0, 2, 1))

        def _l2norm(x, eps=1e-06):
            return x * jax.lax.rsqrt(jnp.sum(x * x, axis=-1, keepdims=True) + eps)

        def _gated_delta_net(hidden_states, Wq, Wk, Wv, Wg, Wo, conv_q, conv_k, conv_v, Wgk, Wb, b_b, A_log, dt_bias, g_norm_weight):
            b, l, _ = hidden_states.shape
            q = jax.nn.silu(_causal_depthwise_conv(hidden_states @ Wq, conv_q))
            k = jax.nn.silu(_causal_depthwise_conv(hidden_states @ Wk, conv_k))
            v = jax.nn.silu(_causal_depthwise_conv(hidden_states @ Wv, conv_v))
            gk = -jnp.exp(A_log) * jax.nn.softplus(hidden_states @ Wgk + dt_bias)
            beta = jax.nn.sigmoid(hidden_states @ Wb + b_b)
            q = jnp.transpose(q.reshape(b, l, NH, DK), (0, 2, 1, 3))
            k = jnp.transpose(k.reshape(b, l, NH, DK), (0, 2, 1, 3))
            v = jnp.transpose(v.reshape(b, l, NH, DV), (0, 2, 1, 3))
            q = _l2norm(q) * SCALE
            k = _l2norm(k)
            qs = jnp.moveaxis(q, 2, 0)
            ks_ = jnp.moveaxis(k, 2, 0)
            vs = jnp.moveaxis(v, 2, 0)
            bs = jnp.moveaxis(beta, 1, 0)
            gs = jnp.moveaxis(gk, 1, 0)

            def step(S, inp):
                qt, kt, vt, bt, gt = inp
                S = S * jnp.exp(gt)[..., None, None]
                kv = jnp.einsum('bhk,bhkv->bhv', kt, S)
                delta = (vt - kv) * bt[..., None]
                S = S + jnp.einsum('bhk,bhv->bhkv', kt, delta)
                ot = jnp.einsum('bhk,bhkv->bhv', qt, S)
                return (S, ot)
            S0 = jnp.zeros((b, NH, DK, DV), hidden_states.dtype)
            _, os_ = jax.lax.scan(step, S0, (qs, ks_, vs, bs, gs))
            o = jnp.moveaxis(os_, 0, 1)
            g = (hidden_states @ Wg).reshape(b, l, NH, DV)
            var = jnp.mean(o * o, axis=-1, keepdims=True)
            o = o * jax.lax.rsqrt(var + 1e-05) * g_norm_weight
            o = o * g * jax.nn.sigmoid(g)
            return o.reshape(b, l, VD) @ Wo
        return _gated_delta_net(hidden_states, Wq, Wk, Wv, Wg, Wo, conv_q, conv_k, conv_v, Wgk, Wb, b_b, A_log, dt_bias, g_norm_weight)

    def _L0_ffn_ref(X, norm1_w, norm2_w, wq, wk, wv, wo, router_w, sh_gate, sh_up, sh_down, e_gate, e_up, e_down):
        import jax, jax.numpy as jnp
        import numpy as np
        D_MODEL = 128
        N_HEADS = 16
        D_HEAD = D_MODEL // N_HEADS
        N_EXPERTS = 8
        TOP_K = 2
        D_FF = 256
        EPS = 1e-06

        def rmsnorm(x, w):
            return x * jax.lax.rsqrt(jnp.mean(x * x, axis=-1, keepdims=True) + EPS) * w

        def swiglu(x, w_gate, w_up, w_down):
            return jax.nn.silu(x @ w_gate) * (x @ w_up) @ w_down
        B, S, d = X.shape
        scale = 1.0 / jnp.sqrt(jnp.asarray(D_HEAD, X.dtype))
        h = rmsnorm(X, norm1_w)
        q = (h @ wq).reshape(B, S, N_HEADS, D_HEAD)
        k = (h @ wk).reshape(B, S, N_HEADS, D_HEAD)
        v = (h @ wv).reshape(B, S, N_HEADS, D_HEAD)
        scores = jnp.einsum('bshd,bthd->bhst', q, k) * scale
        attn = jax.nn.softmax(scores, axis=-1)
        ctx = jnp.einsum('bhst,bthd->bshd', attn, v).reshape(B, S, d)
        X = X + ctx @ wo
        h2 = rmsnorm(X, norm2_w).reshape(B * S, d)
        logits = h2 @ router_w
        probs = jax.nn.softmax(logits, axis=-1)
        topw, topi = jax.lax.top_k(probs, TOP_K)
        topw = jax.nn.softmax(topw, axis=-1)
        combine = jnp.sum(jax.nn.one_hot(topi, N_EXPERTS, dtype=h2.dtype) * topw[..., None], axis=1)
        shared = swiglu(h2, sh_gate, sh_up, sh_down)
        gate = jnp.einsum('td,edf->etf', h2, e_gate)
        up = jnp.einsum('td,edf->etf', h2, e_up)
        eout = jnp.einsum('etf,efd->etd', jax.nn.silu(gate) * up, e_down)
        spec = jnp.einsum('etd,te->td', eout, combine)
        moe_out = (shared + spec).reshape(B, S, d)
        return X + moe_out
    x = L0_attn_hidden_states
    mod = (_silu(L0_c) @ L0_wmod).reshape(L0_c.shape[0], 6, 1, -1)
    sa, ca, ga, sb, cb, gb = (mod[:, 0], mod[:, 1], mod[:, 2], mod[:, 3], mod[:, 4], mod[:, 5])
    ga = (2 * (ga >= 0) - 1) * jnp.maximum(jnp.abs(ga), 0.25)
    gb = (2 * (gb >= 0) - 1) * jnp.maximum(jnp.abs(gb), 0.25)
    h = _layernorm(x, axis=-1) * (1 + ca) + sa
    x = x + ga * _L0_attn_ref(h, L0_attn_Wq, L0_attn_Wk, L0_attn_Wv, L0_attn_Wg, L0_attn_Wo, L0_attn_conv_q, L0_attn_conv_k, L0_attn_conv_v, L0_attn_Wgk, L0_attn_Wb, L0_attn_b_b, L0_attn_A_log, L0_attn_dt_bias, L0_attn_g_norm_weight)
    h = _layernorm(x, axis=-1) * (1 + cb) + sb
    x = x + gb * _L0_ffn_ref(h, L0_ffn_norm1_w, L0_ffn_norm2_w, L0_ffn_wq, L0_ffn_wk, L0_ffn_wv, L0_ffn_wo, L0_ffn_router_w, L0_ffn_sh_gate, L0_ffn_sh_up, L0_ffn_sh_down, L0_ffn_e_gate, L0_ffn_e_up, L0_ffn_e_down)
    return x

_drawn_inputs = setup_inputs


def setup_inputs(seed=0):
    import zlib

    import numpy as np

    out = dict(_drawn_inputs(seed))
    spreads = {'L0_attn_g_norm_weight': (1.0, 0.554),
     'L0_ffn_norm1_w': (1.0, 0.6),
     'L0_ffn_norm2_w': (1.0, 0.6)}
    factors = {'L0_attn_b_b': 8.0,
     'L0_ffn_wq': 8.0,
     'L0_ffn_wk': 8.0,
     'L0_ffn_wv': 8.0,
     'L0_ffn_wo': 8.0,
     'L0_ffn_router_w': 8.0,
     'L0_ffn_sh_gate': 8.0,
     'L0_ffn_sh_up': 8.0,
     'L0_ffn_sh_down': 8.0,
     'L0_ffn_e_gate': 8.0,
     'L0_ffn_e_up': 8.0,
     'L0_ffn_e_down': 8.0}
    for name, (base, spread) in spreads.items():
        noise = np.random.default_rng([zlib.crc32(name.encode()), seed]).standard_normal(out[name].shape)
        drawn = base * np.exp(spread * noise) if base else spread * noise
        out[name] = jnp.asarray(drawn.astype(out[name].dtype))
    for name, factor in factors.items():
        out[name] = (out[name] * factor).astype(out[name].dtype)
    return out
```

```python
from contextlib import ExitStack

import concourse.bass as bass
from concourse import mybir

F32 = mybir.dt.float32
BF16 = mybir.dt.bfloat16
ALU = mybir.AluOpType
ACT = mybir.ActivationFunctionType
AX = mybir.AxisListType.X

B, L, HID = 8, 512, 128
NH, DK, DV = 12, 64, 128
TAPS = 4
PAD = TAPS - 1
CK = 64
PAIRS = B // 2
TILES = L // CK
HALF = TILES // 2
KD, VD = NH * DK, NH * DV
NP = NH // 2
G3 = 3
SYS = HALF * NH
BASE = 16
NBLK = 128 // BASE
AH, AD = 16, 8
SLOT = 64
TQ = L // 128
NE, DFF = 8, 256
NEG = -30000.0


class Phase:

    def __init__(self, nc, tag=""):
        self.nc, self.ctx, self.sems, self.tag = nc, ExitStack(), [], tag

    def sb(self, name, shape, dt=F32):
        return self.ctx.enter_context(self.nc.sbuf_tensor(name + self.tag, shape, dt))

    def ps(self, name, shape, dt=F32):
        return self.ctx.enter_context(self.nc.psum_tensor(name + self.tag, shape, dt))

    def sem(self, name):
        s = self.ctx.enter_context(self.nc.semaphore(name + self.tag))
        self.sems.append(s.num)
        return s

    def close(self):
        self.ctx.close()
        self.nc.all_engine_barrier(sems_to_clear=range(min(self.sems), max(self.sems) + 1))


def linker(eng, sem):
    count = [0]

    def link(ins):
        count[0] += 1
        ins.then_inc(sem, 1)
        eng.wait_ge(sem, count[0])

    return link


def bc(ap, *shape):
    return ap.broadcast_to(list(shape))


def load_weights(nc, t, src):
    p = Phase(nc)
    raw = p.sb("raw_w", [128, 2 * KD + VD])
    taps = p.sb("taps_row", [1, (2 * KD + VD) * TAPS])
    row = p.sb("head_row", [1, 3 * NH])
    crow = p.sb("c_row", [B, HID])
    wmod = p.sb("wmod_sb", [HID, 6 * HID])
    csil = p.sb("c_silu", [B, HID])
    cT = p.sb("c_silu_T", [HID, B])
    msgn = p.sb("mod_sign", [B, HID])
    mabs = p.sb("mod_abs", [B, HID])
    blk8 = p.sb("blk8", [128, NBLK])
    blk8s = p.sb("blk8_shift", [128, NBLK])
    gnw = p.sb("gnw", [DV, 1])
    tap_ps = p.ps("tap_ps", [128, 4, 512])
    misc_ps = p.ps("misc_ps", [128, 4, 512])
    loaded, consts, pchain, vchain = p.sem("loaded"), p.sem("consts"), p.sem("pool_chain"), p.sem("vec_chain")
    tap_done, tap_used = p.sem("tap_done"), p.sem("tap_used")
    a_log, row_done, c_silu, cT_ps, cT_sb, mod_ps, nA_done = (p.sem(n) for n in (
        "a_log", "row_done", "c_silu_done", "cT_ps", "cT_sb", "mod_ps_done", "nA_done"))
    cols = 2 * KD + VD
    chunks = cols // 512
    with nc.Block() as block:
        @block.sync
        def _(sp):
            n = 0
            for name, at, w in (("L0_attn_Wk", 0, KD), ("L0_attn_Wq", KD, KD), ("L0_attn_Wv", 2 * KD, VD)):
                sp.dma_start(raw[:, at:at + w], src[name]).then_inc(loaded, 16)
                n += 1
            for name, at, w in (("L0_attn_conv_k", 0, KD), ("L0_attn_conv_q", KD, KD), ("L0_attn_conv_v", 2 * KD, VD)):
                sp.dma_start(taps[:, at * TAPS:(at + w) * TAPS],
                             src[name].rearrange("(a c) k -> a (c k)", a=1)).then_inc(loaded, 16)
            for name, at in (("L0_attn_dt_bias", 0), ("L0_attn_b_b", NH), ("L0_attn_A_log", 2 * NH)):
                sp.dma_start(row[:, at:at + NH], src[name].rearrange("(a c) -> a c", a=1)).then_inc(loaded, 16)
            sp.dma_start(crow[:, :], src["L0_c"]).then_inc(loaded, 16)
            sp.dma_start(wmod[:, :], src["L0_wmod"]).then_inc(loaded, 16)
            sp.dma_start(t.wg[:, :], src["L0_attn_Wg"]).then_inc(loaded, 16)
            sp.dma_start(t.wo[:, :, :], src["L0_attn_Wo"].rearrange("(h p) d -> p h d", p=DV)).then_inc(loaded, 16)
            sp.dma_start(t.wgb[:, 0:NH], src["L0_attn_Wgk"]).then_inc(loaded, 16)
            sp.dma_start(t.wgb[:, NH:2 * NH], src["L0_attn_Wb"]).then_inc(loaded, 16)
            for m, name in enumerate(("L0_ffn_wq", "L0_ffn_wk", "L0_ffn_wv")):
                sp.dma_start(t.wqkv[:, m * HID:(m + 1) * HID], src[name]).then_inc(loaded, 16)
            sp.dma_start(t.wo2[:, :], src["L0_ffn_wo"]).then_inc(loaded, 16)
            sp.dma_start(t.wr[:, :], src["L0_ffn_router_w"]).then_inc(loaded, 16)
            sp.dma_start(gnw[:, :], src["L0_attn_g_norm_weight"].rearrange("(p a) -> p a", a=1)).then_inc(loaded, 16)
            sp.dma_start(t.n1w[:, :], src["L0_ffn_norm1_w"].rearrange("(p a) -> p a", a=1)).then_inc(loaded, 16)
            sp.dma_start(t.n2w[:, :], src["L0_ffn_norm2_w"].rearrange("(p a) -> p a", a=1)).then_inc(loaded, 16)
        NLOAD = 16 * 23

        @block.gpsimd
        def _(g):
            link = linker(g, pchain)
            link(g.memset(t.ident[:, :], 0.0))
            link(g.affine_select(out=t.ident[:, :], in_=t.ident[:, :], compare_op=ALU.not_equal, fill=1.0,
                                 base=0, pattern=[[-1, 128]], channel_multiplier=1))
            g.memset(t.ones[:, :], 1.0).then_inc(consts, 1)
            link(g.memset(t.later[:, :], 1.0))
            link(g.affine_select(out=t.later[:, :], in_=t.later[:, :], compare_op=ALU.is_gt, fill=0.0,
                                 base=0, pattern=[[-1, 128]], channel_multiplier=1))
            link(g.memset(t.later[CK:128, 0:CK], 0.0))
            link(g.memset(t.upto[:, :], 1.0))
            link(g.affine_select(out=t.upto[:, :], in_=t.upto[:, :], compare_op=ALU.is_ge, fill=0.0,
                                 base=0, pattern=[[1, 128]], channel_multiplier=-1))
            link(g.memset(t.upto[0:CK, CK:128], 0.0))
            link(g.tensor_copy(t.tri[0:CK, :], t.upto[0:CK, 0:CK]))
            link(g.tensor_copy(t.tri[CK:128, :], t.upto[CK:128, CK:128]))
            for m, off in ((blk8, 0), (blk8s, BASE)):
                link(g.memset(m[:, :], 1.0))
                link(g.affine_select(out=m[:, :], in_=m[:, :], compare_op=ALU.is_ge, fill=0.0,
                                     base=-off, pattern=[[-BASE, NBLK]], channel_multiplier=1))
                link(g.affine_select(out=m[:, :], in_=m[:, :], compare_op=ALU.is_ge, fill=0.0,
                                     base=off + BASE - 1, pattern=[[BASE, NBLK]], channel_multiplier=-1))
            link(g.memset(blk8s[:, 1:NBLK:2], 0.0))
            for s in range(2):
                rows = slice(s * CK, (s + 1) * CK)
                link(g.tensor_copy(t.blk[rows, :], blk8[rows, 4 * s:4 * s + 4]))
                link(g.tensor_copy(t.low16[rows, :].rearrange("p (b c) -> p b c", c=BASE),
                                   bc(blk8s[rows, 4 * s:4 * s + 4].unsqueeze(2), CK, 4, BASE)))
            link(g.memset(t.low32[:, :], 0.0))
            link(g.memset(t.low32[32:64, 0:32], 1.0))
            link(g.memset(t.low32[96:128, 0:32], 1.0))
            link(g.memset(t.mhalf[:, :], -0.5))
            for b in range(NE):
                link(g.memset(t.rank[:, b:b + 1], float(NE - b)))
            link(g.memset(t.pick[:, :, :], 0.0))
            link(g.affine_select(out=t.pick[:, :, :], in_=t.pick[:, :, :], compare_op=ALU.not_equal, fill=1.0,
                                 base=0, pattern=[[-2, PAIRS], [-1, 2]], channel_multiplier=1))
            g.memset(t.gmask[:, :, :, :], 0.0).then_inc(consts, 1)

        @block.scalar
        def _(a):
            a.wait_ge(loaded, NLOAD)
            a.activation(csil[:, :], crow[:, :], ACT.Silu).then_inc(c_silu, 1)
            a.wait_ge(cT_ps, 1)
            a.activation(cT[:, :], misc_ps[:, 1, 0:B], ACT.Copy).then_inc(cT_sb, 1)
            a.wait_ge(a_log, 1)
            a.activation(t.nA[:, :], t.nA[:, :], ACT.Exp).then_inc(nA_done, 1)

        @block.tensor
        def _(pe):
            pe.wait_ge(loaded, NLOAD)
            pe.wait_ge(consts, 2)
            pe.matmul(misc_ps[:, 0, 0:3 * NH], t.ones[0:1, :], row[:, :], start=True, stop=True).then_inc(row_done, 1)
            pe.wait_ge(c_silu, 1)
            pe.transpose(misc_ps[:, 1, 0:B], csil[:, :], t.ident[0:B, 0:B]).then_inc(cT_ps, 1)
            tv = taps[:, :].rearrange("a (c k) -> a k c", k=TAPS)
            n = 0
            for j in range(TAPS):
                for c in range(chunks):
                    if n >= 4:
                        pe.wait_ge(tap_used, n - 3)
                    pe.matmul(tap_ps[:, n % 4, :], t.ones[0:1, :], tv[:, j, c * 512:(c + 1) * 512],
                              start=True, stop=True).then_inc(tap_done, 1)
                    n += 1
            pe.wait_ge(cT_sb, 1)
            for c in range(2):
                m = pe.matmul(misc_ps[0:B, 2 + c, 0:384], cT[:, :], wmod[:, c * 384:(c + 1) * 384], start=True, stop=True)
            m.then_inc(mod_ps, 1)

        @block.vector
        def _(v):
            link = linker(v, vchain)
            v.wait_ge(loaded, NLOAD)
            v.wait_ge(consts, 2)
            n = 0
            for j in range(TAPS):
                for c in range(chunks):
                    v.wait_ge(tap_done, n + 1)
                    v.tensor_tensor(t.wc[:, j, c * 512:(c + 1) * 512], tap_ps[:, n % 4, :],
                                    raw[:, c * 512:(c + 1) * 512], ALU.mult).then_inc(tap_used, 1)
                    n += 1
            v.wait_ge(row_done, 1)
            link(v.tensor_copy(t.hrow[:, :], misc_ps[:, 0, 0:2 * NH]))
            v.tensor_copy(t.nA[:, :], misc_ps[:, 0, 2 * NH:3 * NH]).then_inc(a_log, 1)
            v.wait_ge(nA_done, 1)
            link(v.tensor_scalar(t.nA[:, :], t.nA[:, :], -1.0, None, ALU.mult))
            link(v.tensor_scalar(t.wo[:, :, :].rearrange("p h d -> p (h d)"), t.wo[:, :, :].rearrange("p h d -> p (h d)"),
                                 gnw[:, 0:1], None, ALU.mult))
            link(v.tensor_copy(t.identb[:, :], t.ident[:, :]))
            for k in range(NP):
                link(v.tensor_scalar(t.negm[:, k * CK:(k + 1) * CK], t.tri[:, :], -NEG, NEG, ALU.mult, ALU.add))
            v.wait_ge(mod_ps, 1)
            for m in range(6):
                o, i = t.mod[:, m * HID:(m + 1) * HID], misc_ps[0:B, 2 + m // 3, (m % 3) * HID:(m % 3 + 1) * HID]
                if m % 3 == 0:
                    link(v.tensor_copy(o, i))
                elif m % 3 == 1:
                    link(v.tensor_scalar(o, i, 1.0, None, ALU.add))
                else:
                    link(v.tensor_scalar(msgn[:, :], i, 0.0, 2.0, ALU.is_ge, ALU.mult))
                    link(v.tensor_scalar(mabs[:, :], i, -1.0, None, ALU.mult))
                    link(v.tensor_tensor(mabs[:, :], i, mabs[:, :], ALU.max))
                    link(v.tensor_scalar(mabs[:, :], mabs[:, :], 0.25, None, ALU.max))
                    link(v.tensor_scalar(msgn[:, :], msgn[:, :], -1.0, None, ALU.add))
                    link(v.tensor_tensor(o, msgn[:, :], mabs[:, :], ALU.mult))
    p.close()


def start_pair(nc, t, src, i):
    p = Phase(nc)
    cen, sq = p.sb("cen", [128, TILES, HID]), p.sb("sq", [128, TILES, HID])
    st = p.sb("ln_st", [128, 2, TILES])
    sel = p.sb("sel", [B, 128])
    zg, zb, za, ze = (p.sb(n, [128, TILES, NH]) for n in ("zg", "zb", "za", "ze"))
    hT = p.sb("hT", [128, 2, PAD + L])
    ps = p.ps("ps_a1", [128, 8, 512])
    x_in, vch, pow_in, pow_out, sel_ok, mod_ok = (p.sem(n) for n in ("x_in", "vch", "pow_in", "pow_out", "sel_ok", "mod_ok"))
    modbc, h_ok, hT_ps, hT_ok, z_ps, z_ok = (p.sem(n) for n in ("modbc_ok", "h_ok", "hT_ps", "hT_ok", "z_ps", "z_ok"))
    e_ok, l_in, l_ok, g_ok, stat_ps, stat_ok = (p.sem(n) for n in ("e_ok", "l_in", "l_ok", "g_ok", "stat_ps", "stat_ok"))
    beta_ok, s0, pad_ok, hS_ok, hS_pool = (p.sem(n) for n in ("beta_ok", "s0", "pad_ok", "hS_ok", "hS_pool"))
    with nc.Block() as block:
        @block.sync
        def _(sp):
            for s in range(2):
                sp.dma_start(t.x[s * CK:(s + 1) * CK, :, :],
                             src["L0_attn_hidden_states"][bass.ds(2 * i + s, 1), :, :]
                             .rearrange("a (c t) d -> t (a c) d", t=CK)).then_inc(x_in, 16)

        @block.gpsimd
        def _(g):
            g.memset(hT[:, :, 0:PAD], 0.0).then_inc(pad_ok, 1)
            g.memset(t.S[:, :, :, :], 0.0).then_inc(s0, 1)
            g.wait_ge(pow_in, 1)
            g.tensor_tensor(st[:, 1, :], st[:, 1, :], t.mhalf[:, 0:TILES], ALU.pow).then_inc(pow_out, 1)
            g.wait_ge(hT_ok, 2)
            g.wait_ge(pad_ok, 1)
            for s in range(2):
                for j in (1, 0):
                    g.tensor_copy(t.hS[:, j, :, s * CK:(s + 1) * CK],
                                  hT[:, s, j:j + L].rearrange("p (c t) -> p c t", c=TILES)).then_inc(hS_pool, 1)

        @block.vector
        def _(v):
            link = linker(v, vch)

            v.tensor_copy(sel[:, :].rearrange("b (s t) -> b s t", s=2),
                          bc(t.pick[:, bass.ds(i, 1), :].rearrange("b a s -> b (a s)").unsqueeze(2), B, 2, CK)).then_inc(sel_ok, 1)
            v.wait_ge(x_in, 32)
            sh = [128, TILES, HID]
            link(v.tensor_reduce(st[:, 0, :], t.x[:, :, :], AX, ALU.add))
            link(v.tensor_scalar(st[:, 0, :], st[:, 0, :], 1.0 / HID, None, ALU.mult))
            link(v.tensor_tensor(cen[:, :, :], t.x[:, :, :], bc(st[:, 0, :].unsqueeze(2), *sh), ALU.subtract))
            link(v.tensor_tensor(sq[:, :, :], cen[:, :, :], cen[:, :, :], ALU.mult))
            link(v.tensor_reduce(st[:, 1, :], sq[:, :, :], AX, ALU.add))
            v.tensor_scalar(st[:, 1, :], st[:, 1, :], 1.0 / HID, 1e-5, ALU.mult, ALU.add).then_inc(pow_in, 1)
            v.wait_ge(mod_ok, 1)
            v.tensor_copy(t.modbc[:, 0:512], ps[:, 0, :]).then_inc(modbc, 1)
            v.tensor_copy(t.modbc[:, 512:768], ps[:, 1, 0:256]).then_inc(modbc, 1)
            v.wait_ge(pow_out, 1)
            link(v.tensor_tensor(cen[:, :, :], cen[:, :, :], bc(st[:, 1, :].unsqueeze(2), *sh), ALU.mult))
            v.wait_ge(modbc, 2)
            link(v.tensor_tensor(cen[:, :, :], cen[:, :, :], bc(t.modbc[:, HID:2 * HID].unsqueeze(1), *sh), ALU.mult))
            v.tensor_tensor(cen[:, :, :], cen[:, :, :], bc(t.modbc[:, 0:HID].unsqueeze(1), *sh), ALU.add).then_inc(h_ok, 1)
            v.wait_ge(z_ps, 1)
            z = ps[:, 4, 0:TILES * 2 * NH].rearrange("p (c z) -> p c z", c=TILES)
            hs = [128, TILES, NH]
            link(v.tensor_tensor(zg[:, :, :], z[:, :, 0:NH], bc(t.hrow[:, 0:NH].unsqueeze(1), *hs), ALU.add))
            v.tensor_tensor(zb[:, :, :], z[:, :, NH:2 * NH], bc(t.hrow[:, NH:2 * NH].unsqueeze(1), *hs), ALU.add).then_inc(z_ok, 1)
            link(v.tensor_scalar(za[:, :, :], zg[:, :, :], -1.0, None, ALU.mult))
            v.tensor_tensor(za[:, :, :], zg[:, :, :], za[:, :, :], ALU.max).then_inc(z_ok, 1)
            v.wait_ge(e_ok, 1)
            v.tensor_scalar(ze[:, :, :], ze[:, :, :], 1.0, None, ALU.add).then_inc(l_in, 1)
            link(v.tensor_scalar(zg[:, :, :], zg[:, :, :], 0.0, None, ALU.max))
            v.wait_ge(l_ok, 1)
            link(v.tensor_tensor(zg[:, :, :], zg[:, :, :], ze[:, :, :], ALU.add))
            link(v.tensor_tensor(t.g[:, :, :], zg[:, :, :], bc(t.nA[:, :].unsqueeze(1), *hs), ALU.mult))
            v.tensor_copy(t.gmask[0:CK, :, 0, :], t.g[0:CK, :, :]).then_inc(g_ok, 1)
            v.tensor_copy(t.gmask[CK:128, :, 1, :], t.g[CK:128, :, :]).then_inc(g_ok, 1)
            v.wait_ge(stat_ok, 4)
            v.wait_ge(beta_ok, 1)
            link(v.tensor_tensor(t.kdec[:, :, :], t.kdec[:, :, :], t.beta[:, :, :], ALU.mult))
            link(v.tensor_scalar(t.nGam[:, :, :], t.Gam[:, :, :], -1.0, None, ALU.mult))

        @block.scalar
        def _(a):
            for b in range(2):
                a.wait_ge(hT_ps, b + 1)
                a.activation(hT[:, :, PAD + 256 * b:PAD + 256 * (b + 1)].rearrange("p s (c t) -> p c s t", c=4),
                             ps[:, 2 + b, :].rearrange("p (c s t) -> p c s t", c=4, s=2), ACT.Copy).then_inc(hT_ok, 1)
            a.wait_ge(hT_ok, 2)
            a.wait_ge(pad_ok, 1)
            for s in range(2):
                for j in (3, 2):
                    a.activation(t.hS[:, j, :, s * CK:(s + 1) * CK],
                                 hT[:, s, j:j + L].rearrange("p (c t) -> p c t", c=TILES), ACT.Copy).then_inc(hS_ok, 1)
            a.wait_ge(z_ok, 1)
            a.activation(t.beta[:, :, :], zb[:, :, :], ACT.Sigmoid).then_inc(beta_ok, 1)
            a.wait_ge(z_ok, 2)
            a.activation(ze[:, :, :], za[:, :, :], ACT.Exp, scale=-1.0).then_inc(e_ok, 1)
            a.wait_ge(l_in, 1)
            a.activation(ze[:, :, :], ze[:, :, :], ACT.Ln).then_inc(l_ok, 1)
            a.wait_ge(stat_ps, 1)
            w = TILES * NH
            a.activation(t.Gam[:, :, :].rearrange("p c h -> p (c h)"), ps[:, 5, 0:w], ACT.Exp).then_inc(stat_ok, 1)
            a.activation(t.kdec[:, :, :].rearrange("p c h -> p (c h)"), ps[:, 6, 0:w], ACT.Exp).then_inc(stat_ok, 1)
            gv = ps[:, 7, 0:2 * w].rearrange("p (c s h r) -> p r (c s) h", c=TILES, s=2, r=2)
            for r in range(2):
                rows = slice(r * 64, (r + 1) * 64)
                a.activation(t.gam_all[rows, :, :, :].rearrange("p c s h -> p (c s) h"),
                             gv[rows, r, :, :], ACT.Exp).then_inc(stat_ok, 1)

        @block.tensor
        def _(pe):
            pe.wait_ge(sel_ok, 1)
            pe.matmul(ps[:, 0, :], sel[:, :], t.mod[:, 0:512], start=True, stop=True)
            pe.matmul(ps[:, 1, 0:256], sel[:, :], t.mod[:, 512:768], start=True, stop=True).then_inc(mod_ok, 1)
            pe.wait_ge(h_ok, 1)
            for c in range(TILES):
                m = pe.transpose(ps[:, 2 + c // 4, (c % 4) * 128:(c % 4 + 1) * 128], cen[:, c, :], t.ident[:, :])
                if c % 4 == 3:
                    m.then_inc(hT_ps, 1)
            pe.wait_ge(hS_ok, 4)
            for c in range(TILES):
                m = pe.matmul(ps[:, 4, c * 2 * NH:(c + 1) * 2 * NH], t.hS[:, TAPS - 1, c, :],
                              t.wgb[:, :], start=True, stop=True)
            m.then_inc(z_ps, 1)
            pe.wait_ge(g_ok, 2)
            gf = t.g[:, :, :].rearrange("p c h -> p (c h)")
            pe.matmul(ps[:, 5, 0:TILES * NH], t.upto[:, :], gf, start=True, stop=True)
            pe.matmul(ps[:, 6, 0:TILES * NH], t.later[:, :], gf, start=True, stop=True)
            pe.matmul(ps[:, 7, 0:2 * TILES * NH], t.ones[:, :], t.gmask[:, :, :, :].rearrange("p c s h -> p (c s h)"),
                      start=True, stop=True).then_inc(stat_ps, 1)
    p.close()


def project_keys(nc, t, half):
    p = Phase(nc, f"_{half}")
    kq = p.sb("kq", [128, 2, 2 * NH, DK])
    sq = p.sb("kq_sq", [128, 2 * NH, DK])
    ss = p.sb("kq_ss", [128, 2 * NH])
    co = p.sb("kq_coef", [128, 3, NH])
    kn, qn, qg = (p.sb(n, [128, KD]) for n in ("kn", "qn", "qg"))
    seg = p.sb("seg_rhs", [128, NH, CK])
    ex = p.sb("decay", [128, NH, CK])
    pj = [p.ps(f"proj{b}", [128, 512]) for b in range(3)]
    tp = [p.ps(f"trp{b}", [128, 512]) for b in range(2)]
    sg = p.ps("seg_ps", [128, 512])
    kk = [p.ps(f"kk{b}", [128, 512]) for b in range(2)]
    names = ("proj_ps", "silu_done", "sq_done", "ss_done", "rs_done", "coef_done", "kn_done", "qn_done", "qg_done",
             "kdc_done", "seg_rhs_done", "seg_ps", "exp_done", "decay_done", "trp_ps", "trp_used", "kk_ps", "kk_used",
             "vch2", "ss_eps")
    (proj_ps, silu, sq_done, ss_done, rs_done, coef, kn_done, qn_done, qg_done, kdc_done, seg_rhs, seg_ps, exp_done,
     decay, trp_ps, trp_used, kk_ps, kk_used, vch, ss_eps) = (p.sem(n) for n in names)
    sh = [128, NH, DK]
    with nc.Block() as block:
        @block.tensor
        def _(pe):
            def project(c):
                for b in range(3):
                    if c:
                        pe.wait_ge(silu, 3 * (c - 1) + b + 1)
                    for j in range(TAPS):
                        m = pe.matmul(pj[b][:, :], t.hS[:, j, half * HALF + c, :], t.wc[:, j, b * 512:(b + 1) * 512],
                                      start=j == 0, stop=j == TAPS - 1)
                    m.then_inc(proj_ps, 1)

            def segments(c):
                pe.wait_ge(seg_rhs, c + 1)
                for k in range(2):
                    n = 2 * c + k
                    if n:
                        pe.wait_ge(exp_done, n)
                    o = sg[:, 0:NP * CK]
                    pe.matmul(o, t.later[:, :], seg[:, k * NP:(k + 1) * NP, :].rearrange("p h i -> p (h i)"),
                              start=True, stop=False)
                    pe.matmul(o, t.identb[:, :], t.negm[:, 0:NP * CK], start=False, stop=True).then_inc(seg_ps, 1)

            def transposes(c, which, source):
                for k in range(2):
                    n = 6 * c + 2 * which + k
                    if n >= 2:
                        pe.wait_ge(trp_used, n - 1)
                    for q in range(3):
                        b = 3 * k + q
                        m = pe.transpose(tp[n % 2][:, q * 128:(q + 1) * 128], source[:, b * 128:(b + 1) * 128], t.ident[:, :])
                    m.then_inc(trp_ps, 1)

            def products(c):
                pe.wait_ge(trp_used, 6 * c + 4)
                for q in range(4):
                    n = 4 * c + q
                    if n >= 2:
                        pe.wait_ge(kk_used, n - 1)
                    ph, r = q // 2, q % 2
                    rows = slice(r * 64, (r + 1) * 64)
                    for k in range(G3):
                        for s in range(2):
                            cs = slice(s * CK, (s + 1) * CK)
                            m = pe.matmul(kk[n % 2][cs, k * 128:(k + 1) * 128], t.kqT[rows, c, 3 * ph + k, 0, cs],
                                          t.kqT[rows, c, 3 * ph + k, :, cs], start=True, stop=True)
                    m.then_inc(kk_ps, 1)

            project(0)
            for c in range(HALF):
                segments(c)
                if c + 1 < HALF:
                    project(c + 1)
                pe.wait_ge(kn_done, c + 1)
                transposes(c, 0, kn)
                pe.wait_ge(qn_done, c + 1)
                transposes(c, 1, qn)
                products(c)
                pe.wait_ge(qg_done, c + 1)
                transposes(c, 2, qg)

        @block.scalar
        def _(a):
            def silus(c):
                if c >= 2:
                    a.wait_ge(qg_done, c - 1)
                    a.wait_ge(kdc_done, c - 1)
                    a.wait_ge(qn_done, c - 1)
                for b in range(3):
                    a.wait_ge(proj_ps, 3 * c + b + 1)
                    a.activation(kq[:, c % 2, :, :].rearrange("p h d -> p (h d)")[:, b * 512:(b + 1) * 512], pj[b][:, :],
                                 ACT.Silu).then_inc(silu, 1)
                if c:
                    a.wait_ge(ss_done, c)
                a.wait_ge(silu, 3 * c + 3)
                a.activation(sq[:, :, :], kq[:, c % 2, :, :], ACT.Square).then_inc(sq_done, 1)

            def copies(c, which):
                for k in range(2):
                    n = 6 * c + 2 * which + k
                    a.wait_ge(trp_ps, n + 1)
                    if which == 2 and k == 0:
                        a.wait_ge(kk_ps, 4 * (c + 1))
                    a.activation(t.kqT[:, c, 3 * k:3 * k + 3, min(which, 1), :],
                                 tp[n % 2][:, 0:384].rearrange("p (b i) -> p b i", b=3), ACT.Copy).then_inc(trp_used, 1)

            silus(0)
            for c in range(HALF):
                for k in range(2):
                    a.wait_ge(seg_ps, 2 * c + k + 1)
                    if c and k == 0:
                        a.wait_ge(kk_used, 4 * c)
                    a.activation(ex[:, k * NP:(k + 1) * NP, :].rearrange("p h i -> p (h i)"), sg[:, 0:NP * CK],
                                 ACT.Exp).then_inc(exp_done, 1)
                if c + 1 < HALF:
                    silus(c + 1)
                copies(c, 0)
                copies(c, 1)
                copies(c, 2)

        @block.vector
        def _(v):
            link = linker(v, vch)

            def norms(c):
                C = half * HALF + c
                if c:
                    v.wait_ge(seg_ps, 2 * c)
                v.tensor_tensor(seg[:, :, :], bc(t.g[:, C, :].unsqueeze(2), *sh), bc(t.tri[:, :].unsqueeze(1), *sh),
                                ALU.mult).then_inc(seg_rhs, 1)
                v.wait_ge(sq_done, c + 1)
                v.tensor_reduce(ss[:, :], sq[:, :, :], AX, ALU.add).then_inc(ss_done, 1)
                v.wait_ge(ss_done, c + 1)
                if c:
                    v.wait_ge(qg_done, c)
                    v.wait_ge(kdc_done, c)
                v.tensor_scalar(ss[:, :], ss[:, :], 1e-6, None, ALU.add).then_inc(ss_eps, 1)
                v.wait_ge(rs_done, c + 1)
                link(v.tensor_tensor(co[:, 0, :], ss[:, 0:NH], t.kdec[:, C, :], ALU.mult))
                link(v.tensor_scalar(co[:, 1, :], ss[:, NH:2 * NH], DK ** -0.5, None, ALU.mult))
                v.tensor_tensor(co[:, 2, :], co[:, 1, :], t.Gam[:, C, :], ALU.mult).then_inc(coef, 1)
                if c:
                    v.wait_ge(trp_ps, 6 * (c - 1) + 4)
                v.tensor_tensor(kn[:, :].rearrange("p (h d) -> p h d", d=DK), kq[:, c % 2, 0:NH, :],
                                bc(ss[:, 0:NH].unsqueeze(2), *sh), ALU.mult).then_inc(kn_done, 1)
                v.tensor_tensor(qn[:, :].rearrange("p (h d) -> p h d", d=DK), kq[:, c % 2, NH:2 * NH, :],
                                bc(co[:, 1, :].unsqueeze(2), *sh), ALU.mult).then_inc(qn_done, 1)
                v.wait_ge(kn_done, c + 1)

            def decays(c):
                v.wait_ge(decay, c + 1)
                for q in range(4):
                    v.wait_ge(kk_ps, 4 * c + q + 1)
                    h0 = 6 * (q // 2) + q % 2
                    v.tensor_tensor(t.ap[:, c, h0:h0 + 5:2, :, :],
                                    kk[(4 * c + q) % 2][:, 0:384].rearrange("p (h m i) -> p h m i", h=G3, m=2),
                                    bc(ex[:, h0:h0 + 5:2, :].unsqueeze(2), 128, G3, 2, CK), ALU.mult).then_inc(kk_used, 1)

            for c in range(HALF):
                norms(c)
                decays(c)

        @block.gpsimd
        def _(g):
            for c in range(HALF):
                C = half * HALF + c
                g.wait_ge(ss_eps, c + 1)
                g.tensor_tensor(ss[:, :], ss[:, :], t.mhalf[:, 0:2 * NH], ALU.pow).then_inc(rs_done, 1)
                g.wait_ge(exp_done, 2 * c + 2)
                g.tensor_tensor(ex[:, :, :], ex[:, :, :], bc(t.beta[:, C, :].unsqueeze(2), *sh), ALU.mult).then_inc(decay, 1)
                g.wait_ge(coef, c + 1)
                g.wait_ge(silu, 3 * c + 3)
                g.tensor_tensor(t.kd[:, c, :].rearrange("p (h d) -> p h d", d=DK), kq[:, c % 2, 0:NH, :],
                                bc(co[:, 0, :].unsqueeze(2), *sh), ALU.mult).then_inc(kdc_done, 1)
                if c:
                    g.wait_ge(trp_ps, 6 * c)
                g.tensor_tensor(qg[:, :].rearrange("p (h d) -> p h d", d=DK), kq[:, c % 2, NH:2 * NH, :],
                                bc(co[:, 2, :].unsqueeze(2), *sh), ALU.mult).then_inc(qg_done, 1)
    p.close()


def invert_systems(nc, t, half):
    p = Phase(nc, f"_{half}")
    a16 = p.sb("a16", [SYS, BASE, NBLK, BASE])
    t16 = p.sb("t16", [SYS, BASE, NBLK, BASE])
    c16 = a16
    c16_ok = p.sem("c16_ok")
    tn = p.sb("t_plain", [128, SYS, CK])
    xs = p.sb("x_sb", [128, 2, 8, CK])
    tmp = xs[0:SYS, :, :, :].rearrange("g a b c -> g (a b c)")
    ps = p.ps("ps_inv", [128, 8, 512])
    sel_ps, a16_ok, sub, back_ps, tt_ok, x_ps, x_ok, y_ps, y_ok = (p.sem(n) for n in (
        "sel_ps", "a16_ok", "sub", "back_ps", "blocks_ok", "x_ps", "x_ok", "y_ps", "y_ok"))
    av = t.ap[:, :, :, :, :].rearrange("p c h m i -> p (c h) m i")
    GB = 8
    JOBS = SYS // GB
    SUBS = 2 * (BASE - 1)
    unit_ok = p.sem("unit_ok")
    with nc.Block() as block:
        @block.tensor
        def _(pe):
            idv = t.ident[:, :].rearrange("p (s b j) -> p s b j", s=2, b=4)
            for i in range(BASE):
                for b in range(4):
                    o = ps[0:SYS, i // 4, (i % 4) * 128:(i % 4 + 1) * 128].rearrange("p (s b j) -> p s b j", s=2, b=4)
                    m = pe.matmul(o[:, :, b, :], av[:, :, 0, b * BASE + i], idv[:, :, b, :], start=True, stop=True)
                if i % 4 == 3:
                    m.then_inc(sel_ps, 1)
            pe.wait_ge(sub, SUBS)
            for i in range(BASE):
                m = pe.transpose(ps[:, 4 + i // 8, (i % 8) * SYS:(i % 8 + 1) * SYS],
                                 t16[:, i, :, :].rearrange("g b j -> g (b j)"), t.ident[0:SYS, 0:SYS])
                if i % 8 == 7:
                    m.then_inc(back_ps, 1)
            pe.wait_ge(c16_ok, 1)
            for j in range(BASE):
                m = pe.transpose(ps[:, 6 + j // 8, (j % 8) * SYS:(j % 8 + 1) * SYS],
                                 c16[:, j, :, :].rearrange("g b i -> g (b i)"), t.ident[0:SYS, 0:SYS])
                if j % 8 == 7:
                    m.then_inc(back_ps, 1)

            def times(bank, lhs, rhs):
                for k in range(GB):
                    for s in range(2):
                        rows = slice(s * CK, (s + 1) * CK)
                        m = pe.matmul(ps[rows, bank, k * CK:(k + 1) * CK], lhs(rows, k), rhs(rows, k),
                                      start=True, stop=True)
                return m
            pe.wait_ge(tt_ok, 4)
            for step in range(2):
                for n in range(JOBS + 1):
                    if n < JOBS:
                        if step:
                            pe.wait_ge(y_ok, 2 * (n + 1))
                        N = step * JOBS + n
                        if N >= 4:
                            pe.wait_ge(x_ok, N - 3)
                        times(N % 4, lambda rows, k: av[rows, GB * n + k, 0, :],
                              lambda rows, k: tn[rows, GB * n + k, :]).then_inc(x_ps, 1)
                    if n >= 1:
                        N = step * JOBS + n - 1
                        pe.wait_ge(x_ok, N + 1)
                        for u in range(2 - step):
                            Y = 2 * (n - 1) + u if not step else 2 * JOBS + n - 1
                            if Y >= 4:
                                pe.wait_ge(y_ok, Y - 3)
                            x = lambda rows, k: xs[rows, N % 2, k, :]
                            tt = lambda rows, k: t.tt[rows, GB * (n - 1) + k, :]
                            times(4 + Y % 4, *((tt, x) if u else (x, tt))).then_inc(y_ps, 1)

        @block.gpsimd
        def _(g):
            g.memset(t16[:, :, :, :], 0.0).then_inc(unit_ok, 1)
            g.wait_ge(unit_ok, 1)
            for i in range(BASE):
                g.memset(t16[:, i, :, i:i + 1], 1.0).then_inc(unit_ok, 1)

        @block.scalar
        def _(a):
            for k in range(4):
                a.wait_ge(sel_ps, k + 1)
                a.activation(a16[:, 4 * k:4 * k + 4, :, :].rearrange("g i b j -> g (i b j)"), ps[0:SYS, k, :],
                             ACT.Copy).then_inc(a16_ok, 1)
            a.wait_ge(sub, SUBS)
            a.activation(c16[:, :, :, :].rearrange("g j b i -> g i b j"), t16[:, :, :, :], ACT.Copy).then_inc(c16_ok, 1)

        @block.vector
        def _(v):
            n = [0]

            def link(ins):
                n[0] += 1
                ins.then_inc(sub, 1)
                v.wait_ge(sub, n[0])

            v.wait_ge(unit_ok, 1 + BASE)
            v.wait_ge(a16_ok, 4)
            for j in range(BASE - 1):
                r, w = BASE - 1 - j, j + 1
                o = tmp[:, 0:r * NBLK * w].rearrange("g (i b c) -> g i b c", i=r, b=NBLK)
                sh = [SYS, r, NBLK, w]
                link(v.tensor_tensor(o, bc(a16[:, j + 1:, :, j:j + 1], *sh), bc(t16[:, j:j + 1, :, 0:w], *sh), ALU.mult))
                link(v.tensor_tensor(t16[:, j + 1:, :, 0:w], t16[:, j + 1:, :, 0:w], o, ALU.subtract))
            for which, dst in ((0, t.tt), (1, tn)):
                for k in range(2):
                    v.wait_ge(back_ps, 2 * which + k + 1)
                    sh = [128, SYS, 4, 8]
                    v.tensor_tensor(
                        dst[:, :, :].rearrange("p g (b i) -> p g b i", b=4)[:, :, :, 8 * k:8 * k + 8],
                        bc(ps[:, 4 + 2 * which + k, 0:8 * SYS].rearrange("p (i g) -> p g i", i=8).unsqueeze(2), *sh),
                        bc(t.blk[:, :].unsqueeze(1).unsqueeze(3), *sh), ALU.mult).then_inc(tt_ok, 1)
            v.wait_ge(tt_ok, 4)
            for step in range(2):
                low = t.low32 if step else t.low16
                for n in range(JOBS + 1):
                    if n < JOBS:
                        N = step * JOBS + n
                        v.wait_ge(x_ps, N + 1)
                        if step:
                            v.wait_ge(y_ps, 2 * (n + 1))
                        v.tensor_tensor(xs[:, N % 2, :, :], ps[:, N % 4, :].rearrange("p (g i) -> p g i", g=GB),
                                        bc(low[:, :].unsqueeze(1), 128, GB, CK), ALU.mult).then_inc(x_ok, 1)
                    if n >= 1:
                        gs = slice(GB * (n - 1), GB * n)
                        for u in range(2 - step):
                            Y = 2 * (n - 1) + u if not step else 2 * JOBS + n - 1
                            v.wait_ge(y_ps, (2 * n if not step else Y + 1))
                            d = (t.tt, tn)[u]
                            v.tensor_tensor(d[:, gs, :], d[:, gs, :], ps[:, 4 + Y % 4, :].rearrange("p (g i) -> p g i", g=GB),
                                            ALU.subtract).then_inc(y_ok, 1)
    p.close()


def scan_chunks(nc, t, half):
    p = Phase(nc, f"_{half}")
    vt = p.sb("v_tile", [128, 2, NH, DV])
    gt = p.sb("gate_tile", [128, VD])
    ot = p.sb("o_tile", [128, NH, DV])
    osq = p.sb("o_sq", [128, NP, DV])
    oT = p.sb("o_T", [128, NH, 128])
    ov = p.sb("o_var", [128, NH])
    yt = p.sb("y_tile", [128, HID])
    ks = [p.ps(f"ks{b}", [128, 512]) for b in range(4)]
    us = [p.ps(f"us{b}", [128, 512]) for b in range(2)]
    fl = [p.ps(f"fl{b}", [128, 512]) for b in range(2)]
    names = ("ks_ps", "r_done", "u_ps", "u_done", "o_ps", "o_done", "su_ps", "S_done",
             "v_ps", "v_done", "g_ps", "g_done", "osq_done", "sum_done", "var_done", "rstd_done", "og_done",
             "oT_ps", "oT_done", "y_ps2", "y_done", "vch3", "on_ready", "qs_ps")
    (ks_ps, r_done, u_ps, u_done, o_ps, o_done, su_ps, S_done, v_ps, v_done, g_ps, g_done, osq_done,
     sum_done, var_done, rstd_done, og_done, oT_ps, oT_done, y_ps, y_done, vch, on_ready, qs_ps) = (p.sem(n) for n in names)

    def heads(ph, r):
        return [2 * (3 * ph + k) + r for k in range(G3)]

    order = [("v", 0, b) for b in range(3)]

    def fillers(c):
        v = [("v", c + 1, b) for b in range(3)] if c + 1 < HALF else [None] * 3
        tr = [("t", c - 1, b) for b in range(3)] if c else []
        y = [("y", c - 1, 0)] if c else []
        g = [("g", c, b) for b in range(3)]
        return [[j for j in lot if j] for lot in ([v[0]], [v[1]], tr, y + [v[2]], g[0:2], g[2:3])]

    for c in range(HALF):
        order += [j for lot in fillers(c) for j in lot]
    order += [("t", HALF - 1, b) for b in range(3)] + [("y", HALF - 1, 0)]
    place = {job: n for n, job in enumerate(order)}
    done_of = {"v": v_done, "g": g_done, "t": oT_done, "y": y_done}

    def index(job):
        kind, c, b = job
        return c * (1 if kind == "y" else 3) + b

    def bank_of(job):
        return fl[place[job] % 2]

    with nc.Block() as block:
        @block.tensor
        def _(pe):
            def filler(job):
                kind, c, b = job
                if place[job] >= 2:
                    old = order[place[job] - 2]
                    pe.wait_ge(done_of[old[0]], index(old) + 1)
                o = bank_of(job)
                if kind == "v":
                    for j in range(TAPS):
                        m = pe.matmul(o[:, :], t.hS[:, j, half * HALF + c, :],
                                      t.wc[:, j, 2 * KD + b * 512:2 * KD + (b + 1) * 512], start=j == 0, stop=j == TAPS - 1)
                    m.then_inc(v_ps, 1)
                elif kind == "g":
                    pe.matmul(o[:, :], t.hS[:, TAPS - 1, half * HALF + c, :], t.wg[:, b * 512:(b + 1) * 512],
                              start=True, stop=True).then_inc(g_ps, 1)
                elif kind == "t":
                    pe.wait_ge(og_done, c + 1)
                    for k in range(4):
                        m = pe.transpose(o[:, k * 128:(k + 1) * 128], ot[:, 4 * b + k, :], t.ident[:, :])
                    m.then_inc(oT_ps, 1)
                else:
                    pe.wait_ge(oT_done, 3 * (c + 1))
                    for h in range(NH):
                        m = pe.matmul(o[:, 0:HID], oT[:, h, :], t.wo[:, h, :], start=h == 0, stop=h == NH - 1)
                    m.then_inc(y_ps, 1)

            def state_products(c, ph):
                n = 2 * c + ph
                if c:
                    pe.wait_ge(S_done, 2 * (c - 1) + ph + 1)
                    pe.wait_ge(o_done, 4 * (c - 1) + 2 * ph + 2)
                for r in range(2):
                    rows = slice(r * 64, (r + 1) * 64)
                    for k in range(G3):
                        for s in range(2):
                            cs = slice(s * CK, (s + 1) * CK)
                            m = pe.matmul(ks[2 * ph + r][cs, k * DV:(k + 1) * DV], t.kqT[rows, c, 3 * ph + k, 0, cs],
                                          t.S[rows, s, 3 * ph + k, :], start=True, stop=True)
                    m.then_inc(ks_ps, 1)

            def solve(c, ph):
                n = 2 * c + ph
                if ph:
                    pe.wait_ge(u_done, 4 * c + 2)
                elif c:
                    pe.wait_ge(S_done, 2 * c)
                for r in range(2):
                    pe.wait_ge(r_done, 2 * n + r + 1)
                    for k, h in enumerate(heads(ph, r)):
                        for s in range(2):
                            cs = slice(s * CK, (s + 1) * CK)
                            m = pe.matmul(us[r][cs, k * DV:(k + 1) * DV], t.tt[cs, c * NH + h, :], vt[cs, c % 2, h, :],
                                          start=True, stop=True)
                    m.then_inc(u_ps, 1)

            def outputs(c, ph):
                for r in range(2):
                    rows = slice(r * 64, (r + 1) * 64)
                    pe.wait_ge(u_done, 4 * c + 2 * ph + r + 1)
                    for k, h in enumerate(heads(ph, r)):
                        for s in range(2):
                            cs = slice(s * CK, (s + 1) * CK)
                            m = pe.matmul(ks[2 * ph + r][cs, k * DV:(k + 1) * DV], t.kqT[rows, c, 3 * ph + k, 1, cs],
                                          t.S[rows, s, 3 * ph + k, :], start=k == 0, stop=False, skip_group_check=True)
                    m.then_inc(qs_ps, 1)
                    for s in (r, 1 - r):
                        if s != r:
                            pe.wait_ge(qs_ps, 4 * c + 2 * ph + r + 1)
                        cs = slice(s * CK, (s + 1) * CK)
                        for k, h in enumerate(heads(ph, r)):
                            m = pe.matmul(ks[2 * ph + r][cs, k * DV:(k + 1) * DV], t.ap[cs, c, h, 1, :], vt[cs, c % 2, h, :],
                                          start=False, stop=k == G3 - 1, skip_group_check=True)
                    m.then_inc(o_ps, 1)

            def updates(c, ph):
                pe.wait_ge(u_done, 4 * c + 4)
                if ph:
                    pe.wait_ge(S_done, 2 * c + 1)
                for s in range(2):
                    cs = slice(s * CK, (s + 1) * CK)
                    for k in range(G3):
                        for r in range(2):
                            h = 2 * (3 * ph + k) + r
                            m = pe.matmul(us[s][r * 64:(r + 1) * 64, k * DV:(k + 1) * DV], t.kd[cs, c, h * DK:(h + 1) * DK],
                                          vt[cs, c % 2, h, :], start=True, stop=True)
                m.then_inc(su_ps, 1)

            for b in range(3):
                filler(("v", 0, b))
            for c in range(HALF):
                cut = fillers(c)
                state_products(c, 0)
                state_products(c, 1)
                for j in cut[0]:
                    filler(j)
                solve(c, 0)
                for j in cut[1]:
                    filler(j)
                solve(c, 1)
                for j in cut[2]:
                    filler(j)
                outputs(c, 0)
                updates(c, 0)
                for j in cut[3]:
                    filler(j)
                outputs(c, 1)
                updates(c, 1)
                for j in cut[4] + cut[5]:
                    filler(j)
            for b in range(3):
                filler(("t", HALF - 1, b))
            filler(("y", HALF - 1, 0))

        @block.scalar
        def _(a):
            def copy_filler(job):
                kind, c, b = job
                if kind == "v":
                    if c >= 2 and b == 0:
                        a.wait_ge(su_ps, 2 * (c - 1))
                    a.wait_ge(v_ps, 3 * c + b + 1)
                    a.activation(vt[:, c % 2, 4 * b:4 * b + 4, :].rearrange("p h d -> p (h d)"), bank_of(job)[:, :],
                                 ACT.Silu).then_inc(v_done, 1)
                elif kind == "g":
                    if c and b == 0:
                        a.wait_ge(og_done, c)
                    a.wait_ge(g_ps, 3 * c + b + 1)
                    a.activation(gt[:, b * 512:(b + 1) * 512], bank_of(job)[:, :], ACT.Silu).then_inc(g_done, 1)
                elif kind == "t":
                    if c and b == 0:
                        a.wait_ge(y_ps, c)
                    a.wait_ge(oT_ps, 3 * c + b + 1)
                    a.activation(oT[:, 4 * b:4 * b + 4, :].rearrange("p h d -> p (h d)"), bank_of(job)[:, :],
                                 ACT.Copy).then_inc(oT_done, 1)

            def copy_u(c, ph):
                for r in range(2):
                    a.wait_ge(u_ps, 4 * c + 2 * ph + r + 1)
                    a.activation(vt[:, c % 2, 6 * ph + r:6 * ph + r + 5:2, :], us[r][:, 0:G3 * DV].rearrange("p (h d) -> p h d", h=G3),
                                 ACT.Copy).then_inc(u_done, 1)

            def copy_o(c, ph):
                if c and ph == 0:
                    a.wait_ge(oT_ps, 3 * c)
                for r in range(2):
                    a.wait_ge(o_ps, 4 * c + 2 * ph + r + 1)
                    a.activation(ot[:, 6 * ph + r:6 * ph + r + 5:2, :],
                                 ks[2 * ph + r][:, 0:G3 * DV].rearrange("p (h d) -> p h d", h=G3), ACT.Copy).then_inc(o_done, 1)

            for b in range(3):
                copy_filler(("v", 0, b))
            for c in range(HALF):
                cut = fillers(c)
                for j in cut[0]:
                    copy_filler(j)
                copy_u(c, 0)
                for j in cut[1]:
                    copy_filler(j)
                copy_u(c, 1)
                for j in cut[2]:
                    copy_filler(j)
                copy_o(c, 0)
                for j in cut[3]:
                    copy_filler(j)
                copy_o(c, 1)
                for j in cut[4] + cut[5]:
                    copy_filler(j)
            for b in range(3):
                copy_filler(("t", HALF - 1, b))

        @block.gpsimd
        def _(g):
            for c in range(HALF):
                for ph in range(2):
                    g.wait_ge(o_done, 4 * c + 2 * ph + 2)
                    if c + ph:
                        g.wait_ge(sum_done, 2 * c + ph)
                    hs = slice(6 * ph, 6 * ph + 6)
                    g.tensor_tensor(osq[:, :, :], ot[:, hs, :], ot[:, hs, :], ALU.mult).then_inc(osq_done, 1)
                g.wait_ge(var_done, c + 1)
                g.tensor_tensor(ov[:, :], ov[:, :], t.mhalf[:, 0:NH], ALU.pow).then_inc(rstd_done, 1)
                g.wait_ge(rstd_done, c + 1)
                g.tensor_tensor(ot[:, :, :], ot[:, :, :], bc(ov[:, :].unsqueeze(2), 128, NH, DV), ALU.mult).then_inc(on_ready, 1)

        @block.vector
        def _(v):
            link = linker(v, vch)

            def residuals(c, ph):
                v.wait_ge(v_done, 3 * (c + 1))
                for r in range(2):
                    v.wait_ge(ks_ps, 4 * c + 2 * ph + r + 1)
                    for k, h in enumerate(heads(ph, r)):
                        m = v.scalar_tensor_tensor(out=vt[:, c % 2, h, :], in0=ks[2 * ph + r][:, k * DV:(k + 1) * DV],
                                                   scalar=t.nGam[:, half * HALF + c, h:h + 1], in1=vt[:, c % 2, h, :],
                                                   op0=ALU.mult, op1=ALU.add)
                    m.then_inc(r_done, 1)

            def new_state(c, ph):
                v.wait_ge(o_ps, 4 * c + 2 * ph + 2)
                v.wait_ge(su_ps, 2 * c + ph + 1)
                for s in range(2):
                    for k in range(G3):
                        q = 3 * ph + k
                        m = v.scalar_tensor_tensor(out=t.S[:, s, q, :], in0=t.S[:, s, q, :],
                                                   scalar=t.gam_all[:, half * HALF + c, s, q:q + 1],
                                                   in1=us[s][:, k * DV:(k + 1) * DV], op0=ALU.mult, op1=ALU.add)
                m.then_inc(S_done, 1)

            def variances(c):
                if c:
                    v.wait_ge(on_ready, c)
                for ph in range(2):
                    v.wait_ge(osq_done, 2 * c + ph + 1)
                    v.tensor_reduce(ov[:, 6 * ph:6 * ph + 6], osq[:, :, :], AX, ALU.add).then_inc(sum_done, 1)
                v.wait_ge(sum_done, 2 * c + 2)
                v.tensor_scalar(ov[:, :], ov[:, :], 1.0 / DV, 1e-5, ALU.mult, ALU.add).then_inc(var_done, 1)

            def gate(c):
                v.wait_ge(on_ready, c + 1)
                v.wait_ge(g_done, 3 * (c + 1))
                v.tensor_tensor(ot[:, :, :].rearrange("p h d -> p (h d)"), ot[:, :, :].rearrange("p h d -> p (h d)"),
                                gt[:, :], ALU.mult).then_inc(og_done, 1)

            def project(c):
                v.wait_ge(y_ps, c + 1)
                link(v.tensor_tensor(yt[:, :], bank_of(("y", c, 0))[:, 0:HID], t.modbc[:, 2 * HID:3 * HID], ALU.mult))
                v.tensor_tensor(t.x[:, half * HALF + c, :], t.x[:, half * HALF + c, :], yt[:, :], ALU.add).then_inc(y_done, 1)

            for c in range(HALF):
                residuals(c, 0)
                residuals(c, 1)
                new_state(c, 0)
                new_state(c, 1)
                if c:
                    project(c - 1)
                variances(c)
                gate(c)
            project(HALF - 1)
    p.close()


def second_norm(nc, t):
    p = Phase(nc)
    sq, st = p.sb("sq_b", [128, TILES, HID]), p.sb("st_b", [128, 3, TILES])
    hn = p.sb("h_rms", [128, TILES, HID])
    ps = p.ps("ps_b1", [128, 2, 512])
    vch, pow_in, pow_out, hn_ok, hT_ps, hT_ok = (p.sem(n) for n in ("vch_b", "pow_in_b", "pow_out_b", "hn_ok", "h1T_ps", "h1T_ok"))
    with nc.Block() as block:
        @block.gpsimd
        def _(g):
            for k in range(2):
                g.wait_ge(pow_in, k + 1)
                g.tensor_tensor(st[:, 1 + k, :], st[:, 1 + k, :], t.mhalf[:, 0:TILES], ALU.pow).then_inc(pow_out, 1)

        @block.vector
        def _(v):
            link = linker(v, vch)
            sh = [128, TILES, HID]
            h = t.hf
            link(v.tensor_reduce(st[:, 0, :], t.x[:, :, :], AX, ALU.add))
            link(v.tensor_scalar(st[:, 0, :], st[:, 0, :], 1.0 / HID, None, ALU.mult))
            link(v.tensor_tensor(h[:, :, :], t.x[:, :, :], bc(st[:, 0, :].unsqueeze(2), *sh), ALU.subtract))
            link(v.tensor_tensor(sq[:, :, :], h[:, :, :], h[:, :, :], ALU.mult))
            link(v.tensor_reduce(st[:, 1, :], sq[:, :, :], AX, ALU.add))
            v.tensor_scalar(st[:, 1, :], st[:, 1, :], 1.0 / HID, 1e-5, ALU.mult, ALU.add).then_inc(pow_in, 1)
            v.wait_ge(pow_out, 1)
            link(v.tensor_tensor(h[:, :, :], h[:, :, :], bc(st[:, 1, :].unsqueeze(2), *sh), ALU.mult))
            link(v.tensor_tensor(h[:, :, :], h[:, :, :], bc(t.modbc[:, 4 * HID:5 * HID].unsqueeze(1), *sh), ALU.mult))
            link(v.tensor_tensor(h[:, :, :], h[:, :, :], bc(t.modbc[:, 3 * HID:4 * HID].unsqueeze(1), *sh), ALU.add))
            link(v.tensor_tensor(sq[:, :, :], h[:, :, :], h[:, :, :], ALU.mult))
            link(v.tensor_reduce(st[:, 2, :], sq[:, :, :], AX, ALU.add))
            v.tensor_scalar(st[:, 2, :], st[:, 2, :], 1.0 / HID, 1e-6, ALU.mult, ALU.add).then_inc(pow_in, 1)
            v.wait_ge(pow_out, 2)
            v.tensor_tensor(hn[:, :, :], h[:, :, :], bc(st[:, 2, :].unsqueeze(2), *sh), ALU.mult).then_inc(hn_ok, 1)

        @block.tensor
        def _(pe):
            pe.wait_ge(hn_ok, 1)
            for c in range(TILES):
                m = pe.transpose(ps[:, c // 4, (c % 4) * 128:(c % 4 + 1) * 128], hn[:, c, :], t.ident[:, :])
                if c % 4 == 3:
                    m.then_inc(hT_ps, 1)

        @block.scalar
        def _(a):
            for b in range(2):
                a.wait_ge(hT_ps, b + 1)
                a.activation(t.h1T[:, :, 256 * b:256 * (b + 1)].rearrange("p s (c t) -> p c s t", c=4),
                             ps[:, b, :].rearrange("p (c s t) -> p c s t", c=4, s=2), ACT.Copy,
                             scale=t.n1w[:, 0:1]).then_inc(hT_ok, 1)
    p.close()


def attention_scores(nc, t, s):
    p = Phase(nc, f"_{s}")
    qk = p.sb("qk_f32", [128, 2, 2, 128])
    re = p.sb("qk_rest", [128, 2, 128])
    part = p.sb("qk_parts", [128, 3, 2, 128], BF16)
    qs = p.sb("q_slots", [128, TQ, AH, SLOT], BF16)
    kx = p.sb("k_slots", [128, AH, SLOT], BF16)
    mx = p.sb("row_max", [128, TQ, AH])
    mr = p.sb("max_rest", [128, TQ, AH])
    pr = [p.ps(f"qkv_ps{b}", [128, 512]) for b in range(2)]
    sc = [p.ps(f"sc_ps{b}", [128, 2, 512]) for b in range(2)]
    tb = [p.ps(f"tr_ps{b}", [128, 8, 128], BF16) for b in range(2)]
    (vch, init, qkv_ps, qkv_ok, parts_ok, slots_ok, tr_ps, tr_ok, sc_ps, max_ok, neg_ok, pinit) = (p.sem(n) for n in (
        "vch_s", "slots_init", "qkv_ps", "qkv_ok", "parts_ok", "slots_ok", "tr_ps", "tr_ok", "sc_ps", "max_ok", "neg_ok",
        "pool_init"))
    QSL = ((0, 0), (8, 0), (16, 1), (24, 0), (40, 2), (48, 1))
    KSL = ((0, 0), (8, 1), (16, 0), (24, 2), (40, 0), (48, 1))
    with nc.Block() as block:
        @block.gpsimd
        def _(g):
            g.memset(qs[:, :, :, :], 0.0).then_inc(init, 1)
            g.memset(kx[:, :, :], 0.0).then_inc(pinit, 1)
            g.wait_ge(pinit, 1)
            g.memset(kx[:, :, 32:35], 1.0).then_inc(init, 1)
            g.memset(t.va[:, :, :, :], 1.0).then_inc(init, 1)
            g.wait_ge(init, 3)
            for q in range(TQ):
                g.wait_ge(parts_ok, q + 1)
                if q:
                    g.wait_ge(tr_ps, 2 * q)
                for dst, which, slots in ((qs[:, q, :, :], 0, QSL), (kx[:, :, :], 1, KSL)):
                    for at, m in slots:
                        g.tensor_copy(dst[:, :, at:at + AD],
                                      part[:, m, which, :].rearrange("p (h d) -> p h d", d=AD)).then_inc(slots_ok, 1)

        @block.scalar
        def _(a):
            a.wait_ge(init, 3)
            for q in range(TQ):
                a.wait_ge(qkv_ps, q + 1)
                if q >= 2:
                    a.wait_ge(parts_ok, q - 1)
                a.activation(qk[:, q % 2, 0, :], pr[q % 2][:, 0:128], ACT.Copy, scale=AD ** -0.5).then_inc(qkv_ok, 1)
                a.activation(qk[:, q % 2, 1, :], pr[q % 2][:, 128:256], ACT.Copy).then_inc(qkv_ok, 1)
                a.activation(t.va[:, q, :, 0:AD], pr[q % 2][:, 256:384].rearrange("p (h d) -> p h d", d=AD),
                             ACT.Copy).then_inc(qkv_ok, 1)
                for k in range(2):
                    a.wait_ge(tr_ps, 2 * q + k + 1)
                    a.activation((t.qT, t.kT)[k][:, :, q * 128:(q + 1) * 128], tb[k][:, :, :], ACT.Copy).then_inc(tr_ok, 1)
            for q in range(TQ):
                a.wait_ge(tr_ps, 2 * TQ + q + 1)
                a.activation(t.qT[:, :, q * 128:(q + 1) * 128], tb[q % 2][:, :, :], ACT.Copy).then_inc(tr_ok, 1)

        @block.tensor
        def _(pe):
            def project(q):
                if q >= 2:
                    pe.wait_ge(qkv_ok, 3 * (q - 1))
                pe.matmul(pr[q % 2][:, 0:384], t.h1T[:, s, q * 128:(q + 1) * 128], t.wqkv[:, :],
                          start=True, stop=True).then_inc(qkv_ps, 1)

            project(0)
            for q in range(TQ):
                if q + 1 < TQ:
                    project(q + 1)
                pe.wait_ge(slots_ok, 12 * (q + 1))
                if q:
                    pe.wait_ge(tr_ok, 2 * q)
                for k, w in ((0, qs[:, q, :, :]), (1, kx[:, :, :])):
                    wv = w.rearrange("p h z -> p (h z)")
                    for b in range(8):
                        m = pe.transpose(tb[k][:, b, :], wv[:, b * 128:(b + 1) * 128], t.identb[:, :])
                    m.then_inc(tr_ps, 1)
            pe.wait_ge(tr_ok, 2 * TQ)
            n = 0
            for q in range(TQ):
                for b in range(8):
                    if n >= 2:
                        pe.wait_ge(max_ok, n - 1)
                    for r in range(2):
                        rows = slice(64 * r, 64 * r + 64)
                        m = pe.matmul(sc[n % 2][:, r, :], t.qT[rows, b, q * 128:(q + 1) * 128], t.kT[rows, b, :],
                                      start=True, stop=True)
                    m.then_inc(sc_ps, 1)
                    n += 1
            for q in range(TQ):
                pe.wait_ge(neg_ok, 3)
                if q >= 2:
                    pe.wait_ge(tr_ok, 2 * TQ + q - 1)
                wv = qs[:, q, :, :].rearrange("p h z -> p (h z)")
                for b in range(8):
                    m = pe.transpose(tb[q % 2][:, b, :], wv[:, b * 128:(b + 1) * 128], t.identb[:, :])
                m.then_inc(tr_ps, 1)

        @block.vector
        def _(v):
            link = linker(v, vch)

            def split(out, rest, x):
                link(v.tensor_copy(out(0), x))
                link(v.tensor_tensor(rest, x, out(0), ALU.subtract))
                link(v.tensor_copy(out(1), rest))
                link(v.tensor_tensor(rest, rest, out(1), ALU.subtract))
                return v.tensor_copy(out(2), rest)

            for q in range(TQ):
                v.wait_ge(qkv_ok, 3 * q + 2)
                if q:
                    v.wait_ge(slots_ok, 12 * q)
                split(lambda m: part[:, m, :, :], re[:, :, :], qk[:, q % 2, :, :]).then_inc(parts_ok, 1)
            n = 0
            for q in range(TQ):
                for b in range(8):
                    v.wait_ge(sc_ps, n + 1)
                    v.tensor_reduce(mx[:, q, 2 * b:2 * b + 2], sc[n % 2][:, :, :], AX, ALU.max).then_inc(max_ok, 1)
                    n += 1
            v.wait_ge(max_ok, 8 * TQ)
            link(v.tensor_scalar(mx[:, :, :], mx[:, :, :], -1.0, None, ALU.mult))
            v.tensor_copy(qs[:, :, :, 32], mx[:, :, :]).then_inc(neg_ok, 1)
            v.wait_ge(neg_ok, 1)
            link(v.tensor_tensor(mr[:, :, :], mx[:, :, :], qs[:, :, :, 32], ALU.subtract))
            v.tensor_copy(qs[:, :, :, 33], mr[:, :, :]).then_inc(neg_ok, 1)
            v.wait_ge(neg_ok, 2)
            link(v.tensor_tensor(mr[:, :, :], mr[:, :, :], qs[:, :, :, 33], ALU.subtract))
            v.tensor_copy(qs[:, :, :, 34], mr[:, :, :]).then_inc(neg_ok, 1)
    p.close()


def attention_values(nc, t, s):
    p = Phase(nc, f"_{s}")
    pt = p.sb("probs", [128, 2, 4, TQ, 512])
    sc = [p.ps(f"sT_ps{b}", [128, 2, 512]) for b in range(3)]
    cx = [p.ps(f"ctx_ps{b}", [128, 512]) for b in range(2)]
    sc_ps, exp_ok, cx_ps, cx_ok = (p.sem(n) for n in ("sT_ps", "exp_ok", "ctx_ps", "ctx_ok"))
    GROUPS = AH // 4
    with nc.Block() as block:
        @block.tensor
        def _(pe):
            def scores(g):
                for j in range(4):
                    h = 4 * g + j
                    rows = slice(64 * (h % 2), 64 * (h % 2) + 64)
                    for u in range(2):
                        n = 8 * g + 2 * j + u
                        if n >= 3:
                            pe.wait_ge(exp_ok, n - 2)
                        for k in range(2):
                            tb = 2 * u + k
                            m = pe.matmul(sc[n % 3][:, k, :], t.kT[rows, h // 2, tb * 128:(tb + 1) * 128],
                                          t.qT[rows, h // 2, :], start=True, stop=True)
                        m.then_inc(sc_ps, 1)

            def values(g):
                pe.wait_ge(exp_ok, 8 * (g + 1))
                if g >= 2:
                    pe.wait_ge(cx_ok, g - 1)
                for tb in range(TQ):
                    for j in range(4):
                        m = pe.matmul(cx[g % 2][32 * j:32 * j + 32, :], t.va[:, tb, 4 * g + j, :], pt[:, g % 2, j, tb, :],
                                      start=tb == 0, stop=tb == TQ - 1)
                m.then_inc(cx_ps, 1)

            scores(0)
            for g in range(GROUPS):
                if g + 1 < GROUPS:
                    scores(g + 1)
                values(g)

        @block.scalar
        def _(a):
            for g in range(GROUPS):
                if g >= 2:
                    a.wait_ge(cx_ps, g - 1)
                for j in range(4):
                    for u in range(2):
                        n = 8 * g + 2 * j + u
                        a.wait_ge(sc_ps, n + 1)
                        a.activation(pt[:, g % 2, j, 2 * u:2 * u + 2, :], sc[n % 3][:, :, :], ACT.Exp).then_inc(exp_ok, 1)

        @block.vector
        def _(v):
            for g in range(GROUPS):
                v.wait_ge(cx_ps, g + 1)
                v.tensor_copy(t.cx[:, g, :, s, :], cx[g % 2][:, :].rearrange("p (c t) -> p c t", t=CK)).then_inc(cx_ok, 1)
    p.close()


def attention_output(nc, t, src):
    p = Phase(nc)
    rc = p.sb("rec_sum", [128, TILES, AH])
    cn = p.sb("ctx_n", [128, TILES, AH, AD])
    cT = p.sb("ctx_nT", [128, TILES, 128])
    sq, st, hn = p.sb("sq_c", [128, TILES, HID]), p.sb("st_c", [128, TILES]), p.sb("h2_rms", [128, TILES, HID])
    lg, eq, oh1, oh2 = (p.sb(n, [128, TILES, NE]) for n in ("logits", "eq", "first", "second"))
    sm = p.sb("route_st", [128, 6, TILES])
    ps = p.ps("ps_c", [128, 8, 512])
    (vch, cx_ps, cn_ok, cT_ps, cT_ok, y_ps, pow_in, pow_out, hn_ok, h2_ps, h2_ok, lg_ps, ex_in, ex_ok) = (p.sem(n) for n in (
        "vch_c", "cxT_ps", "cn_ok", "cT_ps_c", "cT_ok", "y_ps_c", "pow_in_c", "pow_out_c", "hn_ok_c", "h2T_ps", "h2T_ok",
        "lg_ps", "ex_in", "ex_ok"))
    wl = p.sem("moe_weights")
    with nc.Block() as block:
        @block.sync
        def _(sp):
            for m, (one, many) in enumerate((("L0_ffn_sh_gate", "L0_ffn_e_gate"), ("L0_ffn_sh_up", "L0_ffn_e_up"))):
                sp.dma_start(t.wgu[:, NE, m, :], src[one]).then_inc(wl, 16)
                sp.dma_start(t.wgu[:, 0:NE, m, :], src[many].rearrange("e d f -> d e f")).then_inc(wl, 16)
            sp.dma_start(t.wdn[:, NE, :, :], src["L0_ffn_sh_down"].rearrange("(b f) d -> f b d", b=2)).then_inc(wl, 16)
            for b in range(2):
                sp.dma_start(t.wdn[:, 0:NE, b, :], src["L0_ffn_e_down"][:, 128 * b:128 * (b + 1), :]
                             .rearrange("e f d -> f e d")).then_inc(wl, 16)
            sp.wait_ge(wl, 16 * 7)

        @block.tensor
        def _(pe):
            for c in range(TILES):
                if c >= 4:
                    pe.wait_ge(cn_ok, c - 3)
                for g in range(4):
                    m = pe.transpose(ps[:, c % 4, g * 128:(g + 1) * 128], t.cx[:, g, c, :, :].rearrange("p s t -> p (s t)"), t.ident[:, :])
                m.then_inc(cx_ps, 1)
            for c in range(TILES):
                pe.wait_ge(cn_ok, c + 1)
                m = pe.transpose(ps[:, 4 + c // 4, (c % 4) * 128:(c % 4 + 1) * 128],
                                 cn[:, c, :, :].rearrange("p h d -> p (h d)"), t.ident[:, :])
                if c % 4 == 3:
                    m.then_inc(cT_ps, 1)
            pe.wait_ge(cT_ok, 2)
            for c in range(TILES):
                m = pe.matmul(ps[:, 6 + c // 4, (c % 4) * 128:(c % 4 + 1) * 128], cT[:, c, :], t.wo2[:, :],
                              start=True, stop=True)
                if c % 4 == 3:
                    m.then_inc(y_ps, 1)
            pe.wait_ge(hn_ok, 1)
            for c in range(TILES):
                m = pe.transpose(ps[:, c // 4, (c % 4) * 128:(c % 4 + 1) * 128], hn[:, c, :], t.ident[:, :])
                if c % 4 == 3:
                    m.then_inc(h2_ps, 1)
            pe.wait_ge(h2_ok, 2)
            for c in range(TILES):
                m = pe.matmul(ps[:, 2, c * NE:(c + 1) * NE], t.h2T[:, c * 128:(c + 1) * 128], t.wr[:, :],
                              start=True, stop=True)
            m.then_inc(lg_ps, 1)

        @block.scalar
        def _(a):
            for b in range(2):
                a.wait_ge(cT_ps, b + 1)
                a.activation(cT[:, 4 * b:4 * b + 4, :].rearrange("p c i -> p (c i)"), ps[:, 4 + b, :], ACT.Copy).then_inc(cT_ok, 1)
            for b in range(2):
                a.wait_ge(h2_ps, b + 1)
                a.activation(t.h2T[:, 512 * b:512 * (b + 1)], ps[:, b, :], ACT.Copy, scale=t.n2w[:, 0:1]).then_inc(h2_ok, 1)
            for k, x in ((0, lg[:, :, :]), (1, sm[:, 3, :])):
                a.wait_ge(ex_in, k + 1)
                a.activation(x, x, ACT.Exp).then_inc(ex_ok, 1)

        @block.gpsimd
        def _(g):
            g.wait_ge(pow_in, 1)
            g.tensor_tensor(st[:, :], st[:, :], t.mhalf[:, 0:TILES], ALU.pow).then_inc(pow_out, 1)

        @block.vector
        def _(v):
            link = linker(v, vch)
            for c in range(TILES):
                v.wait_ge(cx_ps, c + 1)
                z = ps[:, c % 4, :].rearrange("p (h z) -> p h z", h=AH)
                link(v.reciprocal(rc[:, c, :], z[:, :, AD]))
                v.tensor_tensor(cn[:, c, :, :], z[:, :, 0:AD], bc(rc[:, c, :].unsqueeze(2), 128, AH, AD),
                                ALU.mult).then_inc(cn_ok, 1)
            for b in range(2):
                v.wait_ge(y_ps, b + 1)
                h = t.hf[:, 4 * b:4 * b + 4, :].rearrange("p c d -> p (c d)")
                link(v.tensor_tensor(h, h, ps[:, 6 + b, :], ALU.add))
            sh = [128, TILES, HID]
            link(v.tensor_tensor(sq[:, :, :], t.hf[:, :, :], t.hf[:, :, :], ALU.mult))
            link(v.tensor_reduce(st[:, :], sq[:, :, :], AX, ALU.add))
            v.tensor_scalar(st[:, :], st[:, :], 1.0 / HID, 1e-6, ALU.mult, ALU.add).then_inc(pow_in, 1)
            v.wait_ge(pow_out, 1)
            v.tensor_tensor(hn[:, :, :], t.hf[:, :, :], bc(st[:, :].unsqueeze(2), *sh), ALU.mult).then_inc(hn_ok, 1)
            se = [128, TILES, NE]
            up = lambda x: bc(x.unsqueeze(2), *se)
            v.wait_ge(lg_ps, 1)
            link(v.tensor_copy(lg[:, :, :], ps[:, 2, 0:TILES * NE].rearrange("p (c e) -> p c e", e=NE)))
            link(v.tensor_reduce(sm[:, 0, :], lg[:, :, :], AX, ALU.max))
            v.tensor_tensor(lg[:, :, :], lg[:, :, :], up(sm[:, 0, :]), ALU.subtract).then_inc(ex_in, 1)
            v.wait_ge(ex_ok, 1)
            link(v.tensor_reduce(sm[:, 1, :], lg[:, :, :], AX, ALU.add))
            link(v.reciprocal(sm[:, 1, :], sm[:, 1, :]))
            link(v.tensor_tensor(lg[:, :, :], lg[:, :, :], up(sm[:, 1, :]), ALU.mult))
            for k, oh in enumerate((oh1, oh2)):
                link(v.tensor_reduce(sm[:, 2 + k, :], lg[:, :, :], AX, ALU.max))
                link(v.tensor_tensor(eq[:, :, :], lg[:, :, :], up(sm[:, 2 + k, :]), ALU.is_equal))
                link(v.tensor_tensor(eq[:, :, :], eq[:, :, :], bc(t.rank[:, :].unsqueeze(1), *se), ALU.mult))
                link(v.tensor_reduce(sm[:, 4, :], eq[:, :, :], AX, ALU.max))
                link(v.tensor_tensor(oh[:, :, :], eq[:, :, :], up(sm[:, 4, :]), ALU.is_equal))
                if k == 0:
                    link(v.scalar_tensor_tensor(out=lg[:, :, :], in0=oh[:, :, :], scalar=-2.0, in1=lg[:, :, :],
                                                op0=ALU.mult, op1=ALU.add))
            v.tensor_tensor(sm[:, 3, :], sm[:, 3, :], sm[:, 2, :], ALU.subtract).then_inc(ex_in, 1)
            v.wait_ge(ex_ok, 2)
            link(v.tensor_scalar(sm[:, 4, :], sm[:, 3, :], 1.0, None, ALU.add))
            link(v.reciprocal(sm[:, 4, :], sm[:, 4, :]))
            link(v.tensor_tensor(sm[:, 5, :], sm[:, 3, :], sm[:, 4, :], ALU.mult))
            link(v.tensor_tensor(oh1[:, :, :], oh1[:, :, :], up(sm[:, 4, :]), ALU.mult))
            link(v.tensor_tensor(oh2[:, :, :], oh2[:, :, :], up(sm[:, 5, :]), ALU.mult))
            link(v.tensor_tensor(t.comb[:, :, :], oh1[:, :, :], oh2[:, :, :], ALU.add))
    p.close()


def experts(nc, t, out, i):
    p = Phase(nc)
    sg = p.sb("gate_silu", [128, 2, 512])
    hid = p.sb("hidden", [128, 2, 2, 512])
    gp = [p.ps(f"gate_ps{b}", [128, 512]) for b in range(3)]
    up = [p.ps(f"up_ps{b}", [128, 512]) for b in range(3)]
    dn = [p.ps(f"down_ps{b}", [128, 512]) for b in range(2)]
    vch, gu_ps, sg_ok, hid_ok, dn_ps, dn_ok, out_ok, stored = (p.sem(n) for n in (
        "vch_m", "gu_ps", "sg_ok", "hid_ok", "dn_ps", "dn_ok", "out_ok", "stored"))
    jobs = [(e, b) for e in range(NE, -1, -1) for b in range(2)]
    with nc.Block() as block:
        @block.tensor
        def _(pe):
            def gate_up(n):
                e, b = jobs[n]
                for f in range(2):
                    k = 2 * n + f
                    if k >= 3:
                        pe.wait_ge(hid_ok, k - 2)
                    pe.matmul(gp[k % 3][:, :], t.wgu[:, e, 0, f * 128:(f + 1) * 128], t.h2T[:, b * 512:(b + 1) * 512],
                              start=True, stop=True)
                    pe.matmul(up[k % 3][:, :], t.wgu[:, e, 1, f * 128:(f + 1) * 128], t.h2T[:, b * 512:(b + 1) * 512],
                              start=True, stop=True).then_inc(gu_ps, 1)

            def down(n):
                e, b = jobs[n]
                pe.wait_ge(hid_ok, 2 * n + 2)
                if n >= 2:
                    pe.wait_ge(dn_ok, 4 * (n - 1))
                for c in range(4):
                    for f in range(2):
                        m = pe.matmul(dn[n % 2][:, c * 128:(c + 1) * 128], hid[:, n % 2, f, c * 128:(c + 1) * 128],
                                      t.wdn[:, e, f, :], start=f == 0, stop=f == 1)
                m.then_inc(dn_ps, 1)

            gate_up(0)
            for n in range(len(jobs)):
                if n + 1 < len(jobs):
                    gate_up(n + 1)
                down(n)

        @block.scalar
        def _(a):
            for k in range(2 * len(jobs)):
                a.wait_ge(gu_ps, k + 1)
                if k >= 2:
                    a.wait_ge(hid_ok, k - 1)
                a.activation(sg[:, k % 2, :], gp[k % 3][:, :], ACT.Silu).then_inc(sg_ok, 1)

        @block.vector
        def _(v):
            link = linker(v, vch)

            def hidden(n):
                for f in range(2):
                    k = 2 * n + f
                    v.wait_ge(sg_ok, k + 1)
                    if n >= 2:
                        v.wait_ge(dn_ps, n - 1)
                    v.tensor_tensor(hid[:, n % 2, f, :], up[k % 3][:, :], sg[:, k % 2, :], ALU.mult).then_inc(hid_ok, 1)

            def combine(n):
                e, b = jobs[n]
                v.wait_ge(dn_ps, n + 1)
                if n >= 2:
                    v.wait_ge(dn_ok, 4 * (n - 1))
                for c in range(4):
                    h = t.hf[:, 4 * b + c, :]
                    v.scalar_tensor_tensor(out=h, in0=dn[n % 2][:, c * 128:(c + 1) * 128],
                                           scalar=1.0 if e == NE else t.comb[:, 4 * b + c, e:e + 1], in1=h,
                                           op0=ALU.mult, op1=ALU.add).then_inc(dn_ok, 1)

            hidden(0)
            for n in range(len(jobs)):
                if n + 1 < len(jobs):
                    hidden(n + 1)
                combine(n)
            v.wait_ge(dn_ok, 4 * len(jobs))
            sh = [128, TILES, HID]
            link(v.tensor_tensor(t.hf[:, :, :], t.hf[:, :, :], bc(t.modbc[:, 5 * HID:6 * HID].unsqueeze(1), *sh), ALU.mult))
            v.tensor_tensor(t.x[:, :, :], t.x[:, :, :], t.hf[:, :, :], ALU.add).then_inc(out_ok, 1)

        @block.sync
        def _(sp):
            sp.wait_ge(out_ok, 1)
            for s in range(2):
                sp.dma_start(out[bass.ds(2 * i + s, 1), :, :].rearrange("a (c t) d -> t (a c) d", t=CK),
                             t.x[s * CK:(s + 1) * CK, :, :]).then_inc(stored, 16)
            sp.wait_ge(stored, 32)
    p.close()


class Tensors:
    pass


def build(nc, src, out):
    with ExitStack() as ctx:
        def sb(name, shape, dt=F32, c=ctx):
            return c.enter_context(nc.sbuf_tensor(name, shape, dt))

        t = Tensors()
        t.wc = sb("conv_w", [128, TAPS, 2 * KD + VD])
        t.wg = sb("wg", [128, VD])
        t.wo = sb("wo", [DV, NH, HID])
        t.wgb = sb("wgk_wb", [128, 2 * NH])
        t.wqkv = sb("wqkv", [128, 3 * HID])
        t.wo2 = sb("wo_ffn", [128, HID])
        t.wr = sb("router_w", [128, NE])
        t.n1w, t.n2w = sb("norm1_w", [128, 1]), sb("norm2_w", [128, 1])
        t.hrow = sb("dt_bias_b_b", [128, 2 * NH])
        t.nA = sb("neg_A", [128, NH])
        t.ident, t.identb = sb("ident", [128, 128]), sb("ident_bf16", [128, 128], BF16)
        t.ones, t.later, t.upto = sb("ones", [128, 128]), sb("later", [128, 128]), sb("upto", [128, 128])
        t.tri = sb("tri", [128, CK])
        t.negm = sb("neg_mask", [128, NP * CK], BF16)
        t.blk = sb("blk", [128, 4])
        t.low16, t.low32 = sb("low16", [128, CK]), sb("low32", [128, CK])
        t.mhalf = sb("minus_half", [128, 2 * NH])
        t.rank = sb("rank", [128, NE])
        t.pick = sb("pick", [B, PAIRS, 2])
        t.mod = sb("mod", [B, 6 * HID])
        t.x = sb("x", [128, TILES, HID])
        t.modbc = sb("mod_rows", [128, 6 * HID])
        t.hS = sb("h_shifted", [128, TAPS, TILES, 128])
        t.g, t.beta, t.Gam, t.nGam, t.kdec = (sb(n, [128, TILES, NH]) for n in ("g", "beta", "Gam", "neg_Gam", "k_decay"))
        t.gmask = sb("g_masked", [128, TILES, 2, NH])
        t.gam_all = sb("gam_all", [128, TILES, 2, NP])

        load_weights(nc, t, src)
        with nc.Fori(0, PAIRS) as i:
            with ExitStack() as a:
                t.S = sb("state", [128, 2, NP, DV], c=a)
                t.kqT = sb("kq_T", [128, HALF, NP, 2, 128], c=a)
                t.kd = sb("k_end", [128, HALF, KD], c=a)
                t.ap = sb("sys_and_qk", [128, HALF, NH, 2, CK], c=a)
                start_pair(nc, t, src, i)
                for half in range(2):
                    project_keys(nc, t, half)
                    with ExitStack() as b:
                        t.tt = sb(f"inverse_T_{half}", [128, SYS, CK], c=b)
                        invert_systems(nc, t, half)
                        scan_chunks(nc, t, half)
            with ExitStack() as a:
                t.hf = sb("h_ffn", [128, TILES, HID], c=a)
                t.cx = sb("ctx", [128, 4, TILES, 2, CK], c=a)
                t.h1T = sb("h1T", [128, 2, L], c=a)
                second_norm(nc, t)
                with ExitStack() as b:
                    t.qT, t.kT = (sb(n, [128, 8, L], BF16, c=b) for n in ("q_T", "k_T"))
                    t.va = sb("v_and_one", [128, TQ, AH, 32], c=b)
                    for s in range(2):
                        attention_scores(nc, t, s)
                        attention_values(nc, t, s)
                t.h2T = sb("h2T", [128, TILES * 128], c=a)
                t.comb = sb("combine", [128, TILES, NE], c=a)
                t.wgu = sb("gate_up_w", [128, NE + 1, 2, DFF], c=a)
                t.wdn = sb("down_w", [128, NE + 1, 2, HID], c=a)
                attention_output(nc, t, src)
                experts(nc, t, out, i)


def kernel(**inputs):
    import numpy as _np
    import concourse.bacc as _bacc
    from concourse import mybir as _mybir
    from concourse.bass_utils import run_bass_kernel_spmd as _run

    nc = _bacc.Bacc("TRN2", target_bir_lowering=False, num_devices=1)
    arrays, src = {}, {}
    for name in inputs:
        a = _np.ascontiguousarray(inputs[name])
        arrays[f"in_{name}"] = a
        src[name] = nc.dram_tensor(f"in_{name}", a.shape, _mybir.dt.from_np(a.dtype), kind="ExternalInput").ap()
    out = nc.dram_tensor("out0", (B, L, HID), F32, kind="ExternalOutput").ap()
    build(nc, src, out)
    r = _run(nc, [arrays], core_ids=[0])
    return r.results[0]["out0"]
```

```python
from contextlib import ExitStack

import concourse.bass as bass
from concourse import mybir

F32 = mybir.dt.float32
BF16 = mybir.dt.bfloat16
ALU = mybir.AluOpType
ACT = mybir.ActivationFunctionType
AX = mybir.AxisListType.X

B, L, HID = 8, 512, 128
NH, DK, DV = 12, 64, 128
TAPS = 4
PAD = TAPS - 1
CK = 64
PAIRS = B // 2
TILES = L // CK
HALF = TILES // 2
KD, VD = NH * DK, NH * DV
NP = NH // 2
G3 = 3
SYS = HALF * NH
BASE = 16
NBLK = 128 // BASE
AH, AD = 16, 8
SLOT = 64
NCH = (2 * KD + VD) // 128
TQ = L // 128
NE, DFF = 8, 256
NEG = -30000.0


class Phase:

    def __init__(self, nc, tag=""):
        self.nc, self.ctx, self.sems, self.tag = nc, ExitStack(), [], tag

    def sb(self, name, shape, dt=F32):
        return self.ctx.enter_context(self.nc.sbuf_tensor(name + self.tag, shape, dt))

    def ps(self, name, shape, dt=F32):
        return self.ctx.enter_context(self.nc.psum_tensor(name + self.tag, shape, dt))

    def sem(self, name):
        s = self.ctx.enter_context(self.nc.semaphore(name + self.tag))
        self.sems.append(s.num)
        return s

    def close(self):
        self.ctx.close()
        self.nc.all_engine_barrier(sems_to_clear=range(min(self.sems), max(self.sems) + 1))


def linker(eng, sem):
    count = [0]

    def link(ins):
        count[0] += 1
        ins.then_inc(sem, 1)
        eng.wait_ge(sem, count[0])

    return link


def bc(ap, *shape):
    return ap.broadcast_to(list(shape))


def load_weights(nc, t, src):
    p = Phase(nc)
    row = p.sb("head_row", [1, 3 * NH])
    crow = p.sb("c_row", [B, HID])
    wmod = p.sb("wmod_sb", [HID, 6 * HID])
    csil = p.sb("c_silu", [B, HID])
    cT = p.sb("c_silu_T", [HID, B])
    msgn = p.sb("mod_sign", [B, HID])
    mabs = p.sb("mod_abs", [B, HID])
    blk8 = p.sb("blk8", [128, NBLK])
    gnw = p.sb("gnw", [DV, 1])
    misc_ps = p.ps("misc_ps", [128, 4, 512])
    loaded, consts, pchain, vchain = p.sem("loaded"), p.sem("consts"), p.sem("pool_chain"), p.sem("vec_chain")
    a_log, row_done, c_silu, cT_ps, cT_sb, mod_ps, nA_done = (p.sem(n) for n in (
        "a_log", "row_done", "c_silu_done", "cT_ps", "cT_sb", "mod_ps_done", "nA_done"))
    with nc.Block() as block:
        @block.sync
        def _(sp):
            for name, at, w in (("L0_attn_Wk", 0, KD), ("L0_attn_Wq", KD, KD), ("L0_attn_Wv", 2 * KD, VD)):
                sp.dma_start(t.w[:, at:at + w], src[name]).then_inc(loaded, 16)
            for name, at, w in (("L0_attn_conv_k", 0, KD), ("L0_attn_conv_q", KD, KD), ("L0_attn_conv_v", 2 * KD, VD)):
                sp.dma_start(t.taps[:, at // 128:(at + w) // 128, :],
                             src[name].rearrange("(b p) k -> p b k", p=128)).then_inc(loaded, 16)
            for name, at in (("L0_attn_dt_bias", 0), ("L0_attn_b_b", NH), ("L0_attn_A_log", 2 * NH)):
                sp.dma_start(row[:, at:at + NH], src[name].rearrange("(a c) -> a c", a=1)).then_inc(loaded, 16)
            sp.dma_start(crow[:, :], src["L0_c"]).then_inc(loaded, 16)
            sp.dma_start(wmod[:, :], src["L0_wmod"]).then_inc(loaded, 16)
            sp.dma_start(t.wg[:, :], src["L0_attn_Wg"]).then_inc(loaded, 16)
            sp.dma_start(t.wo[:, :, :], src["L0_attn_Wo"].rearrange("(h p) d -> p h d", p=DV)).then_inc(loaded, 16)
            sp.dma_start(t.wgb[:, 0:NH], src["L0_attn_Wgk"]).then_inc(loaded, 16)
            sp.dma_start(t.wgb[:, NH:2 * NH], src["L0_attn_Wb"]).then_inc(loaded, 16)
            for m, name in enumerate(("L0_ffn_wq", "L0_ffn_wk", "L0_ffn_wv")):
                sp.dma_start(t.wqkv[:, m * HID:(m + 1) * HID], src[name]).then_inc(loaded, 16)
            sp.dma_start(t.wo2[:, :], src["L0_ffn_wo"]).then_inc(loaded, 16)
            sp.dma_start(t.wr[:, :], src["L0_ffn_router_w"]).then_inc(loaded, 16)
            sp.dma_start(gnw[:, :], src["L0_attn_g_norm_weight"].rearrange("(p a) -> p a", a=1)).then_inc(loaded, 16)
            sp.dma_start(t.n1w[:, :], src["L0_ffn_norm1_w"].rearrange("(p a) -> p a", a=1)).then_inc(loaded, 16)
            sp.dma_start(t.n2w[:, :], src["L0_ffn_norm2_w"].rearrange("(p a) -> p a", a=1)).then_inc(loaded, 16)
        NLOAD = 16 * 23

        @block.gpsimd
        def _(g):
            link = linker(g, pchain)
            link(g.memset(t.ident[:, :], 0.0))
            link(g.affine_select(out=t.ident[:, :], in_=t.ident[:, :], compare_op=ALU.not_equal, fill=1.0,
                                 base=0, pattern=[[-1, 128]], channel_multiplier=1))
            g.memset(t.ones[:, :], 1.0).then_inc(consts, 1)
            link(g.memset(t.later[:, :], 1.0))
            link(g.affine_select(out=t.later[:, :], in_=t.later[:, :], compare_op=ALU.is_gt, fill=0.0,
                                 base=0, pattern=[[-1, 128]], channel_multiplier=1))
            link(g.memset(t.later[CK:128, 0:CK], 0.0))
            link(g.memset(t.upto[:, :], 1.0))
            link(g.affine_select(out=t.upto[:, :], in_=t.upto[:, :], compare_op=ALU.is_ge, fill=0.0,
                                 base=0, pattern=[[1, 128]], channel_multiplier=-1))
            link(g.memset(t.upto[0:CK, CK:128], 0.0))
            link(g.tensor_copy(t.tri[0:CK, :], t.upto[0:CK, 0:CK]))
            link(g.tensor_copy(t.tri[CK:128, :], t.upto[CK:128, CK:128]))
            link(g.memset(blk8[:, :], 1.0))
            link(g.affine_select(out=blk8[:, :], in_=blk8[:, :], compare_op=ALU.is_ge, fill=0.0,
                                 base=0, pattern=[[-BASE, NBLK]], channel_multiplier=1))
            link(g.affine_select(out=blk8[:, :], in_=blk8[:, :], compare_op=ALU.is_ge, fill=0.0,
                                 base=BASE - 1, pattern=[[BASE, NBLK]], channel_multiplier=-1))
            link(g.tensor_copy(t.parity[:, :], blk8[:, 0:2]))
            for b in range(2, NBLK, 2):
                link(g.tensor_tensor(t.parity[:, :], t.parity[:, :], blk8[:, b:b + 2], ALU.add))
            link(g.memset(t.mhalf[:, :], -0.5))
            link(g.memset(t.hT[:, :, 0:PAD], 0.0))
            for b in range(NE):
                link(g.memset(t.rank[:, b:b + 1], float(NE - b)))
            link(g.memset(t.pick[:, :, :], 0.0))
            link(g.affine_select(out=t.pick[:, :, :], in_=t.pick[:, :, :], compare_op=ALU.not_equal, fill=1.0,
                                 base=0, pattern=[[-2, PAIRS], [-1, 2]], channel_multiplier=1))
            g.memset(t.gmask[:, :, :, :], 0.0).then_inc(consts, 1)

        @block.scalar
        def _(a):
            a.wait_ge(loaded, NLOAD)
            a.activation(csil[:, :], crow[:, :], ACT.Silu).then_inc(c_silu, 1)
            a.wait_ge(cT_ps, 1)
            a.activation(cT[:, :], misc_ps[:, 1, 0:B], ACT.Copy).then_inc(cT_sb, 1)
            a.wait_ge(a_log, 1)
            a.activation(t.nA[:, :], t.nA[:, :], ACT.Exp).then_inc(nA_done, 1)

        @block.tensor
        def _(pe):
            pe.wait_ge(loaded, NLOAD)
            pe.wait_ge(consts, 2)
            pe.matmul(misc_ps[:, 0, 0:3 * NH], t.ones[0:1, :], row[:, :], start=True, stop=True).then_inc(row_done, 1)
            pe.wait_ge(c_silu, 1)
            pe.transpose(misc_ps[:, 1, 0:B], csil[:, :], t.ident[0:B, 0:B]).then_inc(cT_ps, 1)
            pe.wait_ge(cT_sb, 1)
            for c in range(2):
                m = pe.matmul(misc_ps[0:B, 2 + c, 0:384], cT[:, :], wmod[:, c * 384:(c + 1) * 384], start=True, stop=True)
            m.then_inc(mod_ps, 1)

        @block.vector
        def _(v):
            link = linker(v, vchain)
            v.wait_ge(loaded, NLOAD)
            v.wait_ge(consts, 2)
            v.wait_ge(row_done, 1)
            link(v.tensor_copy(t.hrow[:, :], misc_ps[:, 0, 0:2 * NH]))
            v.tensor_copy(t.nA[:, :], misc_ps[:, 0, 2 * NH:3 * NH]).then_inc(a_log, 1)
            v.wait_ge(nA_done, 1)
            link(v.tensor_scalar(t.nA[:, :], t.nA[:, :], -1.0, None, ALU.mult))
            link(v.tensor_scalar(t.wo[:, :, :].rearrange("p h d -> p (h d)"), t.wo[:, :, :].rearrange("p h d -> p (h d)"),
                                 gnw[:, 0:1], None, ALU.mult))
            link(v.tensor_copy(t.identb[:, :], t.ident[:, :]))
            for k in range(8):
                link(v.tensor_scalar(t.negm[:, k * CK:(k + 1) * CK], t.tri[:, :], -NEG, NEG, ALU.mult, ALU.add))
            v.wait_ge(mod_ps, 1)
            for m in range(6):
                o, i = t.mod[:, m * HID:(m + 1) * HID], misc_ps[0:B, 2 + m // 3, (m % 3) * HID:(m % 3 + 1) * HID]
                if m % 3 == 0:
                    link(v.tensor_copy(o, i))
                elif m % 3 == 1:
                    link(v.tensor_scalar(o, i, 1.0, None, ALU.add))
                else:
                    link(v.tensor_scalar(msgn[:, :], i, 0.0, 2.0, ALU.is_ge, ALU.mult))
                    link(v.tensor_scalar(mabs[:, :], i, -1.0, None, ALU.mult))
                    link(v.tensor_tensor(mabs[:, :], i, mabs[:, :], ALU.max))
                    link(v.tensor_scalar(mabs[:, :], mabs[:, :], 0.25, None, ALU.max))
                    link(v.tensor_scalar(msgn[:, :], msgn[:, :], -1.0, None, ALU.add))
                    link(v.tensor_tensor(o, msgn[:, :], mabs[:, :], ALU.mult))
    p.close()


def start_pair(nc, t, src, i):
    p = Phase(nc)
    cen, sq = p.sb("cen", [128, TILES, HID]), p.sb("sq", [128, TILES, HID])
    st = p.sb("ln_st", [128, 2, TILES])
    sel = p.sb("sel", [B, 128])
    zg, zb, za, ze = (p.sb(n, [128, TILES, NH]) for n in ("zg", "zb", "za", "ze"))
    ps = p.ps("ps_a1", [128, 8, 512])
    x_in, vch, pow_in, pow_out, sel_ok, mod_ok = (p.sem(n) for n in ("x_in", "vch", "pow_in", "pow_out", "sel_ok", "mod_ok"))
    modbc, h_ok, hT_ps, hT_ok, z_ps, z_ok = (p.sem(n) for n in ("modbc_ok", "h_ok", "hT_ps", "hT_ok", "z_ps", "z_ok"))
    e_ok, l_in, l_ok, g_ok, stat_ps, stat_ok = (p.sem(n) for n in ("e_ok", "l_in", "l_ok", "g_ok", "stat_ps", "stat_ok"))
    beta_ok, s0, hS_ok = (p.sem(n) for n in ("beta_ok", "s0", "hS_ok"))
    with nc.Block() as block:
        @block.sync
        def _(sp):
            for s in range(2):
                sp.dma_start(t.x[s * CK:(s + 1) * CK, :, :],
                             src["L0_attn_hidden_states"][bass.ds(2 * i + s, 1), :, :]
                             .rearrange("a (c t) d -> t (a c) d", t=CK)).then_inc(x_in, 16)

        @block.gpsimd
        def _(g):
            g.memset(t.S[:, :, :, :], 0.0).then_inc(s0, 1)
            g.memset(t.pp[:, :, :, :], 0.0).then_inc(s0, 1)
            g.wait_ge(pow_in, 1)
            g.tensor_tensor(st[:, 1, :], st[:, 1, :], t.mhalf[:, 0:TILES], ALU.pow).then_inc(pow_out, 1)

        @block.vector
        def _(v):
            link = linker(v, vch)

            v.tensor_copy(sel[:, :].rearrange("b (s t) -> b s t", s=2),
                          bc(t.pick[:, bass.ds(i, 1), :].rearrange("b a s -> b (a s)").unsqueeze(2), B, 2, CK)).then_inc(sel_ok, 1)
            v.wait_ge(x_in, 32)
            sh = [128, TILES, HID]
            link(v.tensor_reduce(st[:, 0, :], t.x[:, :, :], AX, ALU.add))
            link(v.tensor_scalar(st[:, 0, :], st[:, 0, :], 1.0 / HID, None, ALU.mult))
            link(v.tensor_tensor(cen[:, :, :], t.x[:, :, :], bc(st[:, 0, :].unsqueeze(2), *sh), ALU.subtract))
            link(v.tensor_tensor(sq[:, :, :], cen[:, :, :], cen[:, :, :], ALU.mult))
            link(v.tensor_reduce(st[:, 1, :], sq[:, :, :], AX, ALU.add))
            v.tensor_scalar(st[:, 1, :], st[:, 1, :], 1.0 / HID, 1e-5, ALU.mult, ALU.add).then_inc(pow_in, 1)
            v.wait_ge(mod_ok, 1)
            v.tensor_copy(t.modbc[:, 0:512], ps[:, 0, :]).then_inc(modbc, 1)
            v.tensor_copy(t.modbc[:, 512:768], ps[:, 1, 0:256]).then_inc(modbc, 1)
            v.wait_ge(pow_out, 1)
            link(v.tensor_tensor(cen[:, :, :], cen[:, :, :], bc(st[:, 1, :].unsqueeze(2), *sh), ALU.mult))
            v.wait_ge(modbc, 2)
            link(v.tensor_tensor(cen[:, :, :], cen[:, :, :], bc(t.modbc[:, HID:2 * HID].unsqueeze(1), *sh), ALU.mult))
            v.tensor_tensor(cen[:, :, :], cen[:, :, :], bc(t.modbc[:, 0:HID].unsqueeze(1), *sh), ALU.add).then_inc(h_ok, 1)
            v.wait_ge(z_ps, 1)
            z = ps[:, 4, 0:TILES * 2 * NH].rearrange("p (c z) -> p c z", c=TILES)
            hs = [128, TILES, NH]
            link(v.tensor_tensor(zg[:, :, :], z[:, :, 0:NH], bc(t.hrow[:, 0:NH].unsqueeze(1), *hs), ALU.add))
            v.tensor_tensor(zb[:, :, :], z[:, :, NH:2 * NH], bc(t.hrow[:, NH:2 * NH].unsqueeze(1), *hs), ALU.add).then_inc(z_ok, 1)
            link(v.tensor_scalar(za[:, :, :], zg[:, :, :], -1.0, None, ALU.mult))
            v.tensor_tensor(za[:, :, :], zg[:, :, :], za[:, :, :], ALU.max).then_inc(z_ok, 1)
            v.wait_ge(e_ok, 1)
            v.tensor_scalar(ze[:, :, :], ze[:, :, :], 1.0, None, ALU.add).then_inc(l_in, 1)
            link(v.tensor_scalar(zg[:, :, :], zg[:, :, :], 0.0, None, ALU.max))
            v.wait_ge(l_ok, 1)
            link(v.tensor_tensor(zg[:, :, :], zg[:, :, :], ze[:, :, :], ALU.add))
            link(v.tensor_tensor(t.g[:, :, :], zg[:, :, :], bc(t.nA[:, :].unsqueeze(1), *hs), ALU.mult))
            v.tensor_copy(t.gmask[0:CK, :, 0, :], t.g[0:CK, :, :]).then_inc(g_ok, 1)
            v.tensor_copy(t.gmask[CK:128, :, 1, :], t.g[CK:128, :, :]).then_inc(g_ok, 1)
            v.wait_ge(stat_ok, 4)
            v.wait_ge(beta_ok, 1)
            link(v.tensor_tensor(t.kdec[:, :, :], t.kdec[:, :, :], t.beta[:, :, :], ALU.mult))
            link(v.tensor_scalar(t.nGam[:, :, :], t.Gam[:, :, :], -1.0, None, ALU.mult))

        @block.scalar
        def _(a):
            for b in range(2):
                a.wait_ge(hT_ps, b + 1)
                a.activation(t.hT[:, :, PAD + 256 * b:PAD + 256 * (b + 1)].rearrange("p s (c t) -> p c s t", c=4),
                             ps[:, 2 + b, :].rearrange("p (c s t) -> p c s t", c=4, s=2), ACT.Copy).then_inc(hT_ok, 1)
            for b in range(2):
                a.activation(t.hS[:, 4 * b:4 * b + 4, :].rearrange("p c t -> p (c t)"), ps[:, 2 + b, :],
                             ACT.Copy).then_inc(hS_ok, 1)
            a.wait_ge(z_ok, 1)
            a.activation(t.beta[:, :, :], zb[:, :, :], ACT.Sigmoid).then_inc(beta_ok, 1)
            a.wait_ge(z_ok, 2)
            a.activation(ze[:, :, :], za[:, :, :], ACT.Exp, scale=-1.0).then_inc(e_ok, 1)
            a.wait_ge(l_in, 1)
            a.activation(ze[:, :, :], ze[:, :, :], ACT.Ln).then_inc(l_ok, 1)
            a.wait_ge(stat_ps, 1)
            w = TILES * NH
            a.activation(t.Gam[:, :, :].rearrange("p c h -> p (c h)"), ps[:, 5, 0:w], ACT.Exp).then_inc(stat_ok, 1)
            a.activation(t.kdec[:, :, :].rearrange("p c h -> p (c h)"), ps[:, 6, 0:w], ACT.Exp).then_inc(stat_ok, 1)
            gv = ps[:, 7, 0:2 * w].rearrange("p (c s h r) -> p r (c s) h", c=TILES, s=2, r=2)
            for r in range(2):
                rows = slice(r * 64, (r + 1) * 64)
                a.activation(t.gam_all[rows, :, :, :].rearrange("p c s h -> p (c s) h"),
                             gv[rows, r, :, :], ACT.Exp).then_inc(stat_ok, 1)

        @block.tensor
        def _(pe):
            pe.wait_ge(sel_ok, 1)
            pe.matmul(ps[:, 0, :], sel[:, :], t.mod[:, 0:512], start=True, stop=True)
            pe.matmul(ps[:, 1, 0:256], sel[:, :], t.mod[:, 512:768], start=True, stop=True).then_inc(mod_ok, 1)
            pe.wait_ge(h_ok, 1)
            for c in range(TILES):
                m = pe.transpose(ps[:, 2 + c // 4, (c % 4) * 128:(c % 4 + 1) * 128], cen[:, c, :], t.ident[:, :])
                if c % 4 == 3:
                    m.then_inc(hT_ps, 1)
            pe.wait_ge(hS_ok, 2)
            for c in range(TILES):
                m = pe.matmul(ps[:, 4, c * 2 * NH:(c + 1) * 2 * NH], t.hS[:, c, :],
                              t.wgb[:, :], start=True, stop=True)
            m.then_inc(z_ps, 1)
            pe.wait_ge(g_ok, 2)
            gf = t.g[:, :, :].rearrange("p c h -> p (c h)")
            pe.matmul(ps[:, 5, 0:TILES * NH], t.upto[:, :], gf, start=True, stop=True)
            pe.matmul(ps[:, 6, 0:TILES * NH], t.later[:, :], gf, start=True, stop=True)
            pe.matmul(ps[:, 7, 0:2 * TILES * NH], t.ones[:, :], t.gmask[:, :, :, :].rearrange("p c s h -> p (c s h)"),
                      start=True, stop=True).then_inc(stat_ps, 1)
    p.close()


def convolve_matmul(pe, t, o, half, block, s):
    at = half * HALF * CK
    return pe.matmul(o, t.w[:, block * 128:(block + 1) * 128], t.hT[:, s, at:at + PAD + HALF * CK], start=True, stop=True)


def project_keys(nc, t, half):
    p = Phase(nc, f"_{half}")
    N = HALF * CK
    ac = p.sb("conv_acc", [128, 2, 2, N])
    sl = p.sb("conv_silu", [128, 2, HALF, 2, CK])
    tk = p.sb("kq_tokens", [128, 2, 2, HALF, 2, DK])
    sq = p.sb("kq_sq", [128, 2 * HALF * 2, DK])
    ss = p.sb("kq_ss", [128, 2, 2, HALF, 2])
    co = p.sb("kq_coef", [128, 2, 3, HALF, 2])
    kn, qn, qg = (p.sb(n, [128, HALF, 2, DK]) for n in ("kn", "qn", "qg"))
    seg = p.sb("seg_rhs", [128, HALF, 2, CK])
    ex = p.sb("decay", [128, 2, HALF, 2, CK])
    cv = [p.ps(f"conv_ps{b}", [128, 2, 512]) for b in range(2)]
    tp = [p.ps(f"trp{b}", [128, 512]) for b in range(2)]
    sk = [p.ps(f"seg_kk{b}", [128, 512]) for b in range(2)]
    names = ("conv_ps", "conv_init", "conv_done", "silu_done", "tok_ps", "tok_done", "sq_done", "ss_done", "ss_eps",
             "rs_done", "coef_done", "kn_done", "qn_done", "qg_done", "kend_done", "seg_rhs_done", "seg_ps", "exp_done",
             "decay_done", "key_ps", "key_done", "kk_ps", "kk_used", "vch2")
    (conv_ps, conv_init, conv_done, silu, tok_ps, tok_done, sq_done, ss_done, ss_eps, rs_done, coef, kn_done, qn_done,
     qg_done, kend_done, seg_rhs, seg_ps, exp_done, decay, key_ps, key_done, kk_ps, kk_used, vch) = (p.sem(n) for n in names)
    sh = [128, HALF, 2, DK]
    C0 = half * HALF
    trs = [("tok", 0), ("tok", 1)]
    for n in range(NP):
        if n + 1 < NP:
            trs += [("tok", 2 * n + 2), ("tok", 2 * n + 3)]
        trs += [("key", 3 * n), ("key", 3 * n + 1), ("key", 3 * n + 2)]
    place = {job: n for n, job in enumerate(trs)}

    with nc.Block() as block:
        @block.tensor
        def _(pe):
            def convolve(n):
                for w in range(2):
                    m = 2 * n + w
                    if m >= 2:
                        pe.wait_ge(conv_done, 3 * (m - 1))
                    for s in range(2):
                        last = convolve_matmul(pe, t, cv[m % 2][:, s, 0:PAD + N], half, w * NP + n, s)
                    last.then_inc(conv_ps, 1)

            def transposes(job, source):
                kind, n = job
                at = place[job]
                if at >= 2:
                    old, m = trs[at - 2]
                    pe.wait_ge(tok_done if old == "tok" else key_done, m + 1)
                for c in range(HALF):
                    last = pe.transpose(tp[at % 2][:, c * 128:(c + 1) * 128], source(c), t.ident[:, :])
                last.then_inc(tok_ps if kind == "tok" else key_ps, 1)

            def tokens(n):
                for w in range(2):
                    pe.wait_ge(silu, 2 * n + w + 1)
                    transposes(("tok", 2 * n + w), lambda c: sl[:, w, c, :, :].rearrange("p s t -> p (s t)"))

            def segments(n):
                pe.wait_ge(seg_rhs, n + 1)
                if n:
                    pe.wait_ge(kk_used, 2 * n - 1)
                o = sk[3 * n % 2][:, :]
                pe.matmul(o, t.later[:, :], seg[:, :, :, :].rearrange("p c h i -> p (c h i)"), start=True, stop=False)
                pe.matmul(o, t.identb[:, :], t.negm[:, :], start=False, stop=True).then_inc(seg_ps, 1)

            def products(n):
                pe.wait_ge(key_done, 3 * n + 2)
                for r in range(2):
                    if n or r:
                        pe.wait_ge(kk_used, 2 * n) if not r else pe.wait_ge(exp_done, n + 1)
                    rows = slice(r * 64, (r + 1) * 64)
                    for c in range(HALF):
                        for s in range(2):
                            cs = slice(s * CK, (s + 1) * CK)
                            m = pe.matmul(sk[(3 * n + 1 + r) % 2][cs, c * 128:(c + 1) * 128], t.kqT[rows, c, n, 0, cs],
                                          t.kqT[rows, c, n, :, cs], start=True, stop=True)
                    m.then_inc(kk_ps, 1)

            convolve(0)
            convolve(1)
            tokens(0)
            for n in range(NP):
                if n + 1 < NP:
                    tokens(n + 1)
                if n + 2 < NP:
                    convolve(n + 2)
                segments(n)
                for k, (ready, source) in enumerate(((kn_done, kn), (qn_done, qn), (qg_done, qg))):
                    if k == 2:
                        products(n)
                    pe.wait_ge(ready, n + 1)
                    transposes(("key", 3 * n + k), lambda c: source[:, c, :, :].rearrange("p h d -> p (h d)"))

        @block.scalar
        def _(a):
            def start_sum(n):
                for w in range(2):
                    a.wait_ge(conv_ps, 2 * n + w + 1)
                    if n:
                        a.wait_ge(silu, 2 * (n - 1) + w + 1)
                    a.activation(ac[:, w, :, :], cv[w][:, :, PAD:PAD + N], ACT.Copy,
                                 scale=t.taps[:, w * NP + n, PAD:PAD + 1]).then_inc(conv_init, 1)

            def silus(n):
                for w in range(2):
                    a.wait_ge(conv_done, 3 * (2 * n + w + 1))
                    if n:
                        a.wait_ge(tok_ps, 2 * (n - 1) + w + 1)
                    a.activation(sl[:, w, :, :, :].rearrange("p c s t -> p s c t"),
                                 ac[:, w, :, :].rearrange("p s (c t) -> p s c t", c=HALF), ACT.Silu).then_inc(silu, 1)

            def tokens(n):
                if n >= 2:
                    a.wait_ge(qn_done, n - 1)
                    a.wait_ge(qg_done, n - 1)
                    a.wait_ge(kend_done, n - 1)
                for w in range(2):
                    a.wait_ge(tok_ps, 2 * n + w + 1)
                    a.activation(tk[:, n % 2, w, :, :, :].rearrange("p c h d -> p (c h d)"),
                                 tp[place[("tok", 2 * n + w)] % 2][:, :], ACT.Copy).then_inc(tok_done, 1)
                a.wait_ge(tok_done, 2 * n + 2)
                if n:
                    a.wait_ge(ss_done, n)
                a.activation(sq[:, :, :].rearrange("p x d -> p (x d)"),
                             tk[:, n % 2, :, :, :, :].rearrange("p w c h d -> p (w c h d)"), ACT.Square).then_inc(sq_done, 1)

            start_sum(0)
            silus(0)
            start_sum(1)
            tokens(0)
            for n in range(NP):
                if n + 1 < NP:
                    silus(n + 1)
                    tokens(n + 1)
                if n + 2 < NP:
                    start_sum(n + 2)
                a.wait_ge(seg_ps, n + 1)
                if n >= 2:
                    a.wait_ge(kk_used, 2 * (n - 1))
                a.activation(ex[:, n % 2, :, :, :].rearrange("p c h i -> p (c h i)"), sk[3 * n % 2][:, :],
                             ACT.Exp).then_inc(exp_done, 1)
                for k in range(3):
                    a.wait_ge(key_ps, 3 * n + k + 1)
                    if k == 2:
                        a.wait_ge(kk_ps, 2 * (n + 1))
                    a.activation(t.kqT[:, :, n, min(k, 1), :],
                                 tp[place[("key", 3 * n + k)] % 2][:, :].rearrange("p (c i) -> p c i", c=HALF),
                                 ACT.Copy).then_inc(key_done, 1)

        @block.vector
        def _(v):
            link = linker(v, vch)

            def convolve(n):
                for w in range(2):
                    v.wait_ge(conv_init, 2 * n + w + 1)
                    for j in range(PAD):
                        if j:
                            v.wait_ge(conv_done, 3 * (2 * n + w) + j)
                        v.scalar_tensor_tensor(out=ac[:, w, :, :], in0=cv[w][:, :, j:j + N],
                                               scalar=t.taps[:, w * NP + n, j:j + 1], in1=ac[:, w, :, :],
                                               op0=ALU.mult, op1=ALU.add).then_inc(conv_done, 1)

            def norms(n):
                S, Co = ss[:, n % 2, :, :, :], co[:, n % 2, :, :, :]
                v.wait_ge(sq_done, n + 1)
                if n >= 2:
                    v.wait_ge(kend_done, n - 1)
                    v.wait_ge(qg_done, n - 1)
                flat = S.rearrange("p w c h -> p (w c h)")
                v.tensor_reduce(flat, sq[:, :, :], AX, ALU.add).then_inc(ss_done, 1)
                v.wait_ge(ss_done, n + 1)
                v.tensor_scalar(flat, flat, 1e-6, None, ALU.add).then_inc(ss_eps, 1)
                v.wait_ge(rs_done, n + 1)
                hs = slice(2 * n, 2 * n + 2)
                v.tensor_tensor(Co[:, 0, :, :], S[:, 0, :, :], t.kdec[:, C0:C0 + HALF, hs], ALU.mult).then_inc(coef, 1)
                link(v.tensor_scalar(Co[:, 1, :, :], S[:, 1, :, :], DK ** -0.5, None, ALU.mult))
                v.tensor_tensor(Co[:, 2, :, :], Co[:, 1, :, :], t.Gam[:, C0:C0 + HALF, hs], ALU.mult).then_inc(coef, 1)
                if n:
                    v.wait_ge(key_ps, 3 * (n - 1) + 2)
                v.tensor_tensor(kn[:, :, :, :], tk[:, n % 2, 0, :, :, :], bc(S[:, 0, :, :].unsqueeze(3), *sh),
                                ALU.mult).then_inc(kn_done, 1)
                v.tensor_tensor(qn[:, :, :, :], tk[:, n % 2, 1, :, :, :], bc(Co[:, 1, :, :].unsqueeze(3), *sh),
                                ALU.mult).then_inc(qn_done, 1)

            convolve(0)
            convolve(1)
            norms(0)
            for n in range(NP):
                if n + 2 < NP:
                    convolve(n + 2)
                if n + 1 < NP:
                    norms(n + 1)
                v.wait_ge(decay, n + 1)
                for r in range(2):
                    v.wait_ge(kk_ps, 2 * n + r + 1)
                    z = sk[(3 * n + 1 + r) % 2][:, :].rearrange("p (c m i) -> p c m i", c=HALF, m=2)
                    e = ex[:, n % 2, :, r, :]
                    v.tensor_tensor(t.aa[:, :, 2 * n + r, :], z[:, :, 0, :], e, ALU.mult)
                    for s in range(2):
                        cs = slice(s * CK, (s + 1) * CK)
                        m = v.tensor_tensor(t.pp[cs, :, 2 * n + r, cs], z[cs, :, 1, :], e[cs, :, :], ALU.mult)
                    m.then_inc(kk_used, 1)

        @block.gpsimd
        def _(g):
            def before(n):
                hs = slice(2 * n, 2 * n + 2)
                if n:
                    g.wait_ge(seg_ps, n)
                g.tensor_tensor(seg[:, :, :, :], bc(t.g[:, C0:C0 + HALF, hs].unsqueeze(3), *sh),
                                bc(t.tri[:, :].unsqueeze(1).unsqueeze(1), *sh), ALU.mult).then_inc(seg_rhs, 1)
                g.wait_ge(ss_eps, n + 1)
                flat = ss[:, n % 2, :, :, :].rearrange("p w c h -> p (w c h)")
                g.tensor_tensor(flat, flat, t.mhalf[:, 0:4 * HALF], ALU.pow).then_inc(rs_done, 1)
                g.wait_ge(coef, 2 * n + 2)
                if n:
                    g.wait_ge(key_ps, 3 * n)
                g.tensor_tensor(qg[:, :, :, :], tk[:, n % 2, 1, :, :, :], bc(co[:, n % 2, 2, :, :].unsqueeze(3), *sh),
                                ALU.mult).then_inc(qg_done, 1)
                g.tensor_tensor(t.kd[:, :, n * 128:(n + 1) * 128].rearrange("p c (h d) -> p c h d", h=2),
                                tk[:, n % 2, 0, :, :, :], bc(co[:, n % 2, 0, :, :].unsqueeze(3), *sh),
                                ALU.mult).then_inc(kend_done, 1)

            before(0)
            for n in range(NP):
                g.wait_ge(exp_done, n + 1)
                g.tensor_tensor(ex[:, n % 2, :, :, :], ex[:, n % 2, :, :, :],
                                bc(t.beta[:, C0:C0 + HALF, 2 * n:2 * n + 2].unsqueeze(3), *sh), ALU.mult).then_inc(decay, 1)
                if n + 1 < NP:
                    before(n + 1)
    p.close()


def invert_systems(nc, t, half):
    p = Phase(nc, f"_{half}")
    N = HALF * CK
    W = 2 * BASE
    G1, J1 = SYS // 2, 2
    G2, J2 = 16, SYS // 16
    first, second = (p.sb(n, [128, BASE * 128]) for n in ("work_a", "work_b"))
    blocks = lambda w: w[0:SYS, :].rearrange("g (i b j) -> g i b j", i=BASE, b=NBLK)
    a16, t16, c16 = blocks(first), blocks(second), blocks(first)
    tt32 = p.sb("blocks_T", [128, SYS, W])
    tn32 = first[:, 0:SYS * W].rearrange("p (g i) -> p g i", g=SYS)
    xs = [second[:, n * G1 * W:(n + 1) * G1 * W].rearrange("p (g i) -> p g i", g=G1) for n in range(J1)]
    x2 = [w[:, at:at + G2 * W].rearrange("p (g i) -> p g i", g=G2)
          for w, at in ((first, SYS * W), (second, SYS * W), (second, 0))]
    scratch = t.tt[:, :, :].rearrange("p g i -> p (g i)")
    ac = scratch[:, 0:4 * N].rearrange("p (r s n) -> p r s n", r=2, s=2)
    sl = scratch[:, 4 * N:8 * N].rearrange("p (r c s n) -> p r c s n", r=2, c=HALF, s=2)
    tmp = scratch[0:SYS, 8 * N:8 * N + 64 * NBLK]
    ps = p.ps("ps_inv", [128, 8, 512])
    names = ("sel_ps", "a16_ok", "unit_ok", "substituted", "c16_ok", "back_ps", "blocks_ok", "xs_zero", "x_ps", "x_ok",
             "y_ps", "y_ok", "conv_ps_v", "conv_init_v", "conv_done_v", "silu_done_v", "v_ps", "v_done", "tt_zero",
             "tt_done")
    (sel_ps, a16_ok, unit_ok, sub, c16_ok, back_ps, blocks_ok, xs_zero, x_ps, x_ok, y_ps, y_ok,
     conv_ps, conv_init, conv_done, silu, v_ps, v_done, tt_zero, tt_done) = (p.sem(n) for n in names)
    av = t.aa[:, :, :, :].rearrange("p c h i -> p (c h) i")
    SUBS = 2 * (BASE - 1)
    cv = lambda n: ps[:, 4 + 2 * (n % 2):6 + 2 * (n % 2), :]
    view = lambda bank, w, g: ps[:, bank, 0:g * w].rearrange("p (g i) -> p g i", g=g)
    x2bank, y2bank = (4, 5, 6), (7, 0, 1)
    quarter = [slice(32 * q, 32 * q + 32) for q in range(4)]
    with nc.Block() as block:
        @block.tensor
        def _(pe):
            idv = t.ident[:, :].rearrange("p (s b j) -> p s b j", s=2, b=4)
            for i in range(BASE):
                for b in range(4):
                    o = ps[0:SYS, i // 4, (i % 4) * 128:(i % 4 + 1) * 128].rearrange("p (s b j) -> p s b j", s=2, b=4)
                    m = pe.matmul(o[:, :, b, :], av[:, :, b * BASE + i], idv[:, :, b, :], start=True, stop=True)
                if i % 4 == 3:
                    m.then_inc(sel_ps, 1)

            def convolve(n):
                if n >= 2:
                    pe.wait_ge(conv_done, 3 * (n - 1))
                for s in range(2):
                    last = convolve_matmul(pe, t, cv(n)[:, s, 0:PAD + N], half, 2 * NP + n, s)
                last.then_inc(conv_ps, 1)

            convolve(0)
            convolve(1)
            pe.wait_ge(a16_ok, 4)
            for n in range(NH):
                if n >= 2:
                    pe.wait_ge(v_done, n - 1)
                if n + 2 < NH:
                    convolve(n + 2)
                pe.wait_ge(silu, n + 1)
                for c in range(HALF):
                    m = pe.transpose(ps[:, n % 2, c * 128:(c + 1) * 128], sl[:, n % 2, c, :, :].rearrange("p s t -> p (s t)"),
                                     t.ident[:, :])
                m.then_inc(v_ps, 1)
            pe.wait_ge(sub, SUBS)
            pe.wait_ge(conv_done, 3 * NH)
            for i in range(BASE):
                m = pe.transpose(ps[:, 2 + i // 8, (i % 8) * SYS:(i % 8 + 1) * SYS],
                                 t16[:, i, :, :].rearrange("g b j -> g (b j)"), t.ident[0:SYS, 0:SYS])
                if i % 8 == 7:
                    m.then_inc(back_ps, 1)
            pe.wait_ge(c16_ok, 1)
            for j in range(BASE):
                m = pe.transpose(ps[:, 4 + j // 8, (j % 8) * SYS:(j % 8 + 1) * SYS],
                                 c16[:, j, :, :].rearrange("g b i -> g (b i)"), t.ident[0:SYS, 0:SYS])
                if j % 8 == 7:
                    m.then_inc(back_ps, 1)

            pe.wait_ge(blocks_ok, 4)
            pe.wait_ge(v_done, NH)
            for n in range(J1):
                for k in range(G1):
                    for q, rows in enumerate(quarter):
                        m = pe.matmul(view(6 + n, BASE, G1)[rows, k, :], av[rows, G1 * n + k, 32 * (q % 2):32 * (q % 2) + 32],
                                      tn32[rows, G1 * n + k, 0:BASE], start=True, stop=True)
                m.then_inc(x_ps, 1)
            for n in range(J1):
                pe.wait_ge(x_ok, n + 1)
                for k in range(G1):
                    for rows in quarter:
                        m = pe.matmul(view(2 * n, BASE, G1)[rows, k, :], xs[n][rows, k, :],
                                      tt32[rows, G1 * n + k, BASE:W], start=True, stop=True)
                m.then_inc(y_ps, 1)
                for k in range(G1):
                    for rows in quarter:
                        m = pe.matmul(view(2 * n + 1, BASE, G1)[rows, k, :], tt32[rows, G1 * n + k, :],
                                      xs[n][rows, k, 0:BASE], start=True, stop=True)
                m.then_inc(y_ps, 1)
            for n in range(J2):
                pe.wait_ge(y_ok, 2 if n == 0 else 4)
                for k in range(G2):
                    for s in range(2):
                        m = pe.matmul(view(x2bank[n], W, G2)[quarter[2 * s + 1], k, :], av[quarter[2 * s], G2 * n + k, W:CK],
                                      tn32[quarter[2 * s], G2 * n + k, :], start=True, stop=True)
                m.then_inc(x_ps, 1)
            for n in range(J2):
                pe.wait_ge(x_ok, J1 + 2 * (n + 1))
                for k in range(G2):
                    for s in range(2):
                        m = pe.matmul(view(y2bank[n], W, G2)[quarter[2 * s], k, :], x2[n][quarter[2 * s + 1], k, :],
                                      tt32[quarter[2 * s + 1], G2 * n + k, :], start=True, stop=True)
                m.then_inc(y_ps, 1)

        @block.gpsimd
        def _(g):
            n = [0]

            def link(ins):
                n[0] += 1
                ins.then_inc(sub, 1)
                g.wait_ge(sub, n[0])

            g.memset(t16[:, :, :, :], 0.0).then_inc(unit_ok, 1)
            g.wait_ge(unit_ok, 1)
            for i in range(BASE):
                g.memset(t16[:, i, :, i:i + 1], 1.0).then_inc(unit_ok, 1)
            g.wait_ge(unit_ok, 1 + BASE)
            g.wait_ge(a16_ok, 4)
            for j in range(BASE - 1):
                r, w = BASE - 1 - j, j + 1
                o = tmp[:, 0:r * NBLK * w].rearrange("g (i b c) -> g i b c", i=r, b=NBLK)
                sh = [SYS, r, NBLK, w]
                link(g.tensor_tensor(o, bc(a16[:, j + 1:, :, j:j + 1], *sh), bc(t16[:, j:j + 1, :, 0:w], *sh), ALU.mult))
                link(g.tensor_tensor(t16[:, j + 1:, :, 0:w], t16[:, j + 1:, :, 0:w], o, ALU.subtract))
            g.wait_ge(c16_ok, 1)
            g.wait_ge(back_ps, 2)
            g.memset(second[:, 0:SYS * W], 0.0).then_inc(xs_zero, 1)
            g.wait_ge(v_ps, NH)
            g.memset(t.tt[:, :, :], 0.0).then_inc(tt_zero, 1)
            g.wait_ge(tt_zero, 1)
            g.wait_ge(y_ok, 4)
            for q, rows in enumerate(quarter):
                g.tensor_copy(t.tt[rows, :, 32 * q:32 * q + 32], tt32[rows, :, :]).then_inc(tt_done, 1)

        @block.scalar
        def _(a):
            for k in range(4):
                a.wait_ge(sel_ps, k + 1)
                a.activation(a16[:, 4 * k:4 * k + 4, :, :].rearrange("g i b j -> g (i b j)"), ps[0:SYS, k, :],
                             ACT.Copy).then_inc(a16_ok, 1)

            def start_sum(n):
                a.wait_ge(conv_ps, n + 1)
                a.activation(ac[:, n % 2, :, :], cv(n)[:, :, PAD:PAD + N], ACT.Copy,
                             scale=t.taps[:, 2 * NP + n, PAD:PAD + 1]).then_inc(conv_init, 1)

            start_sum(0)
            start_sum(1)
            for n in range(NH):
                a.wait_ge(conv_done, 3 * (n + 1))
                if n >= 2:
                    a.wait_ge(v_ps, n - 1)
                a.activation(sl[:, n % 2, :, :, :].rearrange("p c s t -> p s c t"),
                             ac[:, n % 2, :, :].rearrange("p s (c t) -> p s c t", c=HALF), ACT.Silu).then_inc(silu, 1)
                if n:
                    a.wait_ge(v_ps, n)
                    a.activation(t.v[:, :, n - 1, :], ps[:, (n - 1) % 2, :].rearrange("p (c d) -> p c d", c=HALF),
                                 ACT.Copy).then_inc(v_done, 1)
                if n + 2 < NH:
                    a.wait_ge(silu, n + 1)
                    start_sum(n + 2)
            a.wait_ge(v_ps, NH)
            a.activation(t.v[:, :, NH - 1, :], ps[:, (NH - 1) % 2, :].rearrange("p (c d) -> p c d", c=HALF),
                         ACT.Copy).then_inc(v_done, 1)
            a.wait_ge(sub, SUBS)
            a.activation(c16[:, :, :, :].rearrange("g j b i -> g i b j"), t16[:, :, :, :], ACT.Copy).then_inc(c16_ok, 1)
            a.wait_ge(xs_zero, 1)
            for n in range(J1):
                a.wait_ge(x_ps, n + 1)
                a.activation(xs[n][:, :, 0:BASE], view(6 + n, BASE, G1), ACT.Copy, scale=t.parity[:, 1:2]).then_inc(x_ok, 1)
            for n in range(J2):
                a.wait_ge(x_ps, J1 + n + 1)
                if n == J2 - 1:
                    a.wait_ge(y_ps, 2)
                for s in range(2):
                    rows = quarter[2 * s + 1]
                    a.activation(x2[n][rows, :, :], view(x2bank[n], W, G2)[rows, :, :], ACT.Copy).then_inc(x_ok, 1)

        @block.vector
        def _(v):
            for n in range(NH):
                v.wait_ge(conv_init, n + 1)
                for j in range(PAD):
                    if j:
                        v.wait_ge(conv_done, 3 * n + j)
                    v.scalar_tensor_tensor(out=ac[:, n % 2, :, :], in0=cv(n)[:, :, j:j + N],
                                           scalar=t.taps[:, 2 * NP + n, j:j + 1], in1=ac[:, n % 2, :, :],
                                           op0=ALU.mult, op1=ALU.add).then_inc(conv_done, 1)
            sh = [128, SYS, 2, 8]
            for which, dst in ((0, tt32), (1, tn32)):
                for k in range(2):
                    v.wait_ge(back_ps, 4 if which else k + 1)
                    v.tensor_tensor(
                        dst.rearrange("p g (b i) -> p g b i", b=2)[:, :, :, 8 * k:8 * k + 8] if which else
                        dst[:, :, :].rearrange("p g (b i) -> p g b i", b=2)[:, :, :, 8 * k:8 * k + 8],
                        bc(ps[:, 2 + 2 * which + k, 0:8 * SYS].rearrange("p (i g) -> p g i", i=8).unsqueeze(2), *sh),
                        bc(t.parity[:, :].unsqueeze(1).unsqueeze(3), *sh), ALU.mult).then_inc(blocks_ok, 1)
            v.wait_ge(blocks_ok, 4)
            for n in range(J1):
                gs = slice(G1 * n, G1 * (n + 1))
                v.wait_ge(y_ps, 2 * (n + 1))
                for u, d in enumerate((tt32[:, gs, BASE:W], tn32[:, gs, 0:BASE])):
                    v.tensor_tensor(d, d, view(2 * n + u, BASE, G1), ALU.subtract).then_inc(y_ok, 1)
            v.wait_ge(tt_zero, 1)
            for n in range(J2):
                v.wait_ge(y_ps, 2 * J1 + n + 1)
                for s in range(2):
                    rows = quarter[2 * s]
                    v.tensor_scalar(t.tt[rows, G2 * n:G2 * (n + 1), 64 * s + 32:64 * s + 64],
                                    view(y2bank[n], W, G2)[rows, :, :], -1.0, None, ALU.mult)
    p.close()


def scan_chunks(nc, t, half):
    p = Phase(nc, f"_{half}")
    gt = t.aa[:, :, :, :].rearrange("p c h i -> p (c h i)").rearrange("p (r z) -> p r z", r=2)
    ot = p.sb("o_tile", [128, 2, NH, DV])
    osq = p.sb("o_sq", [128, NH, DV])
    oT = p.sb("o_T", [128, NH, 128])
    ov = p.sb("o_var", [128, NH])
    yt = p.sb("y_tile", [128, HID])
    ks = [p.ps(f"ks{b}", [128, 512]) for b in range(4)]
    us = [p.ps(f"us{b}", [128, 512]) for b in range(2)]
    fl = [p.ps(f"fl{b}", [128, 512]) for b in range(2)]
    names = ("ks_ps", "r_done", "u_ps", "u_done", "o_ps", "o_done", "su_ps", "S_done",
             "g_ps", "g_done", "osq_done", "sum_done", "var_done", "rstd_done", "og_done",
             "oT_ps", "oT_done", "y_ps2", "y_done", "vch3", "on_ready")
    (ks_ps, r_done, u_ps, u_done, o_ps, o_done, su_ps, S_done, g_ps, g_done, osq_done,
     sum_done, var_done, rstd_done, og_done, oT_ps, oT_done, y_ps, y_done, vch, on_ready) = (p.sem(n) for n in names)

    def heads(ph, r):
        return [2 * (3 * ph + k) + r for k in range(G3)]

    def fillers(c):
        tr = [("t", c - 2, b) for b in range(3)] if c >= 2 else [None] * 3
        y = ("y", c - 2, 0) if c >= 2 else None
        g = [("g", c, b) for b in range(3)]
        lots = ([tr[0], tr[1]], [tr[2], g[0]], [g[1]], [y], [g[2]])
        return [[j for j in lot if j] for lot in lots]

    rest = [job for c in (HALF - 2, HALF - 1) for job in [("t", c, b) for b in range(3)] + [("y", c, 0)]]
    order = [j for c in range(HALF) for lot in fillers(c) for j in lot] + rest
    place = {job: n for n, job in enumerate(order)}
    done_of = {"g": g_done, "t": oT_done, "y": y_done}

    def index(job):
        kind, c, b = job
        return c * (1 if kind == "y" else 3) + b

    def bank_of(job):
        return fl[place[job] % 2]

    with nc.Block() as block:
        @block.tensor
        def _(pe):
            def filler(job):
                kind, c, b = job
                if place[job] >= 2:
                    old = order[place[job] - 2]
                    pe.wait_ge(done_of[old[0]], index(old) + 1)
                o = bank_of(job)
                if kind == "g":
                    pe.matmul(o[:, :], t.hS[:, half * HALF + c, :], t.wg[:, b * 512:(b + 1) * 512],
                              start=True, stop=True).then_inc(g_ps, 1)
                elif kind == "t":
                    pe.wait_ge(og_done, c + 1)
                    for k in range(4):
                        m = pe.transpose(o[:, k * 128:(k + 1) * 128], ot[:, c % 2, 4 * b + k, :], t.ident[:, :])
                    m.then_inc(oT_ps, 1)
                else:
                    pe.wait_ge(oT_done, 3 * (c + 1))
                    for h in range(NH):
                        m = pe.matmul(o[:, 0:HID], oT[:, h, :], t.wo[:, h, :], start=h == 0, stop=h == NH - 1)
                    m.then_inc(y_ps, 1)

            def state_products(c, ph):
                n = 2 * c + ph
                if c:
                    pe.wait_ge(S_done, 2 * (c - 1) + ph + 1)
                    pe.wait_ge(o_done, 4 * (c - 1) + 2 * ph + 2)
                for r in range(2):
                    rows = slice(r * 64, (r + 1) * 64)
                    for k in range(G3):
                        for s in range(2):
                            cs = slice(s * CK, (s + 1) * CK)
                            m = pe.matmul(ks[2 * ph + r][cs, k * DV:(k + 1) * DV], t.kqT[rows, c, 3 * ph + k, 0, cs],
                                          t.S[rows, s, 3 * ph + k, :], start=True, stop=True)
                    m.then_inc(ks_ps, 1)

            def solve(c, ph):
                n = 2 * c + ph
                if ph:
                    pe.wait_ge(u_done, 4 * c + 2)
                elif c:
                    pe.wait_ge(S_done, 2 * c)
                for r in range(2):
                    pe.wait_ge(r_done, 2 * n + r + 1)
                    for k, h in enumerate(heads(ph, r)):
                        m = pe.matmul(us[r][:, k * DV:(k + 1) * DV], t.tt[:, c * NH + h, :], t.v[:, c, h, :],
                                      start=True, stop=True)
                    m.then_inc(u_ps, 1)

            def outputs(c, ph):
                for r in range(2):
                    rows = slice(r * 64, (r + 1) * 64)
                    pe.wait_ge(u_done, 4 * c + 2 * ph + r + 1)
                    for k, h in enumerate(heads(ph, r)):
                        for s in range(2):
                            cs = slice(s * CK, (s + 1) * CK)
                            m = pe.matmul(ks[2 * ph + r][cs, k * DV:(k + 1) * DV], t.kqT[rows, c, 3 * ph + k, 1, cs],
                                          t.S[rows, s, 3 * ph + k, :], start=k == 0, stop=False, skip_group_check=True)
                    for k, h in enumerate(heads(ph, r)):
                        m = pe.matmul(ks[2 * ph + r][:, k * DV:(k + 1) * DV], t.pp[:, c, h, :], t.v[:, c, h, :],
                                      start=False, stop=k == G3 - 1, skip_group_check=True)
                    m.then_inc(o_ps, 1)

            def updates(c, ph):
                pe.wait_ge(u_done, 4 * c + 4)
                if ph:
                    pe.wait_ge(S_done, 2 * c + 1)
                for s in range(2):
                    cs = slice(s * CK, (s + 1) * CK)
                    for k in range(G3):
                        for r in range(2):
                            h = 2 * (3 * ph + k) + r
                            m = pe.matmul(us[s][r * 64:(r + 1) * 64, k * DV:(k + 1) * DV], t.kd[cs, c, h * DK:(h + 1) * DK],
                                          t.v[cs, c, h, :], start=True, stop=True)
                m.then_inc(su_ps, 1)

            for c in range(HALF):
                cut = fillers(c)
                state_products(c, 0)
                state_products(c, 1)
                for j in cut[0]:
                    filler(j)
                solve(c, 0)
                for j in cut[1]:
                    filler(j)
                solve(c, 1)
                for j in cut[2]:
                    filler(j)
                outputs(c, 0)
                updates(c, 0)
                for j in cut[3]:
                    filler(j)
                outputs(c, 1)
                updates(c, 1)
                for j in cut[4]:
                    filler(j)
            for j in rest:
                filler(j)

        @block.scalar
        def _(a):
            def copy_filler(job):
                kind, c, b = job
                if kind == "g":
                    if c >= 2 and b == 0:
                        a.wait_ge(og_done, c - 1)
                    a.wait_ge(g_ps, 3 * c + b + 1)
                    a.activation(gt[:, c % 2, b * 512:(b + 1) * 512], bank_of(job)[:, :], ACT.Silu).then_inc(g_done, 1)
                elif kind == "t":
                    if c and b == 0:
                        a.wait_ge(y_ps, c)
                    a.wait_ge(oT_ps, 3 * c + b + 1)
                    a.activation(oT[:, 4 * b:4 * b + 4, :].rearrange("p h d -> p (h d)"), bank_of(job)[:, :],
                                 ACT.Copy).then_inc(oT_done, 1)

            def copy_u(c, ph):
                for r in range(2):
                    a.wait_ge(u_ps, 4 * c + 2 * ph + r + 1)
                    a.activation(t.v[:, c, 6 * ph + r:6 * ph + r + 5:2, :], us[r][:, 0:G3 * DV].rearrange("p (h d) -> p h d", h=G3),
                                 ACT.Copy).then_inc(u_done, 1)

            def copy_o(c, ph):
                if c >= 2 and ph == 0:
                    a.wait_ge(oT_ps, 3 * (c - 1))
                for r in range(2):
                    a.wait_ge(o_ps, 4 * c + 2 * ph + r + 1)
                    a.activation(ot[:, c % 2, 6 * ph + r:6 * ph + r + 5:2, :],
                                 ks[2 * ph + r][:, 0:G3 * DV].rearrange("p (h d) -> p h d", h=G3), ACT.Copy).then_inc(o_done, 1)

            for c in range(HALF):
                cut = fillers(c)
                for j in cut[0]:
                    copy_filler(j)
                copy_u(c, 0)
                for j in cut[1]:
                    copy_filler(j)
                copy_u(c, 1)
                for j in cut[2]:
                    copy_filler(j)
                copy_o(c, 0)
                for j in cut[3]:
                    copy_filler(j)
                copy_o(c, 1)
                for j in cut[4]:
                    copy_filler(j)
            for j in rest:
                copy_filler(j)

        @block.gpsimd
        def _(g):
            for c in range(HALF):
                for ph in range(2):
                    g.wait_ge(o_done, 4 * c + 2 * ph + 2)
                    if c:
                        g.wait_ge(sum_done, c)
                    hs = slice(6 * ph, 6 * ph + 6)
                    g.tensor_tensor(osq[:, hs, :], ot[:, c % 2, hs, :], ot[:, c % 2, hs, :], ALU.mult).then_inc(osq_done, 1)
                g.wait_ge(var_done, c + 1)
                g.tensor_tensor(ov[:, :], ov[:, :], t.mhalf[:, 0:NH], ALU.pow).then_inc(rstd_done, 1)
                g.wait_ge(rstd_done, c + 1)
                g.tensor_tensor(ot[:, c % 2, :, :], ot[:, c % 2, :, :], bc(ov[:, :].unsqueeze(2), 128, NH, DV),
                                ALU.mult).then_inc(on_ready, 1)

        @block.vector
        def _(v):
            link = linker(v, vch)

            def residuals(c, ph):
                for r in range(2):
                    v.wait_ge(ks_ps, 4 * c + 2 * ph + r + 1)
                    for k, h in enumerate(heads(ph, r)):
                        m = v.scalar_tensor_tensor(out=t.v[:, c, h, :], in0=ks[2 * ph + r][:, k * DV:(k + 1) * DV],
                                                   scalar=t.nGam[:, half * HALF + c, h:h + 1], in1=t.v[:, c, h, :],
                                                   op0=ALU.mult, op1=ALU.add)
                    m.then_inc(r_done, 1)

            def new_state(c, ph):
                v.wait_ge(o_ps, 4 * c + 2 * ph + 2)
                v.wait_ge(su_ps, 2 * c + ph + 1)
                for s in range(2):
                    for k in range(G3):
                        q = 3 * ph + k
                        m = v.scalar_tensor_tensor(out=t.S[:, s, q, :], in0=t.S[:, s, q, :],
                                                   scalar=t.gam_all[:, half * HALF + c, s, q:q + 1],
                                                   in1=us[s][:, k * DV:(k + 1) * DV], op0=ALU.mult, op1=ALU.add)
                m.then_inc(S_done, 1)

            def variances(c):
                if c:
                    v.wait_ge(on_ready, c)
                v.wait_ge(osq_done, 2 * c + 2)
                v.tensor_reduce(ov[:, :], osq[:, :, :], AX, ALU.add).then_inc(sum_done, 1)
                v.wait_ge(sum_done, c + 1)
                v.tensor_scalar(ov[:, :], ov[:, :], 1.0 / DV, 1e-5, ALU.mult, ALU.add).then_inc(var_done, 1)

            def gate(c):
                v.wait_ge(on_ready, c + 1)
                v.wait_ge(g_done, 3 * (c + 1))
                o = ot[:, c % 2, :, :].rearrange("p h d -> p (h d)")
                v.tensor_tensor(o, o, gt[:, c % 2, :], ALU.mult).then_inc(og_done, 1)

            def project(c):
                v.wait_ge(y_ps, c + 1)
                link(v.tensor_tensor(yt[:, :], bank_of(("y", c, 0))[:, 0:HID], t.modbc[:, 2 * HID:3 * HID], ALU.mult))
                v.tensor_tensor(t.x[:, half * HALF + c, :], t.x[:, half * HALF + c, :], yt[:, :], ALU.add).then_inc(y_done, 1)

            for c in range(HALF):
                residuals(c, 0)
                residuals(c, 1)
                if c:
                    variances(c - 1)
                new_state(c, 0)
                new_state(c, 1)
                if c:
                    gate(c - 1)
                if c >= 2:
                    project(c - 2)
            variances(HALF - 1)
            gate(HALF - 1)
            project(HALF - 2)
            project(HALF - 1)
    p.close()


def second_norm(nc, t):
    p = Phase(nc)
    sq, st = p.sb("sq_b", [128, TILES, HID]), p.sb("st_b", [128, 3, TILES])
    hn = p.sb("h_rms", [128, TILES, HID])
    ps = p.ps("ps_b1", [128, 2, 512])
    vch, pow_in, pow_out, hn_ok, hT_ps, hT_ok = (p.sem(n) for n in ("vch_b", "pow_in_b", "pow_out_b", "hn_ok", "h1T_ps", "h1T_ok"))
    with nc.Block() as block:
        @block.gpsimd
        def _(g):
            for k in range(2):
                g.wait_ge(pow_in, k + 1)
                g.tensor_tensor(st[:, 1 + k, :], st[:, 1 + k, :], t.mhalf[:, 0:TILES], ALU.pow).then_inc(pow_out, 1)

        @block.vector
        def _(v):
            link = linker(v, vch)
            sh = [128, TILES, HID]
            h = t.hf
            link(v.tensor_reduce(st[:, 0, :], t.x[:, :, :], AX, ALU.add))
            link(v.tensor_scalar(st[:, 0, :], st[:, 0, :], 1.0 / HID, None, ALU.mult))
            link(v.tensor_tensor(h[:, :, :], t.x[:, :, :], bc(st[:, 0, :].unsqueeze(2), *sh), ALU.subtract))
            link(v.tensor_tensor(sq[:, :, :], h[:, :, :], h[:, :, :], ALU.mult))
            link(v.tensor_reduce(st[:, 1, :], sq[:, :, :], AX, ALU.add))
            v.tensor_scalar(st[:, 1, :], st[:, 1, :], 1.0 / HID, 1e-5, ALU.mult, ALU.add).then_inc(pow_in, 1)
            v.wait_ge(pow_out, 1)
            link(v.tensor_tensor(h[:, :, :], h[:, :, :], bc(st[:, 1, :].unsqueeze(2), *sh), ALU.mult))
            link(v.tensor_tensor(h[:, :, :], h[:, :, :], bc(t.modbc[:, 4 * HID:5 * HID].unsqueeze(1), *sh), ALU.mult))
            link(v.tensor_tensor(h[:, :, :], h[:, :, :], bc(t.modbc[:, 3 * HID:4 * HID].unsqueeze(1), *sh), ALU.add))
            link(v.tensor_tensor(sq[:, :, :], h[:, :, :], h[:, :, :], ALU.mult))
            link(v.tensor_reduce(st[:, 2, :], sq[:, :, :], AX, ALU.add))
            v.tensor_scalar(st[:, 2, :], st[:, 2, :], 1.0 / HID, 1e-6, ALU.mult, ALU.add).then_inc(pow_in, 1)
            v.wait_ge(pow_out, 2)
            v.tensor_tensor(hn[:, :, :], h[:, :, :], bc(st[:, 2, :].unsqueeze(2), *sh), ALU.mult).then_inc(hn_ok, 1)

        @block.tensor
        def _(pe):
            pe.wait_ge(hn_ok, 1)
            for c in range(TILES):
                m = pe.transpose(ps[:, c // 4, (c % 4) * 128:(c % 4 + 1) * 128], hn[:, c, :], t.ident[:, :])
                if c % 4 == 3:
                    m.then_inc(hT_ps, 1)

        @block.scalar
        def _(a):
            for b in range(2):
                a.wait_ge(hT_ps, b + 1)
                a.activation(t.h1T[:, :, 256 * b:256 * (b + 1)].rearrange("p s (c t) -> p c s t", c=4),
                             ps[:, b, :].rearrange("p (c s t) -> p c s t", c=4, s=2), ACT.Copy,
                             scale=t.n1w[:, 0:1]).then_inc(hT_ok, 1)
    p.close()


Q_EIGHTS = (slice(0, 3), slice(3, 5), slice(6, 7))
K_EIGHTS = (slice(0, 7, 3), slice(1, 5, 3), slice(2, 3))
MAX_AT = 40
UNITS = TQ * AH


class RowMaximum:

    def __init__(self, p, t, s, banks, trs):
        self.t, self.s, self.sc, self.tb = t, s, banks, trs
        self.mx = p.sb("row_max", [128, TQ * AH])
        self.mr = p.sb("max_rest", [128, TQ * AH])
        self.sc_ps, self.max_ok, self.neg_ok, self.again_ps, self.again_ok, self.vch = (p.sem(n) for n in (
            "sc_ps", "max_ok", "neg_ok", "again_ps", "again_ok", "vch_max"))

    def scores(self, pe, n):
        t, s, ring = self.t, self.s, len(self.sc)
        q, h = divmod(n, AH)
        if n >= ring:
            pe.wait_ge(self.max_ok, n - ring + 1)
        rows = slice(64 * (h % 2), 64 * (h % 2) + 64)
        pe.matmul(self.sc[n % ring][:, :], t.qT[rows, s, h // 2, q * 128:(q + 1) * 128], t.kT[rows, s, h // 2, :],
                  start=True, stop=True).then_inc(self.sc_ps, 1)

    def largest(self, v, n):
        v.wait_ge(self.sc_ps, n + 1)
        v.tensor_reduce(self.mx[:, n:n + 1], self.sc[n % len(self.sc)][:, :], AX, ALU.max).then_inc(self.max_ok, 1)

    def into_queries(self, v):
        link = linker(v, self.vch)
        q = self.t.qs[:, self.s, :, :]
        v.wait_ge(self.max_ok, UNITS)
        link(v.tensor_scalar(self.mx[:, :], self.mx[:, :], -1.0, None, ALU.mult))
        link(v.tensor_copy(q[:, :, MAX_AT], self.mx[:, :]))
        link(v.tensor_tensor(self.mr[:, :], self.mx[:, :], q[:, :, MAX_AT], ALU.subtract))
        link(v.tensor_copy(q[:, :, MAX_AT + 1], self.mr[:, :]))
        link(v.tensor_tensor(self.mr[:, :], self.mr[:, :], q[:, :, MAX_AT + 1], ALU.subtract))
        v.tensor_copy(q[:, :, MAX_AT + 2], self.mr[:, :]).then_inc(self.neg_ok, 1)

    def transpose_again(self, pe):
        pe.wait_ge(self.neg_ok, 1)
        wv = self.t.qs[:, self.s, :, :].rearrange("p g z -> p (g z)")
        for q in range(TQ):
            if q >= 2:
                pe.wait_ge(self.again_ok, q - 1)
            for b in range(8):
                m = pe.transpose(self.tb[q % 2][:, b, :], wv[:, (8 * q + b) * 128:(8 * q + b + 1) * 128], self.t.identb[:, :])
            m.then_inc(self.again_ps, 1)

    def copy_again(self, a, q):
        a.wait_ge(self.again_ps, q + 1)
        a.activation(self.t.qT[:, self.s, :, q * 128:(q + 1) * 128], self.tb[q % 2][:, :, :], ACT.Copy).then_inc(self.again_ok, 1)


def attention_scores(nc, t):
    p = Phase(nc)
    kx = p.sb("k_slots", [128, 2, TQ * AH, SLOT], BF16)
    x = p.sb("qk_f32", [128, 2, 2, TQ * HID])
    re = p.sb("qk_rest", [128, 2, TQ * HID])
    bank = [p.ps(f"att_ps{b}", [128, 512]) for b in range(6)]
    tb = [p.ps(f"tr_ps{b}", [128, 8, 128], BF16) for b in range(2)]
    (init, qkv_ps, x_ok, va_ok, hi_ok, mid_ok, slots_ok, tr_ps, tr_ok, vch) = (p.sem(n) for n in (
        "slots_init", "qkv_ps", "x_ok", "va_ok", "hi_ok", "mid_ok", "slots_ok", "tr_ps", "tr_ok", "vch_s"))
    largest = RowMaximum(p, t, 0, bank[0:3], tb)
    side = [(s, w) for s in range(2) for w in range(2)]
    eights = lambda s, w: (t.qs, kx)[w][:, s, :, :].rearrange("p g (k d) -> p g k d", d=AD)
    groups = lambda ap: ap.rearrange("p (g d) -> p g d", d=AD)

    def spread(ap, s, w, m):
        o = eights(s, w)[:, :, (Q_EIGHTS, K_EIGHTS)[w][m], :]
        return o, bc(groups(ap).unsqueeze(2), 128, TQ * AH, (3, 2, 1)[m], AD)

    trs = [(s, w, q) for s, w in side for q in range(TQ)]
    with nc.Block() as block:
        @block.gpsimd
        def _(g):
            for s, w in side:
                e = eights(s, w)
                g.memset(e[:, :, 5:8:2, :], 0.0).then_inc(init, 1)
            g.memset(t.va[:, :, :, :, AD:32], 1.0).then_inc(init, 1)
            g.wait_ge(init, 5)
            for s in range(2):
                g.memset(kx[:, s, :, MAX_AT:MAX_AT + 3], 1.0).then_inc(init, 1)

        @block.tensor
        def _(pe):
            for s in range(2):
                for m in range(3):
                    for q in range(TQ):
                        last = pe.matmul(bank[3 * s + m][:, q * HID:(q + 1) * HID], t.h1T[:, s, q * 128:(q + 1) * 128],
                                         t.wqkv[:, m * HID:(m + 1) * HID], start=True, stop=True)
                    last.then_inc(qkv_ps, 1)
            pe.wait_ge(init, 7)
            for n, (s, w, q) in enumerate(trs):
                pe.wait_ge(slots_ok, 2 * s + w + 1)
                if n >= 2:
                    pe.wait_ge(tr_ok, n - 1)
                wv = (t.qs, kx)[w][:, s, :, :].rearrange("p g z -> p (g z)")
                for b in range(8):
                    m = pe.transpose(tb[n % 2][:, b, :], wv[:, (8 * q + b) * 128:(8 * q + b + 1) * 128], t.identb[:, :])
                m.then_inc(tr_ps, 1)
                if n == 2 * TQ - 1:
                    pe.wait_ge(tr_ok, 2 * TQ)
                    pe.wait_ge(x_ok, 2)
                    pe.wait_ge(va_ok, 1)
                if n >= 2 * TQ:
                    for k in range(8):
                        largest.scores(pe, 8 * (n - 2 * TQ) + k)
            pe.wait_ge(tr_ok, 4 * TQ)
            largest.transpose_again(pe)

        @block.scalar
        def _(a):
            def ready(s, w):
                a.wait_ge(qkv_ps, 3 * s + w + 1)
                a.activation(x[:, s, w, :], bank[3 * s + w][:, :], ACT.Copy, scale=1.0 if w else AD ** -0.5).then_inc(x_ok, 1)
                a.wait_ge(x_ok, 2 * s + w + 1)
                a.activation(*spread(x[:, s, w, :], s, w, 0), ACT.Copy).then_inc(hi_ok, 1)

            def values(s):
                a.wait_ge(qkv_ps, 3 * s + 3)
                a.activation(t.va[:, s, :, :, 0:AD].rearrange("p q h d -> p (q h) d"), groups(bank[3 * s + 2][:, :]),
                             ACT.Copy).then_inc(va_ok, 1)

            def transposed(n):
                s, w, q = trs[n]
                a.wait_ge(tr_ps, n + 1)
                a.activation((t.qT, t.kT)[w][:, s, :, q * 128:(q + 1) * 128], tb[n % 2][:, :, :], ACT.Copy).then_inc(tr_ok, 1)

            ready(0, 0)
            ready(0, 1)
            values(0)
            for n in range(TQ):
                transposed(n)
            ready(1, 0)
            for n in range(TQ, 2 * TQ):
                transposed(n)
            ready(1, 1)
            values(1)
            for n in range(2 * TQ, 4 * TQ):
                transposed(n)
            for q in range(TQ):
                largest.copy_again(a, q)

        @block.vector
        def _(v):
            link = linker(v, vch)

            def parts(s, w):
                X, r = x[:, s, w, :], re[:, w, :]
                e = eights(s, w)
                hi, mid = (e[:, :, (Q_EIGHTS, K_EIGHTS)[w][m].start, :] for m in range(2))
                v.wait_ge(hi_ok, 2 * s + w + 1)
                link(v.tensor_tensor(groups(r), groups(X), hi, ALU.subtract))
                link(v.tensor_copy(*spread(r, s, w, 1)))
                link(v.tensor_tensor(groups(r), groups(r), mid, ALU.subtract))
                v.tensor_copy(*spread(r, s, w, 2)).then_inc(slots_ok, 1)

            parts(0, 0)
            parts(0, 1)
            v.wait_ge(slots_ok, 2)
            parts(1, 0)
            parts(1, 1)
            for n in range(UNITS):
                largest.largest(v, n)
            largest.into_queries(v)
    p.close()


def attention_values(nc, t, s):
    p = Phase(nc, f"_{s}")
    pt = p.sb("probs", [128, 2, 4, TQ, 512])
    other = 1 if s == 0 else None
    RING = 2 if s == 0 else 3
    sc = [p.ps(f"sT_ps{b}", [128, 2, 512]) for b in range(RING)]
    cx = [p.ps(f"ctx_ps{b}", [128, 512]) for b in range(2)]
    sc_ps, exp_ok, cx_ps, cx_ok = (p.sem(n) for n in ("sT_ps", "exp_ok", "ctx_ps", "ctx_ok"))
    GROUPS = AH // 4
    if other:
        mb = [p.ps(f"max_ps{b}", [128, 512]) for b in range(2)]
        tb = [sc[b][:, 0, :].bitcast(BF16).rearrange("p (b z) -> p b z", b=8) for b in range(2)]
        largest = RowMaximum(p, t, other, mb, tb)
    PER = UNITS // (8 * GROUPS)
    with nc.Block() as block:
        @block.tensor
        def _(pe):
            def scores(g):
                for j in range(4):
                    h = 4 * g + j
                    rows = slice(64 * (h % 2), 64 * (h % 2) + 64)
                    for u in range(2):
                        n = 8 * g + 2 * j + u
                        if n >= RING:
                            pe.wait_ge(exp_ok, n - RING + 1)
                        for k in range(2):
                            tb = 2 * u + k
                            m = pe.matmul(sc[n % RING][:, k, :], t.kT[rows, s, h // 2, tb * 128:(tb + 1) * 128],
                                          t.qT[rows, s, h // 2, :], start=True, stop=True)
                        m.then_inc(sc_ps, 1)
                        if other:
                            for k in range(PER):
                                largest.scores(pe, PER * n + k)

            def values(g):
                pe.wait_ge(exp_ok, 8 * (g + 1))
                if g >= 2:
                    pe.wait_ge(cx_ok, g - 1)
                for tb in range(TQ):
                    for j in range(4):
                        m = pe.matmul(cx[g % 2][32 * j:32 * j + 32, :], t.va[:, s, tb, 4 * g + j, :], pt[:, g % 2, j, tb, :],
                                      start=tb == 0, stop=tb == TQ - 1)
                m.then_inc(cx_ps, 1)

            scores(0)
            for g in range(GROUPS):
                if g + 1 < GROUPS:
                    scores(g + 1)
                values(g)
            if other:
                largest.transpose_again(pe)

        @block.scalar
        def _(a):
            for g in range(GROUPS):
                if g >= 2:
                    a.wait_ge(cx_ps, g - 1)
                for j in range(4):
                    for u in range(2):
                        n = 8 * g + 2 * j + u
                        a.wait_ge(sc_ps, n + 1)
                        a.activation(pt[:, g % 2, j, 2 * u:2 * u + 2, :], sc[n % RING][:, :, :], ACT.Exp).then_inc(exp_ok, 1)
            if other:
                for q in range(TQ):
                    largest.copy_again(a, q)

        @block.vector
        def _(v):
            def context(g):
                v.wait_ge(cx_ps, g + 1)
                v.tensor_copy(t.cx[:, g, :, s, :], cx[g % 2][:, :].rearrange("p (c t) -> p c t", c=TILES)).then_inc(cx_ok, 1)

            for g in range(GROUPS):
                if other:
                    for n in range(8 * PER * g, 8 * PER * (g + 1)):
                        largest.largest(v, n)
                if g >= 2:
                    context(g - 2)
            context(GROUPS - 2)
            if other:
                largest.into_queries(v)
            context(GROUPS - 1)
    p.close()


def attention_output(nc, t, src):
    p = Phase(nc)
    rc = p.sb("rec_sum", [128, TILES, AH])
    cn = p.sb("ctx_n", [128, TILES, AH, AD])
    cT = p.sb("ctx_nT", [128, TILES, 128])
    sq, st, hn = p.sb("sq_c", [128, TILES, HID]), p.sb("st_c", [128, TILES]), p.sb("h2_rms", [128, TILES, HID])
    lg, eq, oh1, oh2 = (p.sb(n, [128, TILES, NE]) for n in ("logits", "eq", "first", "second"))
    sm = p.sb("route_st", [128, 6, TILES])
    ps = p.ps("ps_c", [128, 8, 512])
    (vch, cx_ps, cn_ok, cT_ps, cT_ok, y_ps, pow_in, pow_out, hn_ok, h2_ps, h2_ok, lg_ps, ex_in, ex_ok) = (p.sem(n) for n in (
        "vch_c", "cxT_ps", "cn_ok", "cT_ps_c", "cT_ok", "y_ps_c", "pow_in_c", "pow_out_c", "hn_ok_c", "h2T_ps", "h2T_ok",
        "lg_ps", "ex_in", "ex_ok"))
    wl = p.sem("moe_weights")
    with nc.Block() as block:
        @block.sync
        def _(sp):
            for m, (one, many) in enumerate((("L0_ffn_sh_gate", "L0_ffn_e_gate"), ("L0_ffn_sh_up", "L0_ffn_e_up"))):
                sp.dma_start(t.wgu[:, NE, m, :], src[one]).then_inc(wl, 16)
                sp.dma_start(t.wgu[:, 0:NE, m, :], src[many].rearrange("e d f -> d e f")).then_inc(wl, 16)
            sp.dma_start(t.wdn[:, NE, :, :], src["L0_ffn_sh_down"].rearrange("(b f) d -> f b d", b=2)).then_inc(wl, 16)
            for b in range(2):
                sp.dma_start(t.wdn[:, 0:NE, b, :], src["L0_ffn_e_down"][:, 128 * b:128 * (b + 1), :]
                             .rearrange("e f d -> f e d")).then_inc(wl, 16)
            sp.wait_ge(wl, 16 * 7)

        @block.tensor
        def _(pe):
            for c in range(TILES):
                if c >= 4:
                    pe.wait_ge(cn_ok, c - 3)
                for g in range(4):
                    m = pe.transpose(ps[:, c % 4, g * 128:(g + 1) * 128], t.cx[:, g, c, :, :].rearrange("p s t -> p (s t)"), t.ident[:, :])
                m.then_inc(cx_ps, 1)
            for c in range(TILES):
                pe.wait_ge(cn_ok, c + 1)
                m = pe.transpose(ps[:, 4 + c // 4, (c % 4) * 128:(c % 4 + 1) * 128],
                                 cn[:, c, :, :].rearrange("p h d -> p (h d)"), t.ident[:, :])
                if c % 4 == 3:
                    m.then_inc(cT_ps, 1)
            pe.wait_ge(cT_ok, 2)
            for c in range(TILES):
                m = pe.matmul(ps[:, 6 + c // 4, (c % 4) * 128:(c % 4 + 1) * 128], cT[:, c, :], t.wo2[:, :],
                              start=True, stop=True)
                if c % 4 == 3:
                    m.then_inc(y_ps, 1)
            pe.wait_ge(hn_ok, 1)
            for c in range(TILES):
                m = pe.transpose(ps[:, c // 4, (c % 4) * 128:(c % 4 + 1) * 128], hn[:, c, :], t.ident[:, :])
                if c % 4 == 3:
                    m.then_inc(h2_ps, 1)
            pe.wait_ge(h2_ok, 2)
            for c in range(TILES):
                m = pe.matmul(ps[:, 2, c * NE:(c + 1) * NE], t.h2T[:, c * 128:(c + 1) * 128], t.wr[:, :],
                              start=True, stop=True)
            m.then_inc(lg_ps, 1)

        @block.scalar
        def _(a):
            for b in range(2):
                a.wait_ge(cT_ps, b + 1)
                a.activation(cT[:, 4 * b:4 * b + 4, :].rearrange("p c i -> p (c i)"), ps[:, 4 + b, :], ACT.Copy).then_inc(cT_ok, 1)
            for b in range(2):
                a.wait_ge(h2_ps, b + 1)
                a.activation(t.h2T[:, 512 * b:512 * (b + 1)], ps[:, b, :], ACT.Copy, scale=t.n2w[:, 0:1]).then_inc(h2_ok, 1)
            for k, x in ((0, lg[:, :, :]), (1, sm[:, 3, :])):
                a.wait_ge(ex_in, k + 1)
                a.activation(x, x, ACT.Exp).then_inc(ex_ok, 1)

        @block.gpsimd
        def _(g):
            g.wait_ge(pow_in, 1)
            g.tensor_tensor(st[:, :], st[:, :], t.mhalf[:, 0:TILES], ALU.pow).then_inc(pow_out, 1)

        @block.vector
        def _(v):
            link = linker(v, vch)
            for c in range(TILES):
                v.wait_ge(cx_ps, c + 1)
                z = ps[:, c % 4, :].rearrange("p (h z) -> p h z", h=AH)
                link(v.reciprocal(rc[:, c, :], z[:, :, AD]))
                v.tensor_tensor(cn[:, c, :, :], z[:, :, 0:AD], bc(rc[:, c, :].unsqueeze(2), 128, AH, AD),
                                ALU.mult).then_inc(cn_ok, 1)
            for b in range(2):
                v.wait_ge(y_ps, b + 1)
                h = t.hf[:, 4 * b:4 * b + 4, :].rearrange("p c d -> p (c d)")
                link(v.tensor_tensor(h, h, ps[:, 6 + b, :], ALU.add))
            sh = [128, TILES, HID]
            link(v.tensor_tensor(sq[:, :, :], t.hf[:, :, :], t.hf[:, :, :], ALU.mult))
            link(v.tensor_reduce(st[:, :], sq[:, :, :], AX, ALU.add))
            v.tensor_scalar(st[:, :], st[:, :], 1.0 / HID, 1e-6, ALU.mult, ALU.add).then_inc(pow_in, 1)
            v.wait_ge(pow_out, 1)
            v.tensor_tensor(hn[:, :, :], t.hf[:, :, :], bc(st[:, :].unsqueeze(2), *sh), ALU.mult).then_inc(hn_ok, 1)
            se = [128, TILES, NE]
            up = lambda x: bc(x.unsqueeze(2), *se)
            v.wait_ge(lg_ps, 1)
            link(v.tensor_copy(lg[:, :, :], ps[:, 2, 0:TILES * NE].rearrange("p (c e) -> p c e", e=NE)))
            link(v.tensor_reduce(sm[:, 0, :], lg[:, :, :], AX, ALU.max))
            v.tensor_tensor(lg[:, :, :], lg[:, :, :], up(sm[:, 0, :]), ALU.subtract).then_inc(ex_in, 1)
            v.wait_ge(ex_ok, 1)
            link(v.tensor_reduce(sm[:, 1, :], lg[:, :, :], AX, ALU.add))
            link(v.reciprocal(sm[:, 1, :], sm[:, 1, :]))
            link(v.tensor_tensor(lg[:, :, :], lg[:, :, :], up(sm[:, 1, :]), ALU.mult))
            for k, oh in enumerate((oh1, oh2)):
                link(v.tensor_reduce(sm[:, 2 + k, :], lg[:, :, :], AX, ALU.max))
                link(v.tensor_tensor(eq[:, :, :], lg[:, :, :], up(sm[:, 2 + k, :]), ALU.is_equal))
                link(v.tensor_tensor(eq[:, :, :], eq[:, :, :], bc(t.rank[:, :].unsqueeze(1), *se), ALU.mult))
                link(v.tensor_reduce(sm[:, 4, :], eq[:, :, :], AX, ALU.max))
                link(v.tensor_tensor(oh[:, :, :], eq[:, :, :], up(sm[:, 4, :]), ALU.is_equal))
                if k == 0:
                    link(v.scalar_tensor_tensor(out=lg[:, :, :], in0=oh[:, :, :], scalar=-2.0, in1=lg[:, :, :],
                                                op0=ALU.mult, op1=ALU.add))
            v.tensor_tensor(sm[:, 3, :], sm[:, 3, :], sm[:, 2, :], ALU.subtract).then_inc(ex_in, 1)
            v.wait_ge(ex_ok, 2)
            link(v.tensor_scalar(sm[:, 4, :], sm[:, 3, :], 1.0, None, ALU.add))
            link(v.reciprocal(sm[:, 4, :], sm[:, 4, :]))
            link(v.tensor_tensor(sm[:, 5, :], sm[:, 3, :], sm[:, 4, :], ALU.mult))
            link(v.tensor_tensor(oh1[:, :, :], oh1[:, :, :], up(sm[:, 4, :]), ALU.mult))
            link(v.tensor_tensor(oh2[:, :, :], oh2[:, :, :], up(sm[:, 5, :]), ALU.mult))
            link(v.tensor_tensor(t.comb[:, :, :], oh1[:, :, :], oh2[:, :, :], ALU.add))
    p.close()


def experts(nc, t, out, i):
    p = Phase(nc)
    sg = p.sb("gate_silu", [128, 2, 512])
    hid = p.sb("hidden", [128, 2, 2, 512])
    gp = [p.ps(f"gate_ps{b}", [128, 512]) for b in range(3)]
    up = [p.ps(f"up_ps{b}", [128, 512]) for b in range(3)]
    dn = [p.ps(f"down_ps{b}", [128, 512]) for b in range(2)]
    vch, gu_ps, sg_ok, hid_ok, dn_ps, dn_ok, out_ok, stored = (p.sem(n) for n in (
        "vch_m", "gu_ps", "sg_ok", "hid_ok", "dn_ps", "dn_ok", "out_ok", "stored"))
    jobs = [(e, b) for e in range(NE, -1, -1) for b in range(2)]
    with nc.Block() as block:
        @block.tensor
        def _(pe):
            def gate_up(n):
                e, b = jobs[n]
                for f in range(2):
                    k = 2 * n + f
                    if k >= 3:
                        pe.wait_ge(hid_ok, k - 2)
                    pe.matmul(gp[k % 3][:, :], t.wgu[:, e, 0, f * 128:(f + 1) * 128], t.h2T[:, b * 512:(b + 1) * 512],
                              start=True, stop=True)
                    pe.matmul(up[k % 3][:, :], t.wgu[:, e, 1, f * 128:(f + 1) * 128], t.h2T[:, b * 512:(b + 1) * 512],
                              start=True, stop=True).then_inc(gu_ps, 1)

            def down(n):
                e, b = jobs[n]
                pe.wait_ge(hid_ok, 2 * n + 2)
                if n >= 2:
                    pe.wait_ge(dn_ok, 4 * (n - 1))
                for c in range(4):
                    for f in range(2):
                        m = pe.matmul(dn[n % 2][:, c * 128:(c + 1) * 128], hid[:, n % 2, f, c * 128:(c + 1) * 128],
                                      t.wdn[:, e, f, :], start=f == 0, stop=f == 1)
                m.then_inc(dn_ps, 1)

            gate_up(0)
            for n in range(len(jobs)):
                if n + 1 < len(jobs):
                    gate_up(n + 1)
                down(n)

        @block.scalar
        def _(a):
            for k in range(2 * len(jobs)):
                a.wait_ge(gu_ps, k + 1)
                if k >= 2:
                    a.wait_ge(hid_ok, k - 1)
                a.activation(sg[:, k % 2, :], gp[k % 3][:, :], ACT.Silu).then_inc(sg_ok, 1)

        @block.vector
        def _(v):
            link = linker(v, vch)

            def hidden(n):
                for f in range(2):
                    k = 2 * n + f
                    v.wait_ge(sg_ok, k + 1)
                    if n >= 2:
                        v.wait_ge(dn_ps, n - 1)
                    v.tensor_tensor(hid[:, n % 2, f, :], up[k % 3][:, :], sg[:, k % 2, :], ALU.mult).then_inc(hid_ok, 1)

            def combine(n):
                e, b = jobs[n]
                v.wait_ge(dn_ps, n + 1)
                if n >= 2:
                    v.wait_ge(dn_ok, 4 * (n - 1))
                for c in range(4):
                    h = t.hf[:, 4 * b + c, :]
                    v.scalar_tensor_tensor(out=h, in0=dn[n % 2][:, c * 128:(c + 1) * 128],
                                           scalar=1.0 if e == NE else t.comb[:, 4 * b + c, e:e + 1], in1=h,
                                           op0=ALU.mult, op1=ALU.add).then_inc(dn_ok, 1)

            hidden(0)
            for n in range(len(jobs)):
                if n + 1 < len(jobs):
                    hidden(n + 1)
                combine(n)
            v.wait_ge(dn_ok, 4 * len(jobs))
            sh = [128, TILES, HID]
            link(v.tensor_tensor(t.hf[:, :, :], t.hf[:, :, :], bc(t.modbc[:, 5 * HID:6 * HID].unsqueeze(1), *sh), ALU.mult))
            v.tensor_tensor(t.x[:, :, :], t.x[:, :, :], t.hf[:, :, :], ALU.add).then_inc(out_ok, 1)

        @block.sync
        def _(sp):
            sp.wait_ge(out_ok, 1)
            for s in range(2):
                sp.dma_start(out[bass.ds(2 * i + s, 1), :, :].rearrange("a (c t) d -> t (a c) d", t=CK),
                             t.x[s * CK:(s + 1) * CK, :, :]).then_inc(stored, 16)
            sp.wait_ge(stored, 32)
    p.close()


class Tensors:
    pass


def build(nc, src, out):
    with ExitStack() as ctx:
        def sb(name, shape, dt=F32, c=ctx):
            return c.enter_context(nc.sbuf_tensor(name, shape, dt))

        t = Tensors()
        t.w = sb("w_kqv", [128, 2 * KD + VD])
        t.taps = sb("taps", [128, NCH, TAPS])
        t.wg = sb("wg", [128, VD])
        t.wo = sb("wo", [DV, NH, HID])
        t.wgb = sb("wgk_wb", [128, 2 * NH])
        t.wqkv = sb("wqkv", [128, 3 * HID])
        t.wo2 = sb("wo_ffn", [128, HID])
        t.wr = sb("router_w", [128, NE])
        t.n1w, t.n2w = sb("norm1_w", [128, 1]), sb("norm2_w", [128, 1])
        t.hrow = sb("dt_bias_b_b", [128, 2 * NH])
        t.nA = sb("neg_A", [128, NH])
        t.ident, t.identb = sb("ident", [128, 128]), sb("ident_bf16", [128, 128], BF16)
        t.ones, t.later, t.upto = sb("ones", [128, 128]), sb("later", [128, 128]), sb("upto", [128, 128])
        t.tri = sb("tri", [128, CK])
        t.negm = sb("neg_mask", [128, 8 * CK], BF16)
        t.parity = sb("block_parity", [128, 2])
        t.mhalf = sb("minus_half", [128, 2 * NH])
        t.rank = sb("rank", [128, NE])
        t.pick = sb("pick", [B, PAIRS, 2])
        t.mod = sb("mod", [B, 6 * HID])
        t.x = sb("x", [128, TILES, HID])
        t.modbc = sb("mod_rows", [128, 6 * HID])
        t.hT = sb("hT", [128, 2, PAD + L])
        t.hS = sb("h_tiles", [128, TILES, 128])
        t.g, t.beta, t.Gam, t.nGam, t.kdec = (sb(n, [128, TILES, NH]) for n in ("g", "beta", "Gam", "neg_Gam", "k_decay"))
        t.gmask = sb("g_masked", [128, TILES, 2, NH])
        t.gam_all = sb("gam_all", [128, TILES, 2, NP])

        load_weights(nc, t, src)
        with nc.Fori(0, PAIRS) as i:
            with ExitStack() as a:
                t.S = sb("state", [128, 2, NP, DV], c=a)
                t.kqT = sb("kq_T", [128, HALF, NP, 2, 128], c=a)
                t.kd = sb("k_end", [128, HALF, KD], c=a)
                t.pp = sb("qk", [128, HALF, NH, 128], c=a)
                t.aa = sb("systems", [128, HALF, NH, CK], c=a)
                start_pair(nc, t, src, i)
                for half in range(2):
                    project_keys(nc, t, half)
                    with ExitStack() as b:
                        t.tt = sb(f"inverse_T_{half}", [128, SYS, 128], c=b)
                        t.v = sb(f"v_{half}", [128, HALF, NH, DV], c=b)
                        invert_systems(nc, t, half)
                        scan_chunks(nc, t, half)
            with ExitStack() as a:
                t.hf = sb("h_ffn", [128, TILES, HID], c=a)
                t.cx = sb("ctx", [128, 4, TILES, 2, CK], c=a)
                t.h1T = sb("h1T", [128, 2, L], c=a)
                second_norm(nc, t)
                with ExitStack() as b:
                    t.qT, t.kT = (sb(n, [128, 2, 8, L], BF16, c=b) for n in ("q_T", "k_T"))
                    t.qs = sb("q_slots", [128, 2, TQ * AH, SLOT], BF16, c=b)
                    t.va = sb("v_and_one", [128, 2, TQ, AH, 32], c=b)
                    attention_scores(nc, t)
                    for s in range(2):
                        attention_values(nc, t, s)
                t.h2T = sb("h2T", [128, TILES * 128], c=a)
                t.comb = sb("combine", [128, TILES, NE], c=a)
                t.wgu = sb("gate_up_w", [128, NE + 1, 2, DFF], c=a)
                t.wdn = sb("down_w", [128, NE + 1, 2, HID], c=a)
                attention_output(nc, t, src)
                experts(nc, t, out, i)


def kernel(**inputs):
    import numpy as _np
    import concourse.bacc as _bacc
    from concourse import mybir as _mybir
    from concourse.bass_utils import run_bass_kernel_spmd as _run

    nc = _bacc.Bacc("TRN2", target_bir_lowering=False, num_devices=1)
    arrays, src = {}, {}
    for name in inputs:
        a = _np.ascontiguousarray(inputs[name])
        arrays[f"in_{name}"] = a
        src[name] = nc.dram_tensor(f"in_{name}", a.shape, _mybir.dt.from_np(a.dtype), kind="ExternalInput").ap()
    out = nc.dram_tensor("out0", (B, L, HID), F32, kind="ExternalOutput").ap()
    build(nc, src, out)
    r = _run(nc, [arrays], core_ids=[0])
    return r.results[0]["out0"]
```

```python
from contextlib import ExitStack

import concourse.bass as bass
from concourse import mybir

F32 = mybir.dt.float32
BF16 = mybir.dt.bfloat16
ALU = mybir.AluOpType
ACT = mybir.ActivationFunctionType
AX = mybir.AxisListType.X

B, L, HID = 8, 512, 128
NH, DK, DV = 12, 64, 128
TAPS = 4
PAD = TAPS - 1
CK = 64
PAIRS = B // 2
TILES = L // CK
HALF = TILES // 2
KD, VD = NH * DK, NH * DV
NP = NH // 2
G3 = 3
SYS = HALF * NH
BASE = 16
NBLK = 128 // BASE
AH, AD = 16, 8
SLOT = 64
NCH = (2 * KD + VD) // 128
TQ = L // 128
NE, DFF = 8, 256
NEG = -30000.0
STORES = 4 * 16


class Phase:

    def __init__(self, nc, tag=""):
        self.nc, self.ctx, self.sems, self.tag = nc, ExitStack(), [], tag

    def sb(self, name, shape, dt=F32):
        return self.ctx.enter_context(self.nc.sbuf_tensor(name + self.tag, shape, dt))

    def ps(self, name, shape, dt=F32):
        return self.ctx.enter_context(self.nc.psum_tensor(name + self.tag, shape, dt))

    def sem(self, name):
        s = self.ctx.enter_context(self.nc.semaphore(name + self.tag))
        self.sems.append(s.num)
        return s

    def close(self):
        self.ctx.close()
        self.nc.all_engine_barrier(sems_to_clear=range(min(self.sems), max(self.sems) + 1))


def linker(eng, sem):
    count = [0]

    def link(ins):
        count[0] += 1
        ins.then_inc(sem, 1)
        eng.wait_ge(sem, count[0])

    return link


def linker_from(eng, sem, done):
    count = [done]

    def link(ins):
        count[0] += 1
        ins.then_inc(sem, 1)
        eng.wait_ge(sem, count[0])

    return link


def bc(ap, *shape):
    return ap.broadcast_to(list(shape))


def load_weights(nc, t, src):
    p = Phase(nc)
    row = p.sb("head_row", [1, 3 * NH])
    crow = p.sb("c_row", [B, HID])
    wmod = p.sb("wmod_sb", [HID, 6 * HID])
    csil = p.sb("c_silu", [B, HID])
    cT = p.sb("c_silu_T", [HID, B])
    msgn = p.sb("mod_sign", [B, HID])
    mabs = p.sb("mod_abs", [B, HID])
    blk8 = p.sb("blk8", [128, NBLK])
    gnw = p.sb("gnw", [DV, 1])
    misc_ps = p.ps("misc_ps", [128, 4, 512])
    loaded, consts, pchain, vchain = p.sem("loaded"), p.sem("consts"), p.sem("pool_chain"), p.sem("vec_chain")
    a_log, row_done, c_silu, cT_ps, cT_sb, mod_ps, nA_done = (p.sem(n) for n in (
        "a_log", "row_done", "c_silu_done", "cT_ps", "cT_sb", "mod_ps_done", "nA_done"))
    with nc.Block() as block:
        @block.sync
        def _(sp):
            for name, at, w in (("L0_attn_Wk", 0, KD), ("L0_attn_Wq", KD, KD), ("L0_attn_Wv", 2 * KD, VD)):
                sp.dma_start(t.w[:, at:at + w], src[name]).then_inc(loaded, 16)
            for name, at, w in (("L0_attn_conv_k", 0, KD), ("L0_attn_conv_q", KD, KD), ("L0_attn_conv_v", 2 * KD, VD)):
                sp.dma_start(t.taps[:, at // 128:(at + w) // 128, :],
                             src[name].rearrange("(b p) k -> p b k", p=128)).then_inc(loaded, 16)
            for name, at in (("L0_attn_dt_bias", 0), ("L0_attn_b_b", NH), ("L0_attn_A_log", 2 * NH)):
                sp.dma_start(row[:, at:at + NH], src[name].rearrange("(a c) -> a c", a=1)).then_inc(loaded, 16)
            sp.dma_start(crow[:, :], src["L0_c"]).then_inc(loaded, 16)
            sp.dma_start(wmod[:, :], src["L0_wmod"]).then_inc(loaded, 16)
            sp.dma_start(t.wg[:, :], src["L0_attn_Wg"]).then_inc(loaded, 16)
            sp.dma_start(t.wo[:, :, :], src["L0_attn_Wo"].rearrange("(h p) d -> p h d", p=DV)).then_inc(loaded, 16)
            sp.dma_start(t.wgb[:, 0:NH], src["L0_attn_Wgk"]).then_inc(loaded, 16)
            sp.dma_start(t.wgb[:, NH:2 * NH], src["L0_attn_Wb"]).then_inc(loaded, 16)
            for m, name in enumerate(("L0_ffn_wq", "L0_ffn_wk", "L0_ffn_wv")):
                sp.dma_start(t.wqkv[:, m * HID:(m + 1) * HID], src[name]).then_inc(loaded, 16)
            sp.dma_start(t.wo2[:, :], src["L0_ffn_wo"]).then_inc(loaded, 16)
            sp.dma_start(t.wr[:, :], src["L0_ffn_router_w"]).then_inc(loaded, 16)
            sp.dma_start(gnw[:, :], src["L0_attn_g_norm_weight"].rearrange("(p a) -> p a", a=1)).then_inc(loaded, 16)
            sp.dma_start(t.n1w[:, :], src["L0_ffn_norm1_w"].rearrange("(p a) -> p a", a=1)).then_inc(loaded, 16)
            sp.dma_start(t.n2w[:, :], src["L0_ffn_norm2_w"].rearrange("(p a) -> p a", a=1)).then_inc(loaded, 16)
        NLOAD = 16 * 23

        @block.gpsimd
        def _(g):
            link = linker(g, pchain)
            link(g.memset(t.ident[:, :], 0.0))
            link(g.affine_select(out=t.ident[:, :], in_=t.ident[:, :], compare_op=ALU.not_equal, fill=1.0,
                                 base=0, pattern=[[-1, 128]], channel_multiplier=1))
            g.memset(t.ones[:, :], 1.0).then_inc(consts, 1)
            link(g.memset(t.later[:, :], 1.0))
            link(g.affine_select(out=t.later[:, :], in_=t.later[:, :], compare_op=ALU.is_gt, fill=0.0,
                                 base=0, pattern=[[-1, 128]], channel_multiplier=1))
            link(g.memset(t.later[CK:128, 0:CK], 0.0))
            link(g.memset(t.upto[:, :], 1.0))
            link(g.affine_select(out=t.upto[:, :], in_=t.upto[:, :], compare_op=ALU.is_ge, fill=0.0,
                                 base=0, pattern=[[1, 128]], channel_multiplier=-1))
            link(g.memset(t.upto[0:CK, CK:128], 0.0))
            link(g.tensor_copy(t.tri[0:CK, :], t.upto[0:CK, 0:CK]))
            link(g.tensor_copy(t.tri[CK:128, :], t.upto[CK:128, CK:128]))
            link(g.memset(blk8[:, :], 1.0))
            link(g.affine_select(out=blk8[:, :], in_=blk8[:, :], compare_op=ALU.is_ge, fill=0.0,
                                 base=0, pattern=[[-BASE, NBLK]], channel_multiplier=1))
            link(g.affine_select(out=blk8[:, :], in_=blk8[:, :], compare_op=ALU.is_ge, fill=0.0,
                                 base=BASE - 1, pattern=[[BASE, NBLK]], channel_multiplier=-1))
            link(g.tensor_copy(t.parity[:, :], blk8[:, 0:2]))
            for b in range(2, NBLK, 2):
                link(g.tensor_tensor(t.parity[:, :], t.parity[:, :], blk8[:, b:b + 2], ALU.add))
            link(g.memset(t.mhalf[:, :], -0.5))
            link(g.memset(t.hT[:, :, 0:PAD], 0.0))
            for b in range(NE):
                link(g.memset(t.rank[:, b:b + 1], float(NE - b)))
            link(g.memset(t.pick[:, :, :], 0.0))
            link(g.affine_select(out=t.pick[:, :, :], in_=t.pick[:, :, :], compare_op=ALU.not_equal, fill=1.0,
                                 base=0, pattern=[[-2, PAIRS], [-1, 2]], channel_multiplier=1))
            g.memset(t.hf[:, 0, 0:1], 0.0).then_inc(t.stored, STORES)
            g.memset(t.gmask[:, :, :, :], 0.0).then_inc(consts, 1)

        @block.scalar
        def _(a):
            a.wait_ge(loaded, NLOAD)
            a.activation(csil[:, :], crow[:, :], ACT.Silu).then_inc(c_silu, 1)
            a.wait_ge(cT_ps, 1)
            a.activation(cT[:, :], misc_ps[:, 1, 0:B], ACT.Copy).then_inc(cT_sb, 1)
            a.wait_ge(a_log, 1)
            a.activation(t.nA[:, :], t.nA[:, :], ACT.Exp).then_inc(nA_done, 1)

        @block.tensor
        def _(pe):
            pe.wait_ge(loaded, NLOAD)
            pe.wait_ge(consts, 2)
            pe.matmul(misc_ps[:, 0, 0:3 * NH], t.ones[0:1, :], row[:, :], start=True, stop=True).then_inc(row_done, 1)
            pe.wait_ge(c_silu, 1)
            pe.transpose(misc_ps[:, 1, 0:B], csil[:, :], t.ident[0:B, 0:B]).then_inc(cT_ps, 1)
            pe.wait_ge(cT_sb, 1)
            for c in range(2):
                m = pe.matmul(misc_ps[0:B, 2 + c, 0:384], cT[:, :], wmod[:, c * 384:(c + 1) * 384], start=True, stop=True)
            m.then_inc(mod_ps, 1)

        @block.vector
        def _(v):
            link = linker(v, vchain)
            v.wait_ge(loaded, NLOAD)
            v.wait_ge(consts, 2)
            v.wait_ge(row_done, 1)
            link(v.tensor_copy(t.hrow[:, :], misc_ps[:, 0, 0:2 * NH]))
            v.tensor_copy(t.nA[:, :], misc_ps[:, 0, 2 * NH:3 * NH]).then_inc(a_log, 1)
            v.wait_ge(nA_done, 1)
            link(v.tensor_scalar(t.nA[:, :], t.nA[:, :], -1.0, None, ALU.mult))
            link(v.tensor_scalar(t.wo[:, :, :].rearrange("p h d -> p (h d)"), t.wo[:, :, :].rearrange("p h d -> p (h d)"),
                                 gnw[:, 0:1], None, ALU.mult))
            link(v.tensor_copy(t.identb[:, :], t.ident[:, :]))
            for k in range(8):
                link(v.tensor_scalar(t.negm[:, k * CK:(k + 1) * CK], t.tri[:, :], -NEG, NEG, ALU.mult, ALU.add))
            v.wait_ge(mod_ps, 1)
            for m in range(6):
                o, i = t.mod[:, m * HID:(m + 1) * HID], misc_ps[0:B, 2 + m // 3, (m % 3) * HID:(m % 3 + 1) * HID]
                if m % 3 == 0:
                    link(v.tensor_copy(o, i))
                elif m % 3 == 1:
                    link(v.tensor_scalar(o, i, 1.0, None, ALU.add))
                else:
                    link(v.tensor_scalar(msgn[:, :], i, 0.0, 2.0, ALU.is_ge, ALU.mult))
                    link(v.tensor_scalar(mabs[:, :], i, -1.0, None, ALU.mult))
                    link(v.tensor_tensor(mabs[:, :], i, mabs[:, :], ALU.max))
                    link(v.tensor_scalar(mabs[:, :], mabs[:, :], 0.25, None, ALU.max))
                    link(v.tensor_scalar(msgn[:, :], msgn[:, :], -1.0, None, ALU.add))
                    link(v.tensor_tensor(o, msgn[:, :], mabs[:, :], ALU.mult))
    p.close()


def start_pair(nc, t, src, i):
    p = Phase(nc)
    cen, sq = p.sb("cen", [128, TILES, HID]), p.sb("sq", [128, TILES, HID])
    st = p.sb("ln_st", [128, 2, TILES])
    sel = p.sb("sel", [B, 128])
    ps = p.ps("ps_a1", [128, 4, 512])
    x_in, vch, pow_in, pow_out, sel_ok, mod_ok = (p.sem(n) for n in ("x_in", "vch", "pow_in", "pow_out", "sel_ok", "mod_ok"))
    modbc, h_ok, hT_ps, hT_ok = (p.sem(n) for n in ("modbc_ok", "h_ok", "hT_ps", "hT_ok"))
    s0, hS_ok = p.sem("s0"), p.sem("hS_ok")
    p.sems.append(t.stored.num)
    with nc.Block() as block:
        @block.sync
        def _(sp):
            for s in range(2):
                sp.dma_start(t.x[s * CK:(s + 1) * CK, :, :],
                             src["L0_attn_hidden_states"][bass.ds(2 * i + s, 1), :, :]
                             .rearrange("a (c t) d -> t (a c) d", t=CK)).then_inc(x_in, 16)
            sp.wait_ge(t.stored, STORES)

        @block.gpsimd
        def _(g):
            g.memset(t.S[:, :, :, :], 0.0).then_inc(s0, 1)
            g.memset(t.pp[:, :, :, :], 0.0).then_inc(s0, 1)
            for b in range(2):
                z = st[:, 1, b * HALF:(b + 1) * HALF]
                g.wait_ge(pow_in, b + 1)
                g.tensor_tensor(z, z, t.mhalf[:, 0:HALF], ALU.pow).then_inc(pow_out, 1)

        @block.vector
        def _(v):
            link = linker(v, vch)

            v.tensor_copy(sel[:, :].rearrange("b (s t) -> b s t", s=2),
                          bc(t.pick[:, bass.ds(i, 1), :].rearrange("b a s -> b (a s)").unsqueeze(2), B, 2, CK)).then_inc(sel_ok, 1)
            v.wait_ge(x_in, 32)
            sh = [128, HALF, HID]
            half = lambda b: slice(b * HALF, (b + 1) * HALF)
            row = lambda m: bc(t.modbc[:, m * HID:(m + 1) * HID].unsqueeze(1), *sh)
            for b in range(2):
                cs = half(b)
                x, h, z, mean, var = t.x[:, cs, :], cen[:, cs, :], sq[:, cs, :], st[:, 0, cs], st[:, 1, cs]
                link(v.tensor_reduce(mean, x, AX, ALU.add))
                link(v.tensor_scalar(mean, mean, 1.0 / HID, None, ALU.mult))
                link(v.tensor_tensor(h, x, bc(mean.unsqueeze(2), *sh), ALU.subtract))
                link(v.tensor_tensor(z, h, h, ALU.mult))
                link(v.tensor_reduce(var, z, AX, ALU.add))
                v.tensor_scalar(var, var, 1.0 / HID, 1e-5, ALU.mult, ALU.add).then_inc(pow_in, 1)
            v.wait_ge(modbc, 2)
            for b in range(2):
                h = cen[:, half(b), :]
                v.wait_ge(pow_out, b + 1)
                link(v.tensor_tensor(h, h, bc(st[:, 1, half(b)].unsqueeze(2), *sh), ALU.mult))
                link(v.tensor_tensor(h, h, row(1), ALU.mult))
                v.tensor_tensor(h, h, row(0), ALU.add).then_inc(h_ok, 1)

        @block.scalar
        def _(a):
            a.wait_ge(mod_ok, 1)
            a.activation(t.modbc[:, 0:512], ps[:, 0, :], ACT.Copy).then_inc(modbc, 1)
            a.activation(t.modbc[:, 512:768], ps[:, 1, 0:256], ACT.Copy).then_inc(modbc, 1)
            for b in range(2):
                a.wait_ge(hT_ps, b + 1)
                a.activation(t.hT[:, :, PAD + 256 * b:PAD + 256 * (b + 1)].rearrange("p s (c t) -> p c s t", c=4),
                             ps[:, 2 + b, :].rearrange("p (c s t) -> p c s t", c=4, s=2), ACT.Copy).then_inc(hT_ok, 1)
            for b in range(2):
                a.activation(t.hS[:, 4 * b:4 * b + 4, :].rearrange("p c t -> p (c t)"), ps[:, 2 + b, :],
                             ACT.Copy).then_inc(hS_ok, 1)

        @block.tensor
        def _(pe):
            pe.wait_ge(sel_ok, 1)
            pe.matmul(ps[:, 0, :], sel[:, :], t.mod[:, 0:512], start=True, stop=True)
            pe.matmul(ps[:, 1, 0:256], sel[:, :], t.mod[:, 512:768], start=True, stop=True).then_inc(mod_ok, 1)
            for c in range(TILES):
                pe.wait_ge(h_ok, c // HALF + 1)
                m = pe.transpose(ps[:, 2 + c // 4, (c % 4) * 128:(c % 4 + 1) * 128], cen[:, c, :], t.ident[:, :])
                if c % 4 == 3:
                    m.then_inc(hT_ps, 1)
    p.close()


def convolve_matmul(pe, t, o, half, block, s):
    at = half * HALF * CK
    return pe.matmul(o, t.w[:, block * 128:(block + 1) * 128], t.hT[:, s, at:at + PAD + HALF * CK], start=True, stop=True)


def project_keys(nc, t, half):
    p = Phase(nc, f"_{half}")
    N = HALF * CK
    ac = p.sb("conv_acc", [128, 2, 2, N])
    sl = p.sb("conv_silu", [128, 2, HALF, 2, CK])
    tk = p.sb("kq_tokens", [128, 2, 2, HALF, 2, DK])
    sq = p.sb("kq_sq", [128, 2 * HALF * 2, DK])
    ss = p.sb("kq_ss", [128, 2, 2, HALF, 2])
    co = p.sb("kq_coef", [128, 2, 3, HALF, 2])
    kn, qn, qg = (p.sb(n, [128, HALF, 2, DK]) for n in ("kn", "qn", "qg"))
    seg = p.sb("seg_rhs", [128, 2, HALF, 2, CK])
    ex = p.sb("decay", [128, NP, HALF, 2, CK])
    cv = [p.ps(f"conv_ps{b}", [128, 2, 512]) for b in range(2)]
    tp = [p.ps(f"trp{b}", [128, 512]) for b in range(2)]
    sk = [p.ps(f"seg_kk{b}", [128, 512]) for b in range(2)]
    names = ("conv_ps", "conv_init", "conv_done", "silu_done", "tok_ps", "tok_done", "sq_done", "ss_done", "ss_eps",
             "rs_done", "coef_done", "kn_done", "qn_done", "qg_done", "kend_done", "seg_rhs_done", "seg_ps", "exp_done",
             "decay_done", "key_ps", "key_done", "kk_ps", "kk_used", "vch2")
    (conv_ps, conv_init, conv_done, silu, tok_ps, tok_done, sq_done, ss_done, ss_eps, rs_done, coef, kn_done, qn_done,
     qg_done, kend_done, seg_rhs, seg_ps, exp_done, decay, key_ps, key_done, kk_ps, kk_used, vch) = (p.sem(n) for n in names)
    sh = [128, HALF, 2, DK]
    C0 = half * HALF
    first = half == 0
    if first:
        zg, zb, za, ze = (p.sb(n, [128, TILES, NH]) for n in ("zg", "zb", "za", "ze"))
        z_ps, z_ok, e_ok, l_in, l_ok, g_ok, stat_ps, stat_ok, beta_ok, zch = (p.sem(n) for n in (
            "z_ps", "z_ok", "e_ok", "l_in", "l_ok", "g_ok", "stat_ps", "stat_ok", "beta_ok", "gate_chain"))
        WT = TILES * NH
        stat = [sk[1][:, 0:WT], sk[1][:, WT:2 * WT], sk[1][:, 2 * WT:4 * WT]]
    trs = [("tok", 0), ("tok", 1)]
    for n in range(NP):
        if n + 1 < NP:
            trs += [("tok", 2 * n + 2), ("tok", 2 * n + 3)]
        trs += [("key", 3 * n), ("key", 3 * n + 1), ("key", 3 * n + 2)]
    place = {job: n for n, job in enumerate(trs)}

    with nc.Block() as block:
        @block.tensor
        def _(pe):
            def convolve(n):
                for w in range(2):
                    m = 2 * n + w
                    if m >= 2:
                        pe.wait_ge(conv_done, 3 * (m - 1))
                    for s in range(2):
                        last = convolve_matmul(pe, t, cv[m % 2][:, s, 0:PAD + N], half, w * NP + n, s)
                    last.then_inc(conv_ps, 1)

            def transposes(job, source):
                kind, n = job
                at = place[job]
                if at >= 2:
                    old, m = trs[at - 2]
                    pe.wait_ge(tok_done if old == "tok" else key_done, m + 1)
                for c in range(HALF):
                    last = pe.transpose(tp[at % 2][:, c * 128:(c + 1) * 128], source(c), t.ident[:, :])
                last.then_inc(tok_ps if kind == "tok" else key_ps, 1)

            def tokens(n):
                for w in range(2):
                    pe.wait_ge(silu, 2 * n + w + 1)
                    transposes(("tok", 2 * n + w), lambda c: sl[:, w, c, :, :].rearrange("p s t -> p (s t)"))

            def segments(n):
                pe.wait_ge(seg_rhs, n + 1)
                if n >= 2:
                    pe.wait_ge(exp_done, n - 1)
                o = sk[n % 2][:, :]
                pe.matmul(o, t.later[:, :], seg[:, n % 2, :, :, :].rearrange("p c h i -> p (c h i)"), start=True, stop=False)
                pe.matmul(o, t.identb[:, :], t.negm[:, :], start=False, stop=True).then_inc(seg_ps, 1)

            def products(n):
                pe.wait_ge(key_done, 3 * n + 2)
                for r in range(2):
                    if n:
                        pe.wait_ge(kk_used, 2 * n + r - 1)
                    else:
                        pe.wait_ge(exp_done, NP)
                    rows = slice(r * 64, (r + 1) * 64)
                    for c in range(HALF):
                        for s in range(2):
                            cs = slice(s * CK, (s + 1) * CK)
                            m = pe.matmul(sk[r][cs, c * 128:(c + 1) * 128], t.kqT[rows, c, n, 0, cs],
                                          t.kqT[rows, c, n, :, cs], start=True, stop=True)
                    m.then_inc(kk_ps, 1)

            if first:
                for c in range(TILES):
                    m = pe.matmul(sk[0][:, c * 2 * NH:(c + 1) * 2 * NH], t.hS[:, c, :], t.wgb[:, :], start=True, stop=True)
                m.then_inc(z_ps, 1)
            convolve(0)
            if first:
                pe.wait_ge(g_ok, 3)
                gf = t.g[:, :, :].rearrange("p c h -> p (c h)")
                pe.matmul(stat[0], t.upto[:, :], gf, start=True, stop=True)
                pe.matmul(stat[1], t.later[:, :], gf, start=True, stop=True)
                pe.matmul(stat[2], t.ones[:, :], t.gmask[:, :, :, :].rearrange("p c s h -> p (c s h)"),
                          start=True, stop=True).then_inc(stat_ps, 1)
            for n in range(NP):
                if first and n == 1:
                    pe.wait_ge(stat_ok, 4)
                segments(n)
            convolve(1)
            tokens(0)
            for n in range(NP):
                if n + 1 < NP:
                    tokens(n + 1)
                if n + 2 < NP:
                    convolve(n + 2)
                for k, (ready, source) in enumerate(((kn_done, kn), (qn_done, qn), (qg_done, qg))):
                    if k == 2:
                        products(n)
                    pe.wait_ge(ready, n + 1)
                    transposes(("key", 3 * n + k), lambda c: source[:, c, :, :].rearrange("p h d -> p (h d)"))

        @block.scalar
        def _(a):
            def start_sum(n):
                for w in range(2):
                    a.wait_ge(conv_ps, 2 * n + w + 1)
                    if n:
                        a.wait_ge(silu, 2 * (n - 1) + w + 1)
                    a.activation(ac[:, w, :, :], cv[w][:, :, PAD:PAD + N], ACT.Copy,
                                 scale=t.taps[:, w * NP + n, PAD:PAD + 1]).then_inc(conv_init, 1)

            def silus(n):
                for w in range(2):
                    a.wait_ge(conv_done, 3 * (2 * n + w + 1))
                    if n:
                        a.wait_ge(tok_ps, 2 * (n - 1) + w + 1)
                    a.activation(sl[:, w, :, :, :].rearrange("p c s t -> p s c t"),
                                 ac[:, w, :, :].rearrange("p s (c t) -> p s c t", c=HALF), ACT.Silu).then_inc(silu, 1)

            def tokens(n):
                if n >= 2:
                    a.wait_ge(qn_done, n - 1)
                    a.wait_ge(qg_done, n - 1)
                    a.wait_ge(kend_done, n - 1)
                for w in range(2):
                    a.wait_ge(tok_ps, 2 * n + w + 1)
                    a.activation(tk[:, n % 2, w, :, :, :].rearrange("p c h d -> p (c h d)"),
                                 tp[place[("tok", 2 * n + w)] % 2][:, :], ACT.Copy).then_inc(tok_done, 1)
                a.wait_ge(tok_done, 2 * n + 2)
                if n:
                    a.wait_ge(ss_done, n)
                a.activation(sq[:, :, :].rearrange("p x d -> p (x d)"),
                             tk[:, n % 2, :, :, :, :].rearrange("p w c h d -> p (w c h d)"), ACT.Square).then_inc(sq_done, 1)

            if first:
                a.wait_ge(z_ok, 1)
                a.activation(t.beta[:, :, :], zb[:, :, :], ACT.Sigmoid).then_inc(beta_ok, 1)
                a.wait_ge(z_ok, 2)
                a.activation(ze[:, :, :], za[:, :, :], ACT.Exp, scale=-1.0).then_inc(e_ok, 1)
                a.wait_ge(l_in, 1)
                a.activation(ze[:, :, :], ze[:, :, :], ACT.Ln).then_inc(l_ok, 1)
            start_sum(0)
            if first:
                a.wait_ge(stat_ps, 1)
                a.activation(t.Gam[:, :, :].rearrange("p c h -> p (c h)"), stat[0], ACT.Exp).then_inc(stat_ok, 1)
                a.activation(t.kdec[:, :, :].rearrange("p c h -> p (c h)"), stat[1], ACT.Exp).then_inc(stat_ok, 1)
                gv = stat[2].rearrange("p (c s h r) -> p r (c s) h", c=TILES, s=2, r=2)
                for r in range(2):
                    rows = slice(r * 64, (r + 1) * 64)
                    a.activation(t.gam_all[rows, :, :, :].rearrange("p c s h -> p (c s) h"),
                                 gv[rows, r, :, :], ACT.Exp).then_inc(stat_ok, 1)
            for n in range(NP):
                a.wait_ge(seg_ps, n + 1)
                a.activation(ex[:, n, :, :, :].rearrange("p c h i -> p (c h i)"), sk[n % 2][:, :], ACT.Exp).then_inc(exp_done, 1)
            silus(0)
            start_sum(1)
            tokens(0)
            for n in range(NP):
                if n + 1 < NP:
                    silus(n + 1)
                    tokens(n + 1)
                if n + 2 < NP:
                    start_sum(n + 2)
                for k in range(3):
                    a.wait_ge(key_ps, 3 * n + k + 1)
                    if k == 2:
                        a.wait_ge(kk_ps, 2 * (n + 1))
                    a.activation(t.kqT[:, :, n, min(k, 1), :],
                                 tp[place[("key", 3 * n + k)] % 2][:, :].rearrange("p (c i) -> p c i", c=HALF),
                                 ACT.Copy).then_inc(key_done, 1)

        @block.vector
        def _(v):
            link = linker(v, vch)

            def convolve(n):
                for w in range(2):
                    v.wait_ge(conv_init, 2 * n + w + 1)
                    for j in range(PAD):
                        if j:
                            v.wait_ge(conv_done, 3 * (2 * n + w) + j)
                        v.scalar_tensor_tensor(out=ac[:, w, :, :], in0=cv[w][:, :, j:j + N],
                                               scalar=t.taps[:, w * NP + n, j:j + 1], in1=ac[:, w, :, :],
                                               op0=ALU.mult, op1=ALU.add).then_inc(conv_done, 1)

            def norms(n):
                S = ss[:, n % 2, :, :, :]
                v.wait_ge(sq_done, n + 1)
                if n >= 2:
                    v.wait_ge(kend_done, n - 1)
                    v.wait_ge(qg_done, n - 1)
                flat = S.rearrange("p w c h -> p (w c h)")
                v.tensor_reduce(flat, sq[:, :, :], AX, ALU.add).then_inc(ss_done, 1)
                v.wait_ge(ss_done, n + 1)
                v.tensor_scalar(flat, flat, 1e-6, None, ALU.add).then_inc(ss_eps, 1)

            def normalise(n):
                S, Co = ss[:, n % 2, :, :, :], co[:, n % 2, :, :, :]
                v.wait_ge(rs_done, n + 1)
                hs = slice(2 * n, 2 * n + 2)
                v.tensor_tensor(Co[:, 0, :, :], S[:, 0, :, :], t.kdec[:, C0:C0 + HALF, hs], ALU.mult).then_inc(coef, 1)
                link(v.tensor_scalar(Co[:, 1, :, :], S[:, 1, :, :], DK ** -0.5, None, ALU.mult))
                v.tensor_tensor(Co[:, 2, :, :], Co[:, 1, :, :], t.Gam[:, C0:C0 + HALF, hs], ALU.mult).then_inc(coef, 1)
                if n:
                    v.wait_ge(key_ps, 3 * (n - 1) + 2)
                v.tensor_tensor(kn[:, :, :, :], tk[:, n % 2, 0, :, :, :], bc(S[:, 0, :, :].unsqueeze(3), *sh),
                                ALU.mult).then_inc(kn_done, 1)
                v.tensor_tensor(qn[:, :, :, :], tk[:, n % 2, 1, :, :, :], bc(Co[:, 1, :, :].unsqueeze(3), *sh),
                                ALU.mult).then_inc(qn_done, 1)

            if first:
                glink = linker(v, zch)
                v.wait_ge(z_ps, 1)
                z = sk[0][:, 0:TILES * 2 * NH].rearrange("p (c z) -> p c z", c=TILES)
                hs = [128, TILES, NH]
                glink(v.tensor_tensor(zg[:, :, :], z[:, :, 0:NH], bc(t.hrow[:, 0:NH].unsqueeze(1), *hs), ALU.add))
                v.tensor_tensor(zb[:, :, :], z[:, :, NH:2 * NH], bc(t.hrow[:, NH:2 * NH].unsqueeze(1), *hs), ALU.add).then_inc(z_ok, 1)
                glink(v.tensor_scalar(za[:, :, :], zg[:, :, :], -1.0, None, ALU.mult))
                v.tensor_tensor(za[:, :, :], zg[:, :, :], za[:, :, :], ALU.max).then_inc(z_ok, 1)
                v.wait_ge(e_ok, 1)
                v.tensor_scalar(ze[:, :, :], ze[:, :, :], 1.0, None, ALU.add).then_inc(l_in, 1)
                glink(v.tensor_scalar(zg[:, :, :], zg[:, :, :], 0.0, None, ALU.max))
                v.wait_ge(l_ok, 1)
                glink(v.tensor_tensor(zg[:, :, :], zg[:, :, :], ze[:, :, :], ALU.add))
                v.tensor_tensor(t.g[:, :, :], zg[:, :, :], bc(t.nA[:, :].unsqueeze(1), *hs), ALU.mult).then_inc(g_ok, 1)
                v.wait_ge(g_ok, 1)
                v.tensor_copy(t.gmask[0:CK, :, 0, :], t.g[0:CK, :, :]).then_inc(g_ok, 1)
                v.tensor_copy(t.gmask[CK:128, :, 1, :], t.g[CK:128, :, :]).then_inc(g_ok, 1)
            convolve(0)
            if first:
                v.wait_ge(stat_ok, 4)
                v.wait_ge(beta_ok, 1)
                glink(v.tensor_tensor(t.kdec[:, :, :], t.kdec[:, :, :], t.beta[:, :, :], ALU.mult))
                glink(v.tensor_scalar(t.nGam[:, :, :], t.Gam[:, :, :], -1.0, None, ALU.mult))
            convolve(1)
            norms(0)
            normalise(0)
            for n in range(NP):
                if n + 1 < NP:
                    norms(n + 1)
                if n + 2 < NP:
                    convolve(n + 2)
                if n + 1 < NP:
                    normalise(n + 1)
                v.wait_ge(decay, n + 1)
                for r in range(2):
                    v.wait_ge(kk_ps, 2 * n + r + 1)
                    z = sk[r][:, :].rearrange("p (c m i) -> p c m i", c=HALF, m=2)
                    e = ex[:, n, :, r, :]
                    v.tensor_tensor(t.aa[:, :, 2 * n + r, :], z[:, :, 0, :], e, ALU.mult)
                    for s in range(2):
                        cs = slice(s * CK, (s + 1) * CK)
                        m = v.tensor_tensor(t.pp[cs, :, 2 * n + r, cs], z[cs, :, 1, :], e[cs, :, :], ALU.mult)
                    m.then_inc(kk_used, 1)

        @block.gpsimd
        def _(g):
            def segment(n):
                if n >= 2:
                    g.wait_ge(seg_ps, n - 1)
                g.tensor_tensor(seg[:, n % 2, :, :, :], bc(t.g[:, C0:C0 + HALF, 2 * n:2 * n + 2].unsqueeze(3), *sh),
                                bc(t.tri[:, :].unsqueeze(1).unsqueeze(1), *sh), ALU.mult).then_inc(seg_rhs, 1)

            def decays(n):
                g.wait_ge(exp_done, n + 1)
                g.tensor_tensor(ex[:, n, :, :, :], ex[:, n, :, :, :],
                                bc(t.beta[:, C0:C0 + HALF, 2 * n:2 * n + 2].unsqueeze(3), *sh), ALU.mult).then_inc(decay, 1)

            if first:
                g.wait_ge(g_ok, 1)
                g.wait_ge(beta_ok, 1)
            for n in range(NP):
                segment(n)
            decays(0)
            decays(1)
            for n in range(NP):
                g.wait_ge(ss_eps, n + 1)
                flat = ss[:, n % 2, :, :, :].rearrange("p w c h -> p (w c h)")
                g.tensor_tensor(flat, flat, t.mhalf[:, 0:4 * HALF], ALU.pow).then_inc(rs_done, 1)
                g.wait_ge(coef, 2 * n + 2)
                if n:
                    g.wait_ge(key_ps, 3 * n)
                g.tensor_tensor(qg[:, :, :, :], tk[:, n % 2, 1, :, :, :], bc(co[:, n % 2, 2, :, :].unsqueeze(3), *sh),
                                ALU.mult).then_inc(qg_done, 1)
                g.tensor_tensor(t.kd[:, :, n * 128:(n + 1) * 128].rearrange("p c (h d) -> p c h d", h=2),
                                tk[:, n % 2, 0, :, :, :], bc(co[:, n % 2, 0, :, :].unsqueeze(3), *sh),
                                ALU.mult).then_inc(kend_done, 1)
                if n + 2 < NP:
                    decays(n + 2)
    p.close()


def invert_systems(nc, t, half):
    p = Phase(nc, f"_{half}")
    N = HALF * CK
    W = 2 * BASE
    G1, J1 = SYS // 2, 2
    G2, J2 = 16, SYS // 16
    first, second = (p.sb(n, [128, BASE * 128]) for n in ("work_a", "work_b"))
    blocks = lambda w: w[0:SYS, :].rearrange("g (i b j) -> g i b j", i=BASE, b=NBLK)
    a16, t16, c16 = blocks(first), blocks(second), blocks(first)
    tt32 = p.sb("blocks_T", [128, SYS, W])
    tn32 = first[:, 0:SYS * W].rearrange("p (g i) -> p g i", g=SYS)
    xs = [second[:, n * G1 * W:(n + 1) * G1 * W].rearrange("p (g i) -> p g i", g=G1) for n in range(J1)]
    x2 = [w[:, at:at + G2 * W].rearrange("p (g i) -> p g i", g=G2)
          for w, at in ((first, SYS * W), (second, SYS * W), (second, 0))]
    scratch = t.tt[:, :, :].rearrange("p g i -> p (g i)")
    ac = scratch[:, 0:4 * N].rearrange("p (r s n) -> p r s n", r=2, s=2)
    sl = scratch[:, 4 * N:8 * N].rearrange("p (r c s n) -> p r c s n", r=2, c=HALF, s=2)
    tmp_pool = scratch[0:SYS, 8 * N:8 * N + 64 * NBLK]
    tmp_dve = scratch[0:SYS, 8 * N + 64 * NBLK:8 * N + 128 * NBLK]
    DB = 1
    ps = p.ps("ps_inv", [128, 8, 512])
    names = ("sel_ps", "a16_ok", "unit_ok", "substituted", "c16_ok", "back_ps", "blocks_ok", "xs_zero", "x_ps", "x_ok",
             "y_ps", "y_ok", "conv_ps_v", "conv_init_v", "conv_done_v", "silu_done_v", "v_ps", "v_done", "tt_zero",
             "tt_done", "substituted_dve")
    (sel_ps, a16_ok, unit_ok, sub, c16_ok, back_ps, blocks_ok, xs_zero, x_ps, x_ok, y_ps, y_ok,
     conv_ps, conv_init, conv_done, silu, v_ps, v_done, tt_zero, tt_done, sub_dve) = (p.sem(n) for n in names)
    av = t.aa[:, :, :, :].rearrange("p c h i -> p (c h) i")
    SUBS = 2 * (BASE - 1)
    cv = lambda n: ps[:, 4 + 2 * (n % 2):6 + 2 * (n % 2), :]
    view = lambda bank, w, g: ps[:, bank, 0:g * w].rearrange("p (g i) -> p g i", g=g)
    x2bank, y2bank = (4, 5, 6), (7, 0, 1)
    quarter = [slice(32 * q, 32 * q + 32) for q in range(4)]

    def diagonal(copy, n, quarters, *args):
        gs = slice(G1 * n, G1 * (n + 1))
        for q in quarters:
            copy(t.tt[quarter[q], gs, 32 * q:32 * q + 32], tt32[quarter[q], gs, :], *args).then_inc(tt_done, 1)

    def substitute(eng, sem, bs, tmp):
        link = linker(eng, sem)
        nb = bs.stop - bs.start
        eng.wait_ge(unit_ok, 1 + BASE)
        eng.wait_ge(a16_ok, 4)
        for j in range(BASE - 1):
            r, w = BASE - 1 - j, j + 1
            o = tmp[:, 0:r * nb * w].rearrange("g (i b c) -> g i b c", i=r, b=nb)
            sh = [SYS, r, nb, w]
            T = t16[:, j + 1:, bs, 0:w]
            link(eng.tensor_tensor(o, bc(a16[:, j + 1:, bs, j:j + 1], *sh), bc(t16[:, j:j + 1, bs, 0:w], *sh), ALU.mult))
            link(eng.tensor_tensor(T, T, o, ALU.subtract))

    with nc.Block() as block:
        @block.tensor
        def _(pe):
            idv = t.ident[:, :].rearrange("p (s b j) -> p s b j", s=2, b=4)

            def select(lot):
                if lot >= 2:
                    pe.wait_ge(a16_ok, lot - 1)
                for i in range(4):
                    o = ps[0:SYS, lot % 2, i * 128:(i + 1) * 128].rearrange("p (s b j) -> p s b j", s=2, b=4)
                    for b in range(4):
                        m = pe.matmul(o[:, :, b, :], av[:, :, b * BASE + 4 * lot + i], idv[:, :, b, :], start=True, stop=True)
                m.then_inc(sel_ps, 1)

            def convolve(n):
                if n >= 2:
                    pe.wait_ge(conv_done, 3 * (n - 1))
                for s in range(2):
                    last = convolve_matmul(pe, t, cv(n)[:, s, 0:PAD + N], half, 2 * NP + n, s)
                last.then_inc(conv_ps, 1)

            convolve(0)
            convolve(1)
            select(0)
            select(1)
            for n in range(NH):
                if n >= 2:
                    pe.wait_ge(v_done, n - 1)
                if n + 2 < NH:
                    convolve(n + 2)
                if n < 2:
                    select(n + 2)
                pe.wait_ge(silu, n + 1)
                for c in range(HALF):
                    m = pe.transpose(ps[:, 2 + n % 2, c * 128:(c + 1) * 128], sl[:, n % 2, c, :, :].rearrange("p s t -> p (s t)"),
                                     t.ident[:, :])
                m.then_inc(v_ps, 1)
            pe.wait_ge(sub, SUBS)
            pe.wait_ge(sub_dve, SUBS)
            pe.wait_ge(conv_done, 3 * NH)
            pe.wait_ge(v_done, NH)
            for i in range(BASE):
                m = pe.transpose(ps[:, 2 + i // 8, (i % 8) * SYS:(i % 8 + 1) * SYS],
                                 t16[:, i, :, :].rearrange("g b j -> g (b j)"), t.ident[0:SYS, 0:SYS])
                if i % 8 == 7:
                    m.then_inc(back_ps, 1)
            pe.wait_ge(c16_ok, 1)
            for j in range(BASE):
                m = pe.transpose(ps[:, 4 + j // 8, (j % 8) * SYS:(j % 8 + 1) * SYS],
                                 c16[:, j, :, :].rearrange("g b i -> g (b i)"), t.ident[0:SYS, 0:SYS])
                if j % 8 == 7:
                    m.then_inc(back_ps, 1)

            pe.wait_ge(blocks_ok, 4)
            for n in range(J1):
                for k in range(G1):
                    for q, rows in enumerate(quarter):
                        m = pe.matmul(view(6 + n, BASE, G1)[rows, k, :], av[rows, G1 * n + k, 32 * (q % 2):32 * (q % 2) + 32],
                                      tn32[rows, G1 * n + k, 0:BASE], start=True, stop=True)
                m.then_inc(x_ps, 1)
            for n in range(J1):
                pe.wait_ge(x_ok, n + 1)
                for k in range(G1):
                    for rows in quarter:
                        m = pe.matmul(view(2 * n, BASE, G1)[rows, k, :], xs[n][rows, k, :],
                                      tt32[rows, G1 * n + k, BASE:W], start=True, stop=True)
                m.then_inc(y_ps, 1)
                for k in range(G1):
                    for rows in quarter[0:3:2]:
                        m = pe.matmul(view(2 * n + 1, BASE, G1)[rows, k, :], tt32[rows, G1 * n + k, :],
                                      xs[n][rows, k, 0:BASE], start=True, stop=True)
                m.then_inc(y_ps, 1)
            for n in range(J2):
                pe.wait_ge(y_ok, 3 if n == 0 else 6)
                for k in range(G2):
                    for s in range(2):
                        m = pe.matmul(view(x2bank[n], W, G2)[quarter[2 * s + 1], k, :], av[quarter[2 * s], G2 * n + k, W:CK],
                                      tn32[quarter[2 * s], G2 * n + k, :], start=True, stop=True)
                m.then_inc(x_ps, 1)
            for n in range(J2):
                pe.wait_ge(x_ok, J1 + 2 * (n + 1))
                for k in range(G2):
                    for s in range(2):
                        m = pe.matmul(view(y2bank[n], W, G2)[quarter[2 * s], k, :], x2[n][quarter[2 * s + 1], k, :],
                                      tt32[quarter[2 * s + 1], G2 * n + k, :], start=True, stop=True)
                m.then_inc(y_ps, 1)

        @block.gpsimd
        def _(g):
            g.memset(t16[:, :, :, :], 0.0).then_inc(unit_ok, 1)
            g.wait_ge(unit_ok, 1)
            for i in range(BASE):
                g.memset(t16[:, i, :, i:i + 1], 1.0).then_inc(unit_ok, 1)
            substitute(g, sub, slice(DB, NBLK), tmp_pool)
            g.wait_ge(c16_ok, 1)
            g.wait_ge(back_ps, 2)
            g.memset(second[:, 0:SYS * W], 0.0).then_inc(xs_zero, 1)
            g.wait_ge(v_ps, NH)
            g.memset(t.tt[:, :, :], 0.0).then_inc(tt_zero, 1)
            g.wait_ge(tt_zero, 1)
            for n in range(J1):
                g.wait_ge(y_ok, 3 * (n + 1))
                diagonal(g.tensor_copy, n, (1, 3))

        @block.scalar
        def _(a):
            def selected(k):
                a.wait_ge(sel_ps, k + 1)
                a.activation(a16[:, 4 * k:4 * k + 4, :, :].rearrange("g i b j -> g (i b j)"), ps[0:SYS, k % 2, :],
                             ACT.Copy).then_inc(a16_ok, 1)

            def start_sum(n):
                a.wait_ge(conv_ps, n + 1)
                a.activation(ac[:, n % 2, :, :], cv(n)[:, :, PAD:PAD + N], ACT.Copy,
                             scale=t.taps[:, 2 * NP + n, PAD:PAD + 1]).then_inc(conv_init, 1)

            start_sum(0)
            start_sum(1)
            selected(0)
            selected(1)
            for n in range(NH):
                a.wait_ge(conv_done, 3 * (n + 1))
                if n >= 2:
                    a.wait_ge(v_ps, n - 1)
                a.activation(sl[:, n % 2, :, :, :].rearrange("p c s t -> p s c t"),
                             ac[:, n % 2, :, :].rearrange("p s (c t) -> p s c t", c=HALF), ACT.Silu).then_inc(silu, 1)
                if n:
                    a.wait_ge(v_ps, n)
                    a.activation(t.v[:, :, n - 1, :], ps[:, 2 + (n - 1) % 2, :].rearrange("p (c d) -> p c d", c=HALF),
                                 ACT.Copy).then_inc(v_done, 1)
                if n + 2 < NH:
                    a.wait_ge(silu, n + 1)
                    start_sum(n + 2)
                if n < 2:
                    selected(n + 2)
            a.wait_ge(v_ps, NH)
            a.activation(t.v[:, :, NH - 1, :], ps[:, 2 + (NH - 1) % 2, :].rearrange("p (c d) -> p c d", c=HALF),
                         ACT.Copy).then_inc(v_done, 1)
            a.wait_ge(sub, SUBS)
            a.wait_ge(sub_dve, SUBS)
            a.activation(c16[:, :, :, :].rearrange("g j b i -> g i b j"), t16[:, :, :, :], ACT.Copy).then_inc(c16_ok, 1)
            a.wait_ge(xs_zero, 1)
            for n in range(J1):
                a.wait_ge(x_ps, n + 1)
                a.activation(xs[n][:, :, 0:BASE], view(6 + n, BASE, G1), ACT.Copy, scale=t.parity[:, 1:2]).then_inc(x_ok, 1)
            a.wait_ge(tt_zero, 1)
            a.wait_ge(y_ok, 3)
            diagonal(a.activation, 0, (0, 2), ACT.Copy)
            for n in range(J2):
                a.wait_ge(x_ps, J1 + n + 1)
                if n == J2 - 1:
                    a.wait_ge(y_ps, 2)
                for s in range(2):
                    rows = quarter[2 * s + 1]
                    a.activation(x2[n][rows, :, :], view(x2bank[n], W, G2)[rows, :, :], ACT.Copy).then_inc(x_ok, 1)
            a.wait_ge(y_ok, 6)
            diagonal(a.activation, 1, (0, 2), ACT.Copy)

        @block.vector
        def _(v):
            for n in range(NH):
                if n == 6:
                    substitute(v, sub_dve, slice(0, DB), tmp_dve)
                v.wait_ge(conv_init, n + 1)
                for j in range(PAD):
                    if j:
                        v.wait_ge(conv_done, 3 * n + j)
                    v.scalar_tensor_tensor(out=ac[:, n % 2, :, :], in0=cv(n)[:, :, j:j + N],
                                           scalar=t.taps[:, 2 * NP + n, j:j + 1], in1=ac[:, n % 2, :, :],
                                           op0=ALU.mult, op1=ALU.add).then_inc(conv_done, 1)
            sh = [128, SYS, 2, 8]
            for which, dst in ((0, tt32), (1, tn32)):
                for k in range(2):
                    v.wait_ge(back_ps, 4 if which else k + 1)
                    v.tensor_tensor(
                        dst.rearrange("p g (b i) -> p g b i", b=2)[:, :, :, 8 * k:8 * k + 8] if which else
                        dst[:, :, :].rearrange("p g (b i) -> p g b i", b=2)[:, :, :, 8 * k:8 * k + 8],
                        bc(ps[:, 2 + 2 * which + k, 0:8 * SYS].rearrange("p (i g) -> p g i", i=8).unsqueeze(2), *sh),
                        bc(t.parity[:, :].unsqueeze(1).unsqueeze(3), *sh), ALU.mult).then_inc(blocks_ok, 1)
            v.wait_ge(blocks_ok, 4)
            for n in range(J1):
                gs = slice(G1 * n, G1 * (n + 1))
                v.wait_ge(y_ps, 2 * (n + 1))
                d = tt32[:, gs, BASE:W]
                v.tensor_tensor(d, d, view(2 * n, BASE, G1), ALU.subtract).then_inc(y_ok, 1)
                for rows in quarter[0:3:2]:
                    d = tn32[rows, gs, 0:BASE]
                    v.tensor_tensor(d, d, view(2 * n + 1, BASE, G1)[rows, :, :], ALU.subtract).then_inc(y_ok, 1)
            v.wait_ge(tt_zero, 1)
            for n in range(J2):
                v.wait_ge(y_ps, 2 * J1 + n + 1)
                for s in range(2):
                    rows = quarter[2 * s]
                    v.tensor_scalar(t.tt[rows, G2 * n:G2 * (n + 1), 64 * s + 32:64 * s + 64],
                                    view(y2bank[n], W, G2)[rows, :, :], -1.0, None, ALU.mult)
    p.close()


def scan_chunks(nc, t, half):
    p = Phase(nc, f"_{half}")
    gt = t.aa[:, :, :, :].rearrange("p c h i -> p (c h i)").rearrange("p (r z) -> p r z", r=2)
    ot = p.sb("o_tile", [128, 2, NH, DV])
    osq = p.sb("o_sq", [128, NH, DV])
    oT = p.sb("o_T", [128, NH, 128])
    ov = p.sb("o_var", [128, NH])
    yt = p.sb("y_tile", [128, HID])
    ks = [p.ps(f"ks{b}", [128, 512]) for b in range(4)]
    us = [p.ps(f"us{b}", [128, 512]) for b in range(2)]
    fl = [p.ps(f"fl{b}", [128, 512]) for b in range(2)]
    names = ("ks_ps", "r_done", "u_ps", "u_done", "o_ps", "o_done", "su_ps", "S_done",
             "g_ps", "g_done", "osq_done", "sum_done", "var_done", "rstd_done", "og_done",
             "oT_ps", "oT_done", "y_ps2", "y_done", "vch3", "on_ready")
    (ks_ps, r_done, u_ps, u_done, o_ps, o_done, su_ps, S_done, g_ps, g_done, osq_done,
     sum_done, var_done, rstd_done, og_done, oT_ps, oT_done, y_ps, y_done, vch, on_ready) = (p.sem(n) for n in names)

    fresh, ends = half == 0, half == 1
    SKIPPED = 4 if fresh else 0

    def heads(ph, r):
        return [2 * (3 * ph + k) + r for k in range(G3)]

    def fillers(c):
        tr = [("t", c - 2, b) for b in range(3)] if c >= 2 else [None] * 3
        y = ("y", c - 2, 0) if c >= 2 else None
        g = [("g", c, b) for b in range(3)]
        lots = ([tr[0], tr[1]], [tr[2], g[0]], [g[1]], [y], [g[2]])
        return [[j for j in lot if j] for lot in lots]

    rest = [job for c in (HALF - 2, HALF - 1) for job in [("t", c, b) for b in range(3)] + [("y", c, 0)]]
    order = [j for c in range(HALF) for lot in fillers(c) for j in lot] + rest
    place = {job: n for n, job in enumerate(order)}
    done_of = {"g": g_done, "t": oT_done, "y": y_done}

    def index(job):
        kind, c, b = job
        return c * (1 if kind == "y" else 3) + b

    def bank_of(job):
        return fl[place[job] % 2]

    def normalise(eng, c):
        o = ot[:, c % 2, :, :]
        eng.tensor_tensor(o, o, bc(ov[:, :].unsqueeze(2), 128, NH, DV), ALU.mult).then_inc(on_ready, 1)

    with nc.Block() as block:
        @block.tensor
        def _(pe):
            def filler(job):
                kind, c, b = job
                if place[job] >= 2:
                    old = order[place[job] - 2]
                    pe.wait_ge(done_of[old[0]], index(old) + 1)
                o = bank_of(job)
                if kind == "g":
                    pe.matmul(o[:, :], t.hS[:, half * HALF + c, :], t.wg[:, b * 512:(b + 1) * 512],
                              start=True, stop=True).then_inc(g_ps, 1)
                elif kind == "t":
                    pe.wait_ge(on_ready, c + 1)
                    for k in range(4):
                        m = pe.transpose(o[:, k * 128:(k + 1) * 128], ot[:, c % 2, 4 * b + k, :], t.ident[:, :])
                    m.then_inc(oT_ps, 1)
                else:
                    pe.wait_ge(oT_done, 3 * (c + 1))
                    for h in range(NH):
                        m = pe.matmul(o[:, 0:HID], oT[:, h, :], t.wo[:, h, :], start=h == 0, stop=h == NH - 1)
                    m.then_inc(y_ps, 1)

            def state_products(c, ph):
                n = 2 * c + ph
                if c:
                    pe.wait_ge(S_done, 2 * (c - 1) + ph + 1)
                    pe.wait_ge(o_done, 4 * (c - 1) + 2 * ph + 2)
                for r in range(2):
                    rows = slice(r * 64, (r + 1) * 64)
                    for k in range(G3):
                        for s in range(2):
                            cs = slice(s * CK, (s + 1) * CK)
                            m = pe.matmul(ks[2 * ph + r][cs, k * DV:(k + 1) * DV], t.kqT[rows, c, 3 * ph + k, 0, cs],
                                          t.S[rows, s, 3 * ph + k, :], start=True, stop=True)
                    m.then_inc(ks_ps, 1)

            def solve(c, ph):
                n = 2 * c + ph
                if ph:
                    pe.wait_ge(u_done, 4 * c + 2)
                elif c:
                    pe.wait_ge(S_done, 2 * c)
                for r in range(2):
                    if c or not fresh:
                        pe.wait_ge(r_done, 2 * n + r + 1 - SKIPPED)
                    for k, h in enumerate(heads(ph, r)):
                        m = pe.matmul(us[r][:, k * DV:(k + 1) * DV], t.tt[:, c * NH + h, :], t.v[:, c, h, :],
                                      start=True, stop=True)
                    m.then_inc(u_ps, 1)

            def outputs(c, ph):
                for r in range(2):
                    rows = slice(r * 64, (r + 1) * 64)
                    pe.wait_ge(u_done, 4 * c + 2 * ph + r + 1)
                    for k, h in enumerate(heads(ph, r) if c or not fresh else ()):
                        for s in range(2):
                            cs = slice(s * CK, (s + 1) * CK)
                            m = pe.matmul(ks[2 * ph + r][cs, k * DV:(k + 1) * DV], t.kqT[rows, c, 3 * ph + k, 1, cs],
                                          t.S[rows, s, 3 * ph + k, :], start=k == 0, stop=False, skip_group_check=True)
                    for k, h in enumerate(heads(ph, r)):
                        m = pe.matmul(ks[2 * ph + r][:, k * DV:(k + 1) * DV], t.pp[:, c, h, :], t.v[:, c, h, :],
                                      start=fresh and c == 0 and k == 0, stop=k == G3 - 1, skip_group_check=True)
                    m.then_inc(o_ps, 1)

            def updates(c, ph):
                pe.wait_ge(u_done, 4 * c + 4)
                if ph:
                    pe.wait_ge(S_done, 2 * c + 1)
                for s in range(2):
                    cs = slice(s * CK, (s + 1) * CK)
                    for k in range(G3):
                        for r in range(2):
                            h = 2 * (3 * ph + k) + r
                            m = pe.matmul(us[s][r * 64:(r + 1) * 64, k * DV:(k + 1) * DV], t.kd[cs, c, h * DK:(h + 1) * DK],
                                          t.v[cs, c, h, :], start=True, stop=True)
                m.then_inc(su_ps, 1)

            for c in range(HALF):
                cut = fillers(c)
                if c or not fresh:
                    state_products(c, 0)
                    state_products(c, 1)
                for j in cut[0]:
                    filler(j)
                solve(c, 0)
                for j in cut[1]:
                    filler(j)
                solve(c, 1)
                for j in cut[2]:
                    filler(j)
                outputs(c, 0)
                if not (ends and c == HALF - 1):
                    updates(c, 0)
                for j in cut[3]:
                    filler(j)
                outputs(c, 1)
                if not (ends and c == HALF - 1):
                    updates(c, 1)
                for j in cut[4]:
                    filler(j)
            for j in rest:
                filler(j)

        @block.scalar
        def _(a):
            def copy_filler(job):
                kind, c, b = job
                if kind == "g":
                    if c >= 2 and b == 0:
                        a.wait_ge(og_done, c - 1)
                    a.wait_ge(g_ps, 3 * c + b + 1)
                    a.activation(gt[:, c % 2, b * 512:(b + 1) * 512], bank_of(job)[:, :], ACT.Silu).then_inc(g_done, 1)
                elif kind == "t":
                    if c and b == 0:
                        a.wait_ge(y_ps, c)
                    a.wait_ge(oT_ps, 3 * c + b + 1)
                    a.activation(oT[:, 4 * b:4 * b + 4, :].rearrange("p h d -> p (h d)"), bank_of(job)[:, :],
                                 ACT.Copy).then_inc(oT_done, 1)

            def copy_u(c, ph):
                for r in range(2):
                    a.wait_ge(u_ps, 4 * c + 2 * ph + r + 1)
                    a.activation(t.v[:, c, 6 * ph + r:6 * ph + r + 5:2, :], us[r][:, 0:G3 * DV].rearrange("p (h d) -> p h d", h=G3),
                                 ACT.Copy).then_inc(u_done, 1)

            def copy_o(c, ph):
                if c >= 2 and ph == 0:
                    a.wait_ge(oT_ps, 3 * (c - 1))
                for r in range(2):
                    a.wait_ge(o_ps, 4 * c + 2 * ph + r + 1)
                    a.activation(ot[:, c % 2, 6 * ph + r:6 * ph + r + 5:2, :],
                                 ks[2 * ph + r][:, 0:G3 * DV].rearrange("p (h d) -> p h d", h=G3), ACT.Copy).then_inc(o_done, 1)

            for c in range(HALF):
                cut = fillers(c)
                for j in cut[0]:
                    copy_filler(j)
                copy_u(c, 0)
                for j in cut[1]:
                    copy_filler(j)
                copy_u(c, 1)
                for j in cut[2]:
                    copy_filler(j)
                copy_o(c, 0)
                for j in cut[3]:
                    copy_filler(j)
                copy_o(c, 1)
                for j in cut[4]:
                    copy_filler(j)
            for j in rest:
                copy_filler(j)

        @block.gpsimd
        def _(g):
            for c in range(HALF):
                for ph in range(2):
                    g.wait_ge(o_done, 4 * c + 2 * ph + 2)
                    if c:
                        g.wait_ge(sum_done, c)
                    hs = slice(6 * ph, 6 * ph + 6)
                    g.tensor_tensor(osq[:, hs, :], ot[:, c % 2, hs, :], ot[:, c % 2, hs, :], ALU.mult).then_inc(osq_done, 1)
                g.wait_ge(var_done, c + 1)
                g.tensor_tensor(ov[:, :], ov[:, :], t.mhalf[:, 0:NH], ALU.pow).then_inc(rstd_done, 1)
                if c < HALF - 1:
                    g.wait_ge(rstd_done, c + 1)
                    g.wait_ge(og_done, c + 1)
                    normalise(g, c)

        @block.vector
        def _(v):
            link = linker(v, vch)

            def residuals(c, ph):
                for r in range(2):
                    v.wait_ge(ks_ps, 4 * c + 2 * ph + r + 1 - SKIPPED)
                    for k, h in enumerate(heads(ph, r)):
                        m = v.scalar_tensor_tensor(out=t.v[:, c, h, :], in0=ks[2 * ph + r][:, k * DV:(k + 1) * DV],
                                                   scalar=t.nGam[:, half * HALF + c, h:h + 1], in1=t.v[:, c, h, :],
                                                   op0=ALU.mult, op1=ALU.add)
                    m.then_inc(r_done, 1)

            def new_state(c, ph):
                v.wait_ge(o_ps, 4 * c + 2 * ph + 2)
                v.wait_ge(su_ps, 2 * c + ph + 1)
                for s in range(2):
                    for k in range(G3):
                        q = 3 * ph + k
                        m = v.scalar_tensor_tensor(out=t.S[:, s, q, :], in0=t.S[:, s, q, :],
                                                   scalar=t.gam_all[:, half * HALF + c, s, q:q + 1],
                                                   in1=us[s][:, k * DV:(k + 1) * DV], op0=ALU.mult, op1=ALU.add)
                m.then_inc(S_done, 1)

            def variances(c):
                if c:
                    v.wait_ge(on_ready, c)
                v.wait_ge(osq_done, 2 * c + 2)
                v.tensor_reduce(ov[:, :], osq[:, :, :], AX, ALU.add).then_inc(sum_done, 1)
                v.wait_ge(sum_done, c + 1)
                v.tensor_scalar(ov[:, :], ov[:, :], 1.0 / DV, 1e-5, ALU.mult, ALU.add).then_inc(var_done, 1)

            def gate(c):
                v.wait_ge(osq_done, 2 * c + 2)
                v.wait_ge(g_done, 3 * (c + 1))
                o = ot[:, c % 2, :, :].rearrange("p h d -> p (h d)")
                v.tensor_tensor(o, o, gt[:, c % 2, :], ALU.mult).then_inc(og_done, 1)

            def project(c):
                v.wait_ge(y_ps, c + 1)
                link(v.tensor_tensor(yt[:, :], bank_of(("y", c, 0))[:, 0:HID], t.modbc[:, 2 * HID:3 * HID], ALU.mult))
                v.tensor_tensor(t.x[:, half * HALF + c, :], t.x[:, half * HALF + c, :], yt[:, :], ALU.add).then_inc(y_done, 1)

            for c in range(HALF):
                if c or not fresh:
                    residuals(c, 0)
                    residuals(c, 1)
                if c:
                    variances(c - 1)
                    gate(c - 1)
                if not (ends and c == HALF - 1):
                    new_state(c, 0)
                    new_state(c, 1)
                if c >= 2:
                    project(c - 2)
            variances(HALF - 1)
            gate(HALF - 1)
            v.wait_ge(og_done, HALF)
            v.wait_ge(rstd_done, HALF)
            normalise(v, HALF - 1)
            project(HALF - 2)
            project(HALF - 1)
    p.close()


def second_norm(nc, t):
    p = Phase(nc)
    sq, st = p.sb("sq_b", [128, TILES, HID]), p.sb("st_b", [128, 3, TILES])
    hn = p.sb("h_rms", [128, TILES, HID])
    half = lambda b: slice(b * HALF, (b + 1) * HALF)
    ps = p.ps("ps_b1", [128, 2, 512])
    vch, pow_in, pow_out, hn_ok, hT_ps, hT_ok, k_zero = (p.sem(n) for n in (
        "vch_b", "pow_in_b", "pow_out_b", "hn_ok", "h1T_ps", "h1T_ok", "k_zero"))
    with nc.Block() as block:
        @block.gpsimd
        def _(g):
            for k in range(4):
                z = st[:, 1 + k // 2, half(k % 2)]
                g.wait_ge(pow_in, k + 1)
                g.tensor_tensor(z, z, t.mhalf[:, 0:HALF], ALU.pow).then_inc(pow_out, 1)

        @block.vector
        def _(v):
            link = linker(v, vch)
            sh = [128, HALF, HID]
            row = lambda m: bc(t.modbc[:, m * HID:(m + 1) * HID].unsqueeze(1), *sh)
            for b in range(2):
                cs = half(b)
                x, h, z, mean, var = t.x[:, cs, :], t.hf[:, cs, :], sq[:, cs, :], st[:, 0, cs], st[:, 1, cs]
                link(v.tensor_reduce(mean, x, AX, ALU.add))
                link(v.tensor_scalar(mean, mean, 1.0 / HID, None, ALU.mult))
                link(v.tensor_tensor(h, x, bc(mean.unsqueeze(2), *sh), ALU.subtract))
                link(v.tensor_tensor(z, h, h, ALU.mult))
                link(v.tensor_reduce(var, z, AX, ALU.add))
                v.tensor_scalar(var, var, 1.0 / HID, 1e-5, ALU.mult, ALU.add).then_inc(pow_in, 1)
            for b in range(2):
                cs = half(b)
                h, z, var = t.hf[:, cs, :], sq[:, cs, :], st[:, 2, cs]
                v.wait_ge(pow_out, b + 1)
                link(v.tensor_tensor(h, h, bc(st[:, 1, cs].unsqueeze(2), *sh), ALU.mult))
                link(v.tensor_tensor(h, h, row(4), ALU.mult))
                link(v.tensor_tensor(h, h, row(3), ALU.add))
                link(v.tensor_tensor(z, h, h, ALU.mult))
                link(v.tensor_reduce(var, z, AX, ALU.add))
                v.tensor_scalar(var, var, 1.0 / HID, 1e-6, ALU.mult, ALU.add).then_inc(pow_in, 1)
            for b in range(2):
                cs = half(b)
                v.wait_ge(pow_out, b + 3)
                v.tensor_tensor(hn[:, cs, :], t.hf[:, cs, :], bc(st[:, 2, cs].unsqueeze(2), *sh), ALU.mult).then_inc(hn_ok, 1)

        @block.tensor
        def _(pe):
            for c in range(TILES):
                pe.wait_ge(hn_ok, c // HALF + 1)
                m = pe.transpose(ps[:, c // 4, (c % 4) * 128:(c % 4 + 1) * 128], hn[:, c, :], t.ident[:, :])
                if c % 4 == 3:
                    m.then_inc(hT_ps, 1)

        @block.scalar
        def _(a):
            for k in range(2):
                rows = slice(64 * k, 64 * k + 64)
                a.activation(t.kT[rows, :, 1 - k:AH:2, :].rearrange("p s h i -> p (s h) i"),
                             bc(t.ones[rows, 0:1].unsqueeze(2), 64, AH, L), ACT.Copy, scale=0.0).then_inc(k_zero, 1)
            for b in range(2):
                a.wait_ge(hT_ps, b + 1)
                a.activation(t.h1T[:, :, 256 * b:256 * (b + 1)].rearrange("p s (c t) -> p c s t", c=4),
                             ps[:, b, :].rearrange("p (c s t) -> p c s t", c=4, s=2), ACT.Copy,
                             scale=t.n1w[:, 0:1]).then_inc(hT_ok, 1)
    p.close()


Q_EIGHTS = (slice(0, 3), slice(3, 5), slice(6, 7))
K_EIGHTS = (slice(0, 7, 3), slice(1, 5, 3), slice(2, 3))
MAX_AT = 40
UNITS = TQ * AH


class RowMaximum:

    def __init__(self, p, t, s, banks, trs):
        self.t, self.s, self.sc, self.tb = t, s, banks, trs
        self.mx = p.sb("row_max", [128, TQ * AH])
        self.mr = p.sb("max_rest", [128, TQ * AH])
        self.sc_ps, self.max_ok, self.neg_ok, self.again_ps, self.again_ok, self.vch = (p.sem(n) for n in (
            "sc_ps", "max_ok", "neg_ok", "again_ps", "again_ok", "vch_max"))

    def scores(self, pe, n):
        t, s, ring = self.t, self.s, len(self.sc)
        q, h = divmod(n, AH)
        if n >= ring:
            pe.wait_ge(self.max_ok, n - ring + 1)
        pe.matmul(self.sc[n % ring][:, :], t.qT[:, s, h // 2, q * 128:(q + 1) * 128], t.kT[:, s, h, :],
                  start=True, stop=True).then_inc(self.sc_ps, 1)

    def largest(self, v, n):
        v.wait_ge(self.sc_ps, n + 1)
        v.tensor_reduce(self.mx[:, n:n + 1], self.sc[n % len(self.sc)][:, :], AX, ALU.max).then_inc(self.max_ok, 1)

    def into_queries(self, v):
        link = linker(v, self.vch)
        q = self.t.qs[:, self.s, :, :]
        v.wait_ge(self.max_ok, UNITS)
        link(v.tensor_scalar(self.mx[:, :], self.mx[:, :], -1.0, None, ALU.mult))
        link(v.tensor_copy(q[:, :, MAX_AT], self.mx[:, :]))
        link(v.tensor_tensor(self.mr[:, :], self.mx[:, :], q[:, :, MAX_AT], ALU.subtract))
        link(v.tensor_copy(q[:, :, MAX_AT + 1], self.mr[:, :]))
        link(v.tensor_tensor(self.mr[:, :], self.mr[:, :], q[:, :, MAX_AT + 1], ALU.subtract))
        v.tensor_copy(q[:, :, MAX_AT + 2], self.mr[:, :]).then_inc(self.neg_ok, 1)

    def transpose_again(self, pe):
        pe.wait_ge(self.neg_ok, 1)
        wv = self.t.qs[:, self.s, :, :].rearrange("p g z -> p (g z)")
        for q in range(TQ):
            if q >= 2:
                pe.wait_ge(self.again_ok, q - 1)
            for b in range(8):
                m = pe.transpose(self.tb[q % 2][:, b, :], wv[:, (8 * q + b) * 128:(8 * q + b + 1) * 128], self.t.identb[:, :])
            m.then_inc(self.again_ps, 1)

    def copy_again(self, a, q):
        a.wait_ge(self.again_ps, q + 1)
        a.activation(self.t.qT[:, self.s, :, q * 128:(q + 1) * 128], self.tb[q % 2][:, :, :], ACT.Copy).then_inc(self.again_ok, 1)


def attention_scores(nc, t):
    p = Phase(nc)
    kx = p.sb("k_slots", [128, 2, TQ * AH, SLOT], BF16)
    x = p.sb("qk_f32", [128, 2, 2, TQ * HID])
    re = p.sb("qk_rest", [128, 2, TQ * HID])
    bank = [p.ps(f"att_ps{b}", [128, 512]) for b in range(6)]
    tb = [p.ps(f"tr_ps{b}", [128, 8, 128], BF16) for b in range(2)]
    (init, qkv_ps, x_ok, va_ok, hi_ok, slots_ok, tr_ps, tr_ok, odd_ok, vch, gch) = (p.sem(n) for n in (
        "slots_init", "qkv_ps", "x_ok", "va_ok", "hi_ok", "slots_ok", "tr_ps", "tr_ok", "odd_ok", "vch_s", "pool_chain_s"))
    largest = RowMaximum(p, t, 0, bank[0:3], tb)
    side = [(s, w) for s in range(2) for w in range(2)]
    eights = lambda s, w: (t.qs, kx)[w][:, s, :, :].rearrange("p g (k d) -> p g k d", d=AD)
    groups = lambda ap: ap.rearrange("p (g d) -> p g d", d=AD)

    def spread(ap, s, w, m):
        o = eights(s, w)[:, :, (Q_EIGHTS, K_EIGHTS)[w][m], :]
        return o, bc(groups(ap).unsqueeze(2), 128, TQ * AH, (3, 2, 1)[m], AD)

    def parts(eng, sem, s, w):
        link = linker_from(eng, sem, 3 * w)
        X, r = x[:, s, w, :], re[:, s, :]
        e = eights(s, w)
        hi, mid = (e[:, :, (Q_EIGHTS, K_EIGHTS)[w][m].start, :] for m in range(2))
        eng.wait_ge(hi_ok, 2 * s + w + 1)
        if w:
            eng.wait_ge(slots_ok, 2 * s + 1)
        link(eng.tensor_tensor(groups(r), groups(X), hi, ALU.subtract))
        link(eng.tensor_copy(*spread(r, s, w, 1)))
        link(eng.tensor_tensor(groups(r), groups(r), mid, ALU.subtract))
        if s and not w:
            eng.wait_ge(slots_ok, 2)
        eng.tensor_copy(*spread(r, s, w, 2)).then_inc(slots_ok, 1)

    trs = [(s, w, q) for s, w in side for q in range(TQ)]
    with nc.Block() as block:
        @block.gpsimd
        def _(g):
            for s, w in side:
                e = eights(s, w)
                g.memset(e[:, :, 5:8:2, :], 0.0).then_inc(init, 1)
            g.memset(t.va[:, :, :, :, AD:32], 1.0).then_inc(init, 1)
            g.wait_ge(init, 5)
            for s in range(2):
                g.memset(kx[:, s, :, MAX_AT:MAX_AT + 3], 1.0).then_inc(init, 1)
            parts(g, gch, 1, 0)
            parts(g, gch, 1, 1)

        @block.tensor
        def _(pe):
            for s in range(2):
                for m in range(3):
                    for q in range(TQ):
                        last = pe.matmul(bank[3 * s + m][:, q * HID:(q + 1) * HID], t.h1T[:, s, q * 128:(q + 1) * 128],
                                         t.wqkv[:, m * HID:(m + 1) * HID], start=True, stop=True)
                    last.then_inc(qkv_ps, 1)
            pe.wait_ge(init, 7)
            lots = 2 * TQ - 1
            for n, (s, w, q) in enumerate(trs):
                if n == 2 * TQ:
                    pe.wait_ge(tr_ok, 2 * TQ)
                    pe.wait_ge(odd_ok, TQ)
                    pe.wait_ge(x_ok, 2)
                    pe.wait_ge(va_ok, 1)
                if 2 * TQ <= n < 2 * TQ + lots:
                    for k in range(UNITS * (n - 2 * TQ) // lots, UNITS * (n - 2 * TQ + 1) // lots):
                        largest.scores(pe, k)
                pe.wait_ge(slots_ok, 2 * s + w + 1)
                if n >= 2:
                    pe.wait_ge(tr_ok, n - 1)
                if TQ + 2 <= n < 2 * TQ + 2:
                    pe.wait_ge(odd_ok, n - TQ - 1)
                wv = (t.qs, kx)[w][:, s, :, :].rearrange("p g z -> p (g z)")
                for b in range(8):
                    m = pe.transpose(tb[n % 2][:, b, :], wv[:, (8 * q + b) * 128:(8 * q + b + 1) * 128], t.identb[:, :])
                m.then_inc(tr_ps, 1)
            pe.wait_ge(tr_ok, 4 * TQ)
            largest.transpose_again(pe)

        @block.scalar
        def _(a):
            def ready(s, w):
                a.wait_ge(qkv_ps, 3 * s + w + 1)
                a.activation(x[:, s, w, :], bank[3 * s + w][:, :], ACT.Copy, scale=1.0 if w else AD ** -0.5).then_inc(x_ok, 1)
                a.wait_ge(x_ok, 2 * s + w + 1)
                a.activation(*spread(x[:, s, w, :], s, w, 0), ACT.Copy).then_inc(hi_ok, 1)

            def values(s):
                a.wait_ge(qkv_ps, 3 * s + 3)
                a.activation(t.va[:, s, :, :, 0:AD].rearrange("p q h d -> p (q h) d"), groups(bank[3 * s + 2][:, :]),
                             ACT.Copy).then_inc(va_ok, 1)

            def transposed(n):
                s, w, q = trs[n]
                a.wait_ge(tr_ps, n + 1)
                if w == 0:
                    a.activation(t.qT[:, s, :, q * 128:(q + 1) * 128], tb[n % 2][:, :, :], ACT.Copy).then_inc(tr_ok, 1)
                    return
                for r in range(1 + s):
                    rows = slice(64 * r, 64 * r + 64)
                    m = a.activation(t.kT[rows, s, r:AH:2, q * 128:(q + 1) * 128], tb[n % 2][rows, :, :], ACT.Copy)
                m.then_inc(tr_ok, 1)

            ready(0, 0)
            ready(0, 1)
            values(0)
            for n in range(TQ):
                transposed(n)
            ready(1, 0)
            for n in range(TQ, 2 * TQ):
                transposed(n)
            ready(1, 1)
            values(1)
            for n in range(2 * TQ, 4 * TQ):
                transposed(n)
            for q in range(TQ):
                largest.copy_again(a, q)

        @block.vector
        def _(v):
            parts(v, vch, 0, 0)
            parts(v, vch, 0, 1)
            for q in range(TQ):
                v.wait_ge(tr_ps, TQ + q + 1)
                v.tensor_copy(t.kT[64:128, 0, 1:AH:2, q * 128:(q + 1) * 128], tb[q % 2][64:128, :, :]).then_inc(odd_ok, 1)
            for n in range(UNITS):
                largest.largest(v, n)
            largest.into_queries(v)
    p.close()


def attention_values(nc, t, s):
    p = Phase(nc, f"_{s}")
    other = 1 if s == 0 else None
    RING = 2 if s == 0 else 3
    PR = 3
    GROUPS, STEPS = AH // 4, AH // 4 * TQ
    pt = p.sb("probs", [128, PR, 4, 512])
    sc = [p.ps(f"sT_ps{b}", [128, 2, 512]) for b in range(RING)]
    cx = [p.ps(f"ctx_ps{b}", [128, 512]) for b in range(2)]
    sc_ps, exp_ok, cx_ps, cx_ok = (p.sem(n) for n in ("sT_ps", "exp_ok", "ctx_ps", "ctx_ok"))
    if other:
        mb = [p.ps(f"max_ps{b}", [128, 512]) for b in range(2)]
        tb = [sc[b][:, 0, :].bitcast(BF16).rearrange("p (b z) -> p b z", b=8) for b in range(2)]
        largest = RowMaximum(p, t, other, mb, tb)
    PER = UNITS // (2 * STEPS)
    with nc.Block() as block:
        @block.tensor
        def _(pe):
            def scores(m):
                g, keys = divmod(m, TQ)
                for pair in range(2):
                    n = 2 * m + pair
                    if n >= RING:
                        pe.wait_ge(exp_ok, n - RING + 1)
                    for k in range(2):
                        h = 4 * g + 2 * pair + k
                        last = pe.matmul(sc[n % RING][:, k, :], t.kT[:, s, h, keys * 128:(keys + 1) * 128],
                                         t.qT[:, s, h // 2, :], start=True, stop=True)
                    last.then_inc(sc_ps, 1)

            def maxima(m, part):
                if other:
                    for k in range(PER):
                        largest.scores(pe, PER * (2 * m + part) + k)

            def values(m):
                g, keys = divmod(m, TQ)
                pe.wait_ge(exp_ok, 2 * (m + 1))
                if g >= 2 and keys == 0:
                    pe.wait_ge(cx_ok, g - 1)
                for j in range(4):
                    last = pe.matmul(cx[g % 2][32 * j:32 * j + 32, :], t.va[:, s, keys, 4 * g + j, :], pt[:, m % PR, j, :],
                                     start=keys == 0, stop=keys == TQ - 1)
                last.then_inc(cx_ps, 1)

            scores(0)
            for m in range(STEPS):
                maxima(m, 0)
                if m + 1 < STEPS:
                    scores(m + 1)
                maxima(m, 1)
                values(m)
            if other:
                largest.transpose_again(pe)

        @block.scalar
        def _(a):
            for m in range(STEPS):
                if m >= PR:
                    a.wait_ge(cx_ps, m - PR + 1)
                for pair in range(2):
                    n = 2 * m + pair
                    a.wait_ge(sc_ps, n + 1)
                    a.activation(pt[:, m % PR, 2 * pair:2 * pair + 2, :], sc[n % RING][:, :, :], ACT.Exp).then_inc(exp_ok, 1)
            if other:
                for q in range(TQ):
                    largest.copy_again(a, q)

        @block.vector
        def _(v):
            def context(g):
                v.wait_ge(cx_ps, TQ * (g + 1))
                v.tensor_copy(t.cx[:, g, :, s, :], cx[g % 2][:, :].rearrange("p (c t) -> p c t", c=TILES)).then_inc(cx_ok, 1)

            for g in range(GROUPS):
                if other:
                    for n in range(2 * TQ * PER * g, 2 * TQ * PER * (g + 1)):
                        largest.largest(v, n)
                        if g and n == 2 * TQ * PER * g + 3 * PER:
                            context(g - 1)
                elif g:
                    context(g - 1)
            if other:
                largest.into_queries(v)
            context(GROUPS - 1)
    p.close()


def attention_output(nc, t, src):
    p = Phase(nc)
    rc = p.sb("rec_sum", [128, TILES, AH])
    cn = p.sb("ctx_n", [128, TILES, AH, AD])
    cT = p.sb("ctx_nT", [128, TILES, 128])
    sq, st, hn = p.sb("sq_c", [128, TILES, HID]), p.sb("st_c", [128, TILES]), p.sb("h2_rms", [128, TILES, HID])
    ps = p.ps("ps_c", [128, 8, 512])
    (vch, cx_ps, cn_ok, cT_ps, cT_ok, y_ps, pow_in, pow_out, hn_ok, h2_ps, h2_ok) = (p.sem(n) for n in (
        "vch_c", "cxT_ps", "cn_ok", "cT_ps_c", "cT_ok", "y_ps_c", "pow_in_c", "pow_out_c", "hn_ok_c", "h2T_ps", "h2T_ok"))
    wl = p.sem("moe_weights")
    with nc.Block() as block:
        @block.sync
        def _(sp):
            for m, (one, many) in enumerate((("L0_ffn_sh_gate", "L0_ffn_e_gate"), ("L0_ffn_sh_up", "L0_ffn_e_up"))):
                sp.dma_start(t.wgu[:, NE, m, :], src[one]).then_inc(wl, 16)
                sp.dma_start(t.wgu[:, 0:NE, m, :], src[many].rearrange("e d f -> d e f")).then_inc(wl, 16)
            sp.dma_start(t.wdn[:, NE, :, :], src["L0_ffn_sh_down"].rearrange("(b f) d -> f b d", b=2)).then_inc(wl, 16)
            for b in range(2):
                sp.dma_start(t.wdn[:, 0:NE, b, :], src["L0_ffn_e_down"][:, 128 * b:128 * (b + 1), :]
                             .rearrange("e f d -> f e d")).then_inc(wl, 16)
            sp.wait_ge(wl, 16 * 7)

        @block.tensor
        def _(pe):
            for c in range(TILES):
                if c >= 4:
                    pe.wait_ge(cn_ok, c - 3)
                for g in range(4):
                    m = pe.transpose(ps[:, c % 4, g * 128:(g + 1) * 128], t.cx[:, g, c, :, :].rearrange("p s t -> p (s t)"), t.ident[:, :])
                m.then_inc(cx_ps, 1)
            for c in range(TILES):
                pe.wait_ge(cn_ok, c + 1)
                m = pe.transpose(ps[:, 4 + c // 4, (c % 4) * 128:(c % 4 + 1) * 128],
                                 cn[:, c, :, :].rearrange("p h d -> p (h d)"), t.ident[:, :])
                if c % 4 == 3:
                    m.then_inc(cT_ps, 1)
            pe.wait_ge(cT_ok, 2)
            for c in range(TILES):
                m = pe.matmul(ps[:, 6 + c // 4, (c % 4) * 128:(c % 4 + 1) * 128], cT[:, c, :], t.wo2[:, :],
                              start=True, stop=True)
                if c % 4 == 3:
                    m.then_inc(y_ps, 1)
            for c in range(TILES):
                pe.wait_ge(hn_ok, c // 4 + 1)
                m = pe.transpose(ps[:, c // 4, (c % 4) * 128:(c % 4 + 1) * 128], hn[:, c, :], t.ident[:, :])
                if c % 4 == 3:
                    m.then_inc(h2_ps, 1)

        @block.scalar
        def _(a):
            for b in range(2):
                a.wait_ge(cT_ps, b + 1)
                a.activation(cT[:, 4 * b:4 * b + 4, :].rearrange("p c i -> p (c i)"), ps[:, 4 + b, :], ACT.Copy).then_inc(cT_ok, 1)
            for b in range(2):
                a.wait_ge(h2_ps, b + 1)
                a.activation(t.h2T[:, 512 * b:512 * (b + 1)], ps[:, b, :], ACT.Copy, scale=t.n2w[:, 0:1]).then_inc(h2_ok, 1)

        @block.gpsimd
        def _(g):
            for b in range(2):
                g.wait_ge(pow_in, b + 1)
                g.tensor_tensor(st[:, 4 * b:4 * b + 4], st[:, 4 * b:4 * b + 4], t.mhalf[:, 0:4], ALU.pow).then_inc(pow_out, 1)

        @block.vector
        def _(v):
            link = linker(v, vch)
            for c in range(TILES):
                v.wait_ge(cx_ps, c + 1)
                z = ps[:, c % 4, :].rearrange("p (h z) -> p h z", h=AH)
                link(v.reciprocal(rc[:, c, :], z[:, :, AD]))
                v.tensor_tensor(cn[:, c, :, :], z[:, :, 0:AD], bc(rc[:, c, :].unsqueeze(2), 128, AH, AD),
                                ALU.mult).then_inc(cn_ok, 1)
            for b in range(2):
                v.wait_ge(y_ps, b + 1)
                cs = slice(4 * b, 4 * b + 4)
                h = t.hf[:, cs, :].rearrange("p c d -> p (c d)")
                link(v.tensor_tensor(h, h, ps[:, 6 + b, :], ALU.add))
                link(v.tensor_tensor(sq[:, cs, :], t.hf[:, cs, :], t.hf[:, cs, :], ALU.mult))
                link(v.tensor_reduce(st[:, cs], sq[:, cs, :], AX, ALU.add))
                v.tensor_scalar(st[:, cs], st[:, cs], 1.0 / HID, 1e-6, ALU.mult, ALU.add).then_inc(pow_in, 1)
            for b in range(2):
                v.wait_ge(pow_out, b + 1)
                cs = slice(4 * b, 4 * b + 4)
                v.tensor_tensor(hn[:, cs, :], t.hf[:, cs, :], bc(st[:, cs].unsqueeze(2), 128, 4, HID), ALU.mult).then_inc(hn_ok, 1)
    p.close()


def experts(nc, t, out, i):
    p = Phase(nc)
    sg = p.sb("gate_silu", [128, 2, 512])
    hid = p.sb("hidden", [128, 2, 2, 512])
    gp = [p.ps(f"gate_ps{b}", [128, 512]) for b in range(3)]
    up = [p.ps(f"up_ps{b}", [128, 512]) for b in range(3)]
    dn = [p.ps(f"down_ps{b}", [128, 512]) for b in range(2)]
    vch, gu_ps, sg_ok, hid_ok, dn_ps, dn_ok, out_ok = (p.sem(n) for n in (
        "vch_m", "gu_ps", "sg_ok", "hid_ok", "dn_ps", "dn_ok", "out_ok"))
    lg, eq, oh1, oh2 = (p.sb(n, [128, TILES, NE]) for n in ("logits", "eq", "first", "second"))
    sm = p.sb("route_st", [128, 6, TILES])
    lg_ps, ex_in, ex_ok, rch = (p.sem(n) for n in ("lg_ps", "ex_in", "ex_ok", "route_chain"))
    jobs = [(e, b) for e in range(NE, -1, -1) for b in range(2)]
    with nc.Block() as block:
        @block.tensor
        def _(pe):
            def gate_up(n):
                e, b = jobs[n]
                for f in range(2):
                    k = 2 * n + f
                    if k >= 3:
                        pe.wait_ge(hid_ok, k - 2)
                    pe.matmul(gp[k % 3][:, :], t.wgu[:, e, 0, f * 128:(f + 1) * 128], t.h2T[:, b * 512:(b + 1) * 512],
                              start=True, stop=True)
                    pe.matmul(up[k % 3][:, :], t.wgu[:, e, 1, f * 128:(f + 1) * 128], t.h2T[:, b * 512:(b + 1) * 512],
                              start=True, stop=True).then_inc(gu_ps, 1)

            def down(n):
                e, b = jobs[n]
                pe.wait_ge(hid_ok, 2 * n + 2)
                if n >= 2:
                    pe.wait_ge(dn_ok, 4 * (n - 1))
                for c in range(4):
                    for f in range(2):
                        m = pe.matmul(dn[n % 2][:, c * 128:(c + 1) * 128], hid[:, n % 2, f, c * 128:(c + 1) * 128],
                                      t.wdn[:, e, f, :], start=f == 0, stop=f == 1)
                m.then_inc(dn_ps, 1)

            for c in range(TILES):
                m = pe.matmul(dn[1][:, c * NE:(c + 1) * NE], t.h2T[:, c * 128:(c + 1) * 128], t.wr[:, :],
                              start=True, stop=True)
            m.then_inc(lg_ps, 1)
            gate_up(0)
            for n in range(len(jobs)):
                if n + 1 < len(jobs):
                    gate_up(n + 1)
                down(n)

        @block.scalar
        def _(a):
            for k, x in ((0, lg[:, :, :]), (1, sm[:, 3, :])):
                a.wait_ge(ex_in, k + 1)
                a.activation(x, x, ACT.Exp).then_inc(ex_ok, 1)
            for k in range(2 * len(jobs)):
                a.wait_ge(gu_ps, k + 1)
                if k >= 2:
                    a.wait_ge(hid_ok, k - 1)
                a.activation(sg[:, k % 2, :], gp[k % 3][:, :], ACT.Silu).then_inc(sg_ok, 1)

        @block.vector
        def _(v):
            link = linker(v, rch)
            se = [128, TILES, NE]
            wide = lambda x: bc(x.unsqueeze(2), *se)
            v.wait_ge(lg_ps, 1)
            link(v.tensor_copy(lg[:, :, :], dn[1][:, 0:TILES * NE].rearrange("p (c e) -> p c e", e=NE)))
            link(v.tensor_reduce(sm[:, 0, :], lg[:, :, :], AX, ALU.max))
            v.tensor_tensor(lg[:, :, :], lg[:, :, :], wide(sm[:, 0, :]), ALU.subtract).then_inc(ex_in, 1)
            v.wait_ge(ex_ok, 1)
            link(v.tensor_reduce(sm[:, 1, :], lg[:, :, :], AX, ALU.add))
            link(v.reciprocal(sm[:, 1, :], sm[:, 1, :]))
            link(v.tensor_tensor(lg[:, :, :], lg[:, :, :], wide(sm[:, 1, :]), ALU.mult))
            for k, oh in enumerate((oh1, oh2)):
                link(v.tensor_reduce(sm[:, 2 + k, :], lg[:, :, :], AX, ALU.max))
                link(v.tensor_tensor(eq[:, :, :], lg[:, :, :], wide(sm[:, 2 + k, :]), ALU.is_equal))
                link(v.tensor_tensor(eq[:, :, :], eq[:, :, :], bc(t.rank[:, :].unsqueeze(1), *se), ALU.mult))
                link(v.tensor_reduce(sm[:, 4, :], eq[:, :, :], AX, ALU.max))
                link(v.tensor_tensor(oh[:, :, :], eq[:, :, :], wide(sm[:, 4, :]), ALU.is_equal))
                if k == 0:
                    link(v.scalar_tensor_tensor(out=lg[:, :, :], in0=oh[:, :, :], scalar=-2.0, in1=lg[:, :, :],
                                                op0=ALU.mult, op1=ALU.add))
            v.tensor_tensor(sm[:, 3, :], sm[:, 3, :], sm[:, 2, :], ALU.subtract).then_inc(ex_in, 1)
            v.wait_ge(ex_ok, 2)
            link(v.tensor_scalar(sm[:, 4, :], sm[:, 3, :], 1.0, None, ALU.add))
            link(v.reciprocal(sm[:, 4, :], sm[:, 4, :]))
            link(v.tensor_tensor(sm[:, 5, :], sm[:, 3, :], sm[:, 4, :], ALU.mult))
            link(v.tensor_tensor(oh1[:, :, :], oh1[:, :, :], wide(sm[:, 4, :]), ALU.mult))
            link(v.tensor_tensor(oh2[:, :, :], oh2[:, :, :], wide(sm[:, 5, :]), ALU.mult))
            link(v.tensor_tensor(t.comb[:, :, :], oh1[:, :, :], oh2[:, :, :], ALU.add))
            link = linker(v, vch)

            def hidden(n):
                for f in range(2):
                    k = 2 * n + f
                    v.wait_ge(sg_ok, k + 1)
                    if n >= 2:
                        v.wait_ge(dn_ps, n - 1)
                    v.tensor_tensor(hid[:, n % 2, f, :], up[k % 3][:, :], sg[:, k % 2, :], ALU.mult).then_inc(hid_ok, 1)

            def combine(n):
                e, b = jobs[n]
                v.wait_ge(dn_ps, n + 1)
                if n >= 2:
                    v.wait_ge(dn_ok, 4 * (n - 1))
                for c in range(4):
                    h = t.hf[:, 4 * b + c, :]
                    v.scalar_tensor_tensor(out=h, in0=dn[n % 2][:, c * 128:(c + 1) * 128],
                                           scalar=1.0 if e == NE else t.comb[:, 4 * b + c, e:e + 1], in1=h,
                                           op0=ALU.mult, op1=ALU.add).then_inc(dn_ok, 1)

            hidden(0)
            for n in range(len(jobs)):
                if n + 1 < len(jobs):
                    hidden(n + 1)
                combine(n)
                if n >= len(jobs) - 2:
                    b = jobs[n][1]
                    h = t.hf[:, 4 * b:4 * b + 4, :]
                    v.wait_ge(dn_ok, 4 * (n + 1))
                    link(v.tensor_tensor(h, h, bc(t.modbc[:, 5 * HID:6 * HID].unsqueeze(1), 128, 4, HID), ALU.mult))
                    v.tensor_tensor(h, h, t.x[:, 4 * b:4 * b + 4, :], ALU.add).then_inc(out_ok, 1)

        @block.sync
        def _(sp):
            for b in range(2):
                sp.wait_ge(out_ok, b + 1)
                for s in range(2):
                    sp.dma_start(out[bass.ds(2 * i + s, 1), 4 * b * CK:4 * (b + 1) * CK, :].rearrange("a (c t) d -> t (a c) d", t=CK),
                                 t.hf[s * CK:(s + 1) * CK, 4 * b:4 * b + 4, :]).then_inc(t.stored, 16)
    p.close()


class Tensors:
    pass


def build(nc, src, out):
    with ExitStack() as ctx:
        def sb(name, shape, dt=F32, c=ctx):
            return c.enter_context(nc.sbuf_tensor(name, shape, dt))

        t = Tensors()
        t.stored = ctx.enter_context(nc.semaphore("stored"))
        t.w = sb("w_kqv", [128, 2 * KD + VD])
        t.taps = sb("taps", [128, NCH, TAPS])
        t.wg = sb("wg", [128, VD])
        t.wo = sb("wo", [DV, NH, HID])
        t.wgb = sb("wgk_wb", [128, 2 * NH])
        t.wqkv = sb("wqkv", [128, 3 * HID])
        t.wo2 = sb("wo_ffn", [128, HID])
        t.wr = sb("router_w", [128, NE])
        t.n1w, t.n2w = sb("norm1_w", [128, 1]), sb("norm2_w", [128, 1])
        t.hrow = sb("dt_bias_b_b", [128, 2 * NH])
        t.nA = sb("neg_A", [128, NH])
        t.ident, t.identb = sb("ident", [128, 128]), sb("ident_bf16", [128, 128], BF16)
        t.ones, t.later, t.upto = sb("ones", [128, 128]), sb("later", [128, 128]), sb("upto", [128, 128])
        t.tri = sb("tri", [128, CK])
        t.negm = sb("neg_mask", [128, 8 * CK], BF16)
        t.parity = sb("block_parity", [128, 2])
        t.mhalf = sb("minus_half", [128, 2 * NH])
        t.rank = sb("rank", [128, NE])
        t.pick = sb("pick", [B, PAIRS, 2])
        t.mod = sb("mod", [B, 6 * HID])
        t.x = sb("x", [128, TILES, HID])
        t.hf = sb("h_ffn", [128, TILES, HID])
        t.modbc = sb("mod_rows", [128, 6 * HID])
        t.hT = sb("hT", [128, 2, PAD + L])
        t.hS = sb("h_tiles", [128, TILES, 128])
        t.g, t.beta, t.Gam, t.nGam, t.kdec = (sb(n, [128, TILES, NH]) for n in ("g", "beta", "Gam", "neg_Gam", "k_decay"))
        t.gmask = sb("g_masked", [128, TILES, 2, NH])
        t.gam_all = sb("gam_all", [128, TILES, 2, NP])

        load_weights(nc, t, src)
        with nc.Fori(0, PAIRS) as i:
            with ExitStack() as a:
                t.S = sb("state", [128, 2, NP, DV], c=a)
                t.kqT = sb("kq_T", [128, HALF, NP, 2, 128], c=a)
                t.kd = sb("k_end", [128, HALF, KD], c=a)
                t.pp = sb("qk", [128, HALF, NH, 128], c=a)
                t.aa = sb("systems", [128, HALF, NH, CK], c=a)
                start_pair(nc, t, src, i)
                for half in range(2):
                    project_keys(nc, t, half)
                    with ExitStack() as b:
                        t.tt = sb(f"inverse_T_{half}", [128, SYS, 128], c=b)
                        t.v = sb(f"v_{half}", [128, HALF, NH, DV], c=b)
                        invert_systems(nc, t, half)
                        scan_chunks(nc, t, half)
            with ExitStack() as a:
                t.cx = sb("ctx", [128, 4, TILES, 2, CK], c=a)
                t.h1T = sb("h1T", [128, 2, L], c=a)
                with ExitStack() as b:
                    t.qT = sb("q_T", [128, 2, AH // 2, L], BF16, c=b)
                    t.kT = sb("k_T", [128, 2, AH, L], BF16, c=b)
                    second_norm(nc, t)
                    t.qs = sb("q_slots", [128, 2, TQ * AH, SLOT], BF16, c=b)
                    t.va = sb("v_and_one", [128, 2, TQ, AH, 32], c=b)
                    attention_scores(nc, t)
                    for s in range(2):
                        attention_values(nc, t, s)
                t.h2T = sb("h2T", [128, TILES * 128], c=a)
                t.comb = sb("combine", [128, TILES, NE], c=a)
                t.wgu = sb("gate_up_w", [128, NE + 1, 2, DFF], c=a)
                t.wdn = sb("down_w", [128, NE + 1, 2, HID], c=a)
                attention_output(nc, t, src)
                experts(nc, t, out, i)
        with nc.Block() as block:
            @block.sync
            def _(sp):
                sp.wait_ge(t.stored, STORES)


def kernel(**inputs):
    import numpy as _np
    import concourse.bacc as _bacc
    from concourse import mybir as _mybir
    from concourse.bass_utils import run_bass_kernel_spmd as _run

    nc = _bacc.Bacc("TRN2", target_bir_lowering=False, num_devices=1)
    arrays, src = {}, {}
    for name in inputs:
        a = _np.ascontiguousarray(inputs[name])
        arrays[f"in_{name}"] = a
        src[name] = nc.dram_tensor(f"in_{name}", a.shape, _mybir.dt.from_np(a.dtype), kind="ExternalInput").ap()
    out = nc.dram_tensor("out0", (B, L, HID), F32, kind="ExternalOutput").ap()
    build(nc, src, out)
    r = _run(nc, [arrays], core_ids=[0])
    return r.results[0]["out0"]
```
